# Optimizing a Trainium2 kernel written in Bass

```python
import numpy as np
import jax
import jax.numpy as jnp

def _softmax(x, axis=-1):
    return jax.nn.softmax(x, axis=axis)

def _gelu(x):
    return jax.nn.gelu(x, approximate=True)

def _silu(x):
    return jax.nn.silu(x)

def _sigmoid(x):
    return jax.nn.sigmoid(x)

def _layernorm(x, axis=-1, eps=1e-05):
    m = jnp.mean(x, axis=axis, keepdims=True)
    v = jnp.var(x, axis=axis, keepdims=True)
    return (x - m) / jnp.sqrt(v + eps)

def _scatter_add(tgt, idx, src, axis=0):
    return tgt.at[idx].add(src)

def _segment_sum(src, seg, n):
    return jax.ops.segment_sum(src, seg, n)
kernel_name = 'mk_xattn_ffn_d2_seqx_r4_2a03cb'

def setup_inputs(seed: int=0):
    np.random.seed(seed)
    _w = jnp.asarray

    def _rec_inputs():
        import jax
        import jax.numpy as jnp
        _rk = jax.random.key(seed)
        x = -0.000929 + 1 * jax.random.normal(jax.random.fold_in(_rk, 1), (4, 512, 512), jnp.float32)
        _lenS = 512 - jax.random.randint(jax.random.fold_in(_rk, 7), (4,), 0, max(1, 512 // 4) + 1, jnp.int32)
        _lenS2 = 1024 - jax.random.randint(jax.random.fold_in(_rk, 8), (4,), 0, max(1, 1024 // 4) + 1, jnp.int32)
        _ctx_2048P = jax.random.normal(jax.random.fold_in(_rk, 11), (4, 16, 512), jnp.float32)
        _ctx_2048c = jax.random.dirichlet(jax.random.fold_in(_rk, 511), 0.3 * jnp.ones((16,), jnp.float32), (4, 1024))
        _ctx_2048t = jnp.einsum('bsk,bkd->bsd', _ctx_2048c, _ctx_2048P)
        _ctx_2048t = _ctx_2048t * jax.lax.rsqrt(jnp.mean(jnp.square(_ctx_2048t)) + 1e-12) * 0.953939
        ctx_2048 = 2.81802e-05 + 1.00001 * (_ctx_2048t + 0.3 * jax.random.normal(jax.random.fold_in(_rk, 611), (4, 1024, 512), jnp.float32))
        _validS = jnp.arange(512)[None, :] < _lenS[:, None]
        _validS2 = jnp.arange(1024)[None, :] < _lenS2[:, None]
        _causal = jnp.tril(jnp.ones((512, 512), dtype=bool))
        mask_BxS2_bk0 = jnp.logical_not(jnp.broadcast_to(_validS2[:, :], (4, 1024)))
        return (x, ctx_2048, mask_BxS2_bk0)
    x, ctx_2048, mask_BxS2_bk0 = _rec_inputs()

    def _L0_xattn_setup():
        import jax, jax.numpy as jnp
        import numpy as np
        from jax import lax
        LN_EPS = 1e-05
        key = jax.random.key(seed)
        ks = jax.random.split(key, 8)
        B, S, T, D = (4, 128, 512, 512)
        scale = 0.02
        return {'Z': jax.random.normal(ks[0], (B, S, D), dtype=jnp.float32), 'kv': jax.random.normal(ks[1], (B, T, D), dtype=jnp.float32), 'decay': jnp.float32(0.9), 'W_in': jax.random.normal(ks[2], (D, D), dtype=jnp.float32) * scale, 'b_in': jnp.zeros((D,), dtype=jnp.float32), 'W_out': jax.random.normal(ks[3], (D, D), dtype=jnp.float32) * scale, 'b_out': jnp.zeros((D,), dtype=jnp.float32), 'gamma': jnp.ones((D,), dtype=jnp.float32), 'beta': jnp.zeros((D,), dtype=jnp.float32)}
    _L0_xattn_all = _L0_xattn_setup()
    _L0_xattn_in = {k: v for k, v in _L0_xattn_all.items() if k in ('decay', 'W_in', 'b_in', 'W_out', 'b_out', 'gamma', 'beta')}
    del _L0_xattn_all

    def _L0_ffn_setup():
        import jax, jax.numpy as jnp
        import numpy as np
        HIDDEN = 512
        INTER = 2048
        SCALE = 64.0

        def fwht(x):
            orig_shape = x.shape
            n = orig_shape[-1]
            x = x.reshape(-1, n)
            h = 1
            while h < n:
                x = x.reshape(-1, n // (2 * h), 2, h)
                a, b = (x[:, :, 0, :], x[:, :, 1, :])
                x = jnp.stack([a + b, a - b], axis=2).reshape(-1, n)
                h *= 2
            return (x / jnp.sqrt(jnp.asarray(n, x.dtype))).reshape(orig_shape)
        key = jax.random.key(seed)
        ks = jax.random.split(key, 8)
        inp = jax.random.normal(ks[0], (4, 512, HIDDEN), dtype=jnp.float32)
        SU_ug = jnp.where(jax.random.bernoulli(ks[1], 0.5, (HIDDEN,)), 1.0, -1.0).astype(jnp.float32)
        SU_dp = jnp.where(jax.random.bernoulli(ks[2], 0.5, (INTER,)), 1.0, -1.0).astype(jnp.float32)
        Wscale_ug = jax.random.uniform(ks[3], (2 * INTER,), jnp.float32, 0.5, 1.5)
        Wscale_dp = jax.random.uniform(ks[4], (HIDDEN,), jnp.float32, 0.5, 1.5)
        W_up = jax.random.normal(ks[5], (INTER, HIDDEN), dtype=jnp.float32) * 0.02
        W_gate = jax.random.normal(ks[6], (INTER, HIDDEN), dtype=jnp.float32) * 0.02
        W_down = jax.random.normal(ks[7], (HIDDEN, INTER), dtype=jnp.float32) * 0.02
        return {'input': inp, 'SU_ug': SU_ug, 'SU_dp': SU_dp, 'Wscale_ug': Wscale_ug, 'Wscale_dp': Wscale_dp, 'W_up': W_up, 'W_gate': W_gate, 'W_down': W_down}
    _L0_ffn_all = _L0_ffn_setup()
    _L0_ffn_in = {k: v for k, v in _L0_ffn_all.items() if k in ('SU_ug', 'SU_dp', 'Wscale_ug', 'Wscale_dp', 'W_up', 'W_gate', 'W_down')}
    del _L0_ffn_all

    def _L1_xattn_setup():
        import jax, jax.numpy as jnp
        import numpy as np
        key = jax.random.key(seed)
        k1, k2, k3 = jax.random.split(key, 3)
        B, S, D, M = (8, 512, 512, 128)
        hidden_states = jax.random.normal(k1, (B, S, D), dtype=jnp.float32)
        memory_tokens = jax.random.normal(k2, (B, M, D), dtype=jnp.float32)
        memory_mask = jax.random.randint(k3, (B, M), 0, 2).astype(jnp.bool_)
        return {'hidden_states': hidden_states, 'memory_tokens': memory_tokens, 'memory_mask': memory_mask}
    _L1_xattn_all = _L1_xattn_setup()
    _L1_xattn_in = {k: v for k, v in _L1_xattn_all.items() if k in ()}
    del _L1_xattn_all

    def _L1_ffn_setup():
        import jax, jax.numpy as jnp
        import numpy as np
        TOP_K = 8
        NUM_EXPERTS = 32
        key = jax.random.key(seed)
        k1, k2, k3, k4, k5 = jax.random.split(key, 5)
        B, S, D, M, E = (4, 256, 512, 192, NUM_EXPERTS)
        return {'hidden_states': jax.random.normal(k1, (B, S, D), dtype=jnp.float32), 'gate_kernel': jax.random.normal(k2, (D, E), dtype=jnp.float32) * 0.02, 'gate_proj': jax.random.normal(k3, (E, D, M), dtype=jnp.float32) * 0.02, 'up_proj': jax.random.normal(k4, (E, D, M), dtype=jnp.float32) * 0.02, 'down_proj': jax.random.normal(k5, (E, M, D), dtype=jnp.float32) * 0.02}
    _L1_ffn_all = _L1_ffn_setup()
    _L1_ffn_in = {k: v for k, v in _L1_ffn_all.items() if k in ('gate_kernel', 'gate_proj', 'up_proj', 'down_proj')}
    del _L1_ffn_all
    return {'x': x, 'ctx_2048': ctx_2048, 'mask_BxS2_bk0': mask_BxS2_bk0, 'L0_xattn_decay': _L0_xattn_in['decay'], 'L0_xattn_W_in': _L0_xattn_in['W_in'], 'L0_xattn_b_in': _L0_xattn_in['b_in'], 'L0_xattn_W_out': _L0_xattn_in['W_out'], 'L0_xattn_b_out': _L0_xattn_in['b_out'], 'L0_xattn_gamma': _L0_xattn_in['gamma'], 'L0_xattn_beta': _L0_xattn_in['beta'], 'L0_ffn_SU_ug': _L0_ffn_in['SU_ug'], 'L0_ffn_SU_dp': _L0_ffn_in['SU_dp'], 'L0_ffn_Wscale_ug': _L0_ffn_in['Wscale_ug'], 'L0_ffn_Wscale_dp': _L0_ffn_in['Wscale_dp'], 'L0_ffn_W_up': _L0_ffn_in['W_up'], 'L0_ffn_W_gate': _L0_ffn_in['W_gate'], 'L0_ffn_W_down': _L0_ffn_in['W_down'], 'L1_ffn_gate_kernel': _L1_ffn_in['gate_kernel'], 'L1_ffn_gate_proj': _L1_ffn_in['gate_proj'], 'L1_ffn_up_proj': _L1_ffn_in['up_proj'], 'L1_ffn_down_proj': _L1_ffn_in['down_proj']}

def reference(x, ctx_2048, mask_BxS2_bk0, L0_xattn_decay, L0_xattn_W_in, L0_xattn_b_in, L0_xattn_W_out, L0_xattn_b_out, L0_xattn_gamma, L0_xattn_beta, L0_ffn_SU_ug, L0_ffn_SU_dp, L0_ffn_Wscale_ug, L0_ffn_Wscale_dp, L0_ffn_W_up, L0_ffn_W_gate, L0_ffn_W_down, L1_ffn_gate_kernel, L1_ffn_gate_proj, L1_ffn_up_proj, L1_ffn_down_proj):
    import jax
    import jax.numpy as jnp

    def _L0_xattn_ref(Z, kv, decay, W_in, b_in, W_out, b_out, gamma, beta):
        import jax, jax.numpy as jnp
        import numpy as np
        from jax import lax
        LN_EPS = 1e-05
        B, T, D = kv.shape
        K = jax.nn.sigmoid(decay)
        x = jnp.einsum('btd,ed->bte', kv, W_in) + b_in

        def scan_fn(s, xt):
            s = K * s + xt
            return (s, s)
        s0 = jnp.zeros((B, D), dtype=kv.dtype)
        _, states = lax.scan(scan_fn, s0, jnp.swapaxes(x, 0, 1))
        states = jnp.swapaxes(states, 0, 1)
        proj = jnp.einsum('btd,ed->bte', states, W_out) + b_out
        summary = jnp.mean(proj, axis=1, keepdims=True)
        y = Z + summary
        mu = jnp.mean(y, axis=-1, keepdims=True)
        var = jnp.mean((y - mu) ** 2, axis=-1, keepdims=True)
        return (y - mu) / jnp.sqrt(var + LN_EPS) * gamma + beta

    def _L0_ffn_ref(input, SU_ug, SU_dp, Wscale_ug, Wscale_dp, W_up, W_gate, W_down):
        import jax, jax.numpy as jnp
        import numpy as np
        HIDDEN = 512
        INTER = 2048
        SCALE = 64.0

        def fwht(x):
            orig_shape = x.shape
            n = orig_shape[-1]
            x = x.reshape(-1, n)
            h = 1
            while h < n:
                x = x.reshape(-1, n // (2 * h), 2, h)
                a, b = (x[:, :, 0, :], x[:, :, 1, :])
                x = jnp.stack([a + b, a - b], axis=2).reshape(-1, n)
                h *= 2
            return (x / jnp.sqrt(jnp.asarray(n, x.dtype))).reshape(orig_shape)
        n = SU_ug.shape[0]
        x = input.reshape(-1, n)
        x = fwht(x * SU_ug) / SCALE
        x_up = x @ W_up.T * (Wscale_ug[:INTER] * SCALE)
        x_gate = x @ W_gate.T * (Wscale_ug[INTER:] * SCALE)
        x = jax.nn.silu(x_gate) * x_up
        x = fwht(x * SU_dp) / SCALE
        x = x @ W_down.T * (Wscale_dp * SCALE)
        return x.reshape(input.shape)

    def _L1_xattn_ref(hidden_states, memory_tokens, memory_mask):
        import jax, jax.numpy as jnp
        import numpy as np
        B, S, D = hidden_states.shape
        scale = 1.0 / jnp.sqrt(jnp.asarray(D, hidden_states.dtype))
        scores = jnp.einsum('bsd,bmd->bsm', hidden_states, memory_tokens) * scale
        neg_inf = jnp.asarray(-1e+30, scores.dtype)
        scores = jnp.where(memory_mask[:, None, :], scores, neg_inf)
        attn = jax.nn.softmax(scores, axis=-1)
        readout = jnp.einsum('bsm,bmd->bsd', attn, memory_tokens)
        valid_b = jnp.any(memory_mask, axis=-1)
        out = jnp.where(valid_b[:, None, None], readout, jnp.zeros_like(readout))
        return out

    def _L1_ffn_ref(hidden_states, gate_kernel, gate_proj, up_proj, down_proj):
        import jax, jax.numpy as jnp
        import numpy as np
        TOP_K = 8
        NUM_EXPERTS = 32
        B, S, D = hidden_states.shape
        T = B * S
        x2d = hidden_states.reshape(T, D)
        router_logits = x2d @ gate_kernel
        routing_weights = jax.nn.softmax(router_logits, axis=-1)
        routing_weights, selected_experts = jax.lax.top_k(routing_weights, TOP_K)
        routing_weights = routing_weights / jnp.sum(routing_weights, axis=-1, keepdims=True)
        flat_experts = selected_experts.reshape(-1)
        sort_idx = jnp.argsort(flat_experts)
        token_rows = sort_idx // TOP_K
        sorted_inputs = jnp.take(x2d, token_rows, axis=0)
        group_sizes = jnp.bincount(flat_experts, length=NUM_EXPERTS).astype(jnp.int32)
        w0 = jax.lax.ragged_dot(sorted_inputs, gate_proj, group_sizes, preferred_element_type=jnp.float32)
        w1 = jax.lax.ragged_dot(sorted_inputs, up_proj, group_sizes, preferred_element_type=jnp.float32)
        inter = jax.nn.silu(w0) * w1
        expert_out = jax.lax.ragged_dot(inter, down_proj, group_sizes, preferred_element_type=jnp.float32)
        unsorted = jnp.take(expert_out, jnp.argsort(sort_idx), axis=0)
        per_token = unsorted.reshape(T, TOP_K, D)
        output = jnp.einsum('BKE,BK->BE', per_token.astype(jnp.float32), routing_weights.astype(jnp.float32))
        return output.reshape(B, S, D)
    x = x + _L0_xattn_ref(_layernorm(x, axis=-1), ctx_2048, L0_xattn_decay, L0_xattn_W_in, L0_xattn_b_in, L0_xattn_W_out, L0_xattn_b_out, L0_xattn_gamma, L0_xattn_beta)
    x = x + _L0_ffn_ref(_layernorm(x, axis=-1), L0_ffn_SU_ug, L0_ffn_SU_dp, L0_ffn_Wscale_ug, L0_ffn_Wscale_dp, L0_ffn_W_up, L0_ffn_W_gate, L0_ffn_W_down)
    x = x + _L1_xattn_ref(_layernorm(x, axis=-1), ctx_2048, mask_BxS2_bk0)
    x = x + _L1_ffn_ref(_layernorm(x, axis=-1), L1_ffn_gate_kernel, L1_ffn_gate_proj, L1_ffn_up_proj, L1_ffn_down_proj)
    return x

_drawn_inputs = setup_inputs


def setup_inputs(seed=0):
    import zlib

    import numpy as np

    out = dict(_drawn_inputs(seed))
    spreads = {'L0_xattn_b_in': (0.0, 0.1),
     'L0_xattn_b_out': (0.0, 0.1),
     'L0_xattn_gamma': (1.0, 0.2),
     'L0_xattn_beta': (0.0, 0.1)}
    factors = {'L0_ffn_Wscale_dp': 3.801,
     'L1_ffn_gate_kernel': 8.0,
     'L1_ffn_gate_proj': 8.0,
     'L1_ffn_up_proj': 8.0,
     'L1_ffn_down_proj': 8.0}
    for name, (base, spread) in spreads.items():
        noise = np.random.default_rng([zlib.crc32(name.encode()), seed]).standard_normal(out[name].shape)
        drawn = base * np.exp(spread * noise) if base else spread * noise
        out[name] = jnp.asarray(drawn.astype(out[name].dtype))
    for name, factor in factors.items():
        out[name] = (out[name] * factor).astype(out[name].dtype)
    return out
```

```python
from contextlib import ExitStack

import numpy as np

import concourse.bass as bass
from concourse import mybir

F32 = mybir.dt.float32
F16 = mybir.dt.float16
U8 = mybir.dt.uint8
ALU = mybir.AluOpType
ACT = mybir.ActivationFunctionType
AXX = mybir.AxisListType.X

P = 128
B, S, D, T2 = 4, 512, 512, 1024
KC = D // P
TT = S // P
NT = B * TT
INTER = 2048
FC = INTER // P
NE, M, TOPK = 32, 192, 8
ML = M - P
EW = KC * 2 * M + 2 * D
KEYC = T2 // P
EPS = 1e-5
W_S = 256.0
U_S = 32.0
H_S = 64.0
C_S = 64.0
P_S = 1024.0
E_S = 64.0
C_BIN, C_SUG, C_SDP, C_WU, C_WG, C_DEC = 0, KC, 2 * KC, 2 * KC + FC, 2 * KC + 2 * FC, 2 * KC + 3 * FC
NCOL = C_DEC + 1


def wait(eng, sem, value):
    if isinstance(value, int) and value <= 0:
        return
    eng.wait_ge(sem, value)


def wait_apart(eng, sem, value, passed):
    eng.wait_ge(sem, value)
    eng.sem_inc(passed, 1)


def build(nc, a_x, a_ctxT, a_ctx, a_mask, a_winT, a_woutT, a_cols, a_rows, a_wupT, a_wgateT, a_wdT,
          a_gk, a_exp, a_ident, a_had, a_out):
    ctx = ExitStack()
    with ctx:
        def sb(name, shape, dt):
            return ctx.enter_context(nc.sbuf_tensor(name, shape, dt))

        def sem(name):
            return ctx.enter_context(nc.semaphore(name))

        X = sb("X", [P, NT * D], F32)
        HT = sb("HT", [P, 8192], F32)
        Z = sb("Z", [P, TT, D], F32)
        SUMM = sb("SUMM", [P, B, D], F32)
        ROWS = sb("ROWS", [P, 4, D], F32)
        COLS = sb("COLS", [P, NCOL], F32)
        BIG = sb("BIG", [P, 24576], F32)
        EX = sb("EX", [P, 3072], F32)
        ident = sb("ident", [P, P], F32)
        had = sb("had", [P, 2, P], F16)
        st = sb("st", [P, TT, 6], F32)
        mv = sb("mv", [P, TT, 2], F32)
        ve = sb("ve", [P, TT], F32)
        rs = sb("rs", [P, TT], F32)
        epsc = sb("epsc", [P, TT], F32)
        mhalf = sb("mhalf", [P, TT], F32)
        sm = sb("sm", [P, 16], F32)
        SG = sb("SG", [P, 2, FC], F32)
        SDPC = sb("SDPC", [P, FC], F32)
        cm = sb("cm", [P, KC, B], F32)
        sT = sb("sT", [P, KC, B], F32)
        valid = sb("valid", [P, B], F32)
        attn = sb("attn", [P, 2, 6], F32)
        G = sb("G", [P, NT, NE], F32)
        gk = sb("gk", [P, KC, NE], F32)
        gkh = sb("gkh", [P, KC, NE], F16)
        gkl = sb("gkl", [P, KC, NE], F16)
        RT = sb("RT", [P, TT, 4, NE], F32)
        M8 = sb("M8", [P, TT, 8], F32)
        RS = sb("RS", [P, TT, 4], F32)
        PS = ctx.enter_context(nc.psum_tensor("PS", [P, 8, 512], F32))

        def f16(t, start, shape):
            n = int(np.prod(shape)) // 2
            v = t[:, start:start + n].bitcast(F16)
            if len(shape) == 2:
                return v.rearrange("p (a b) -> p a b", a=shape[0])
            return v

        def f32(t, start, shape):
            v = t[:, start:start + int(np.prod(shape))]
            if len(shape) == 2:
                return v.rearrange("p (a b) -> p a b", a=shape[0])
            return v

        cxT = [f32(BIG, i * 4096, (KC, T2)) for i in range(2)]
        winT = f32(BIG, 8192, (KC, D))
        woutT = f32(BIG, 10240, (KC, D))
        vrow = BIG[:, 12288:12288 + T2]
        ones = BIG[:, 13312:13312 + T2]
        junk = BIG[:, 14336:14336 + T2]
        sTb = Z[:, :, :].rearrange("p a b -> p (a b)").rearrange("p (i m) -> p i m", m=P)
        WA = f32(HT, 0, (FC, P))
        WB = f32(HT, 2048, (FC, P))
        Sh = f16(EX, 0, (FC, P))
        Sl = f16(EX, 1024, (FC, P))
        wst = [f32(HT, 4096 + i * 2048, (KC, 512)) for i in range(2)]
        wh = f16(BIG, 0, (KC, 2 * INTER))
        wl = f16(BIG, 8192, (KC, 2 * INTER))
        w2h = f16(BIG, 16384, (FC, D))
        w2l = f16(BIG, 20480, (FC, D))
        hh = f16(HT, 0, (KC, S))
        hl = f16(HT, 1024, (KC, S))
        uh = f16(HT, 2048, (KC, S))
        ul = f16(HT, 3072, (KC, S))
        gs = [EX[:, i * 512:(i + 1) * 512] for i in range(2)]
        af = [EX[:, 1024 + i * 512:1536 + i * 512] for i in range(2)]
        ah = [f16(EX, 2048 + i * 256, (512,)) for i in range(2)]
        al = [f16(EX, 2560 + i * 256, (512,)) for i in range(2)]
        qh = f16(HT, 0, (KC, 2 * S))
        ql = f16(HT, 2048, (KC, 2 * S))
        cTst = f32(HT, 4096, (KC, T2))
        cTh = [f16(BIG, i * 8192, (KC, T2)) for i in range(2)]
        cTl = [f16(BIG, i * 8192 + 2048, (KC, T2)) for i in range(2)]
        cNh = [f16(BIG, i * 8192 + 4096, (KEYC, D)) for i in range(2)]
        cNl = [f16(BIG, i * 8192 + 6144, (KEYC, D)) for i in range(2)]
        cNst = f32(BIG, 16384, (KEYC, D))
        bias = BIG[:, 20480:24576]
        mask = EX[:, 0:1024].bitcast(U8)
        sc = EX[:, 0:1024]
        pr = EX[:, 1024:2048]
        pTh = f16(EX, 2048, (KEYC, P))
        pTl = f16(EX, 2560, (KEYC, P))
        th = f16(HT, 0, (KC, B * S))
        tl = f16(HT, 4096, (KC, B * S))
        est = [BIG[:, i * EW:(i + 1) * EW] for i in range(2)]
        eh = [f16(BIG, 2 * EW + i * EW // 2, (EW,)) for i in range(2)]
        el = [f16(BIG, 3 * EW + i * EW // 2, (EW,)) for i in range(2)]
        o = 4 * EW
        mg0 = [BIG[:, o + i * 512:o + (i + 1) * 512] for i in range(2)]
        mg1 = [BIG[:, o + 1024 + i * 512:o + 1536 + i * 512] for i in range(2)]
        ma0 = [BIG[:, o + 2048 + i * 512:o + 2560 + i * 512] for i in range(2)]
        ma1 = [BIG[:, o + 3072 + i * 512:o + 3584 + i * 512] for i in range(2)]
        mh0 = [f16(BIG, o + 4096 + i * 256, (512,)) for i in range(2)]
        ml0 = [f16(BIG, o + 4608 + i * 256, (512,)) for i in range(2)]
        mst = [f16(BIG, o + 5120 + i * 256, (512,)) for i in range(2)]

        def xt(tile):
            return X[:, bass.ds(tile * D, D)]

        s_const, s_wio, s_x, s_gk, s_mask, s_out = (sem(n) for n in (
            "const_landed", "mixer_weights_landed", "x_landed", "router_landed", "mask_landed", "out_landed"))
        s_cx = [sem(f"mixer_context_landed{i}") for i in range(2)]
        s_ws = [sem(f"ffn_weights_landed{i}") for i in range(2)]
        s_wd = sem("down_slice_landed")
        s_cT, s_cN = sem("keys_landed"), sem("values_landed")
        s_ew = [sem(f"expert_landed{i}") for i in range(2)]
        s_setup, s_dec, s_pre = sem("pool_consts_set"), sem("decay_gate_ready"), sem("mixer_step")
        s_ttr, s_st, s_sT, s_sTb, s_smp, s_summ = (sem(n) for n in (
            "context_summed", "states_product", "states_ready", "states_spread", "summary_product", "summary_ready"))
        s_fly, s_sh, s_sl, s_w2p, s_w2f, s_w2h, s_w2l = (sem(n) for n in (
            "butterfly_done", "down_split_hi", "down_split_lo", "down_product", "down_scaled", "down_hi", "down_lo"))
        s_wuh, s_wul = sem("ffn_weights_hi"), sem("ffn_weights_lo")
        s_bn, s_mv, s_ve, s_rs = (sem(n) for n in ("ln_stats", "ln_moments", "ln_var_eps", "ln_rstd"))
        s_z, s_h = sem("mixer_ln_step"), sem("normalised")
        s_tr, s_thi, s_tlo, s_hd = (sem(n) for n in (
            "transposed", "transposed_hi", "transposed_lo", "hadamard_done"))
        s_g, s_u, s_silu, s_a, s_ah, s_al, s_dn, s_x2 = (sem(n) for n in (
            "gate_product", "up_product", "silu_ready", "hidden_ready", "hidden_hi", "hidden_lo",
            "down_used_hidden", "ffn_added"))
        s_passed = sem("wait_passed")
        s_bias, s_val = sem("bias_ready"), sem("valid_ready")
        s_cth, s_ctl, s_cnh, s_cnl = (sem(n) for n in ("keys_hi", "keys_lo", "values_hi", "values_lo"))
        s_sc, s_s, s_mx, s_nm, s_p, s_pt, s_pth, s_ptl, s_rc, s_rv, s_rd, s_xr = (sem(n) for n in (
            "scores_product", "scores_ready", "max_ready", "negmax_ready", "probs_ready", "probs_transposed",
            "probs_hi", "probs_lo", "sum_inverted", "sum_scaled", "readout_product", "readout_added"))
        s_gkh, s_gkl, s_lg, s_ro, s_rex = (sem(n) for n in (
            "router_hi", "router_lo", "logits_product", "router_step", "router_exp"))
        s_eh, s_el = sem("expert_hi"), sem("expert_lo")
        s_mg, s_mm, s_mu, s_ms, s_ma, s_mh, s_ml, s_mdn, s_free = (sem(n) for n in (
            "expert_gate_product", "expert_mixed_product", "expert_up_product", "expert_silu", "expert_hidden",
            "expert_hidden_hi", "expert_hidden_lo", "expert_down_product", "expert_bank_free"))

        block = ctx.enter_context(nc.Block())
        NCONST = 4

        @block.sync
        def _(sp):
            sp.dma_start(COLS[:, :], a_cols).then_inc(s_const, 16)
            sp.dma_start(ROWS[:, :, :], a_rows).then_inc(s_const, 16)
            sp.dma_start(ident[:, :], a_ident).then_inc(s_const, 16)
            sp.dma_start(had[:, :, :], a_had).then_inc(s_const, 16)
            for b in range(B):
                if b >= 2:
                    sp.wait_ge(s_ttr, (b - 1) * KC)
                sp.dma_start(cxT[b % 2], a_ctxT[b].rearrange("(k p) t -> p k t", p=P)).then_inc(s_cx[b % 2], 16)
                if b == 1:
                    sp.dma_start(winT, a_winT.rearrange("(k p) e -> p k e", p=P)).then_inc(s_wio, 16)
                    sp.dma_start(woutT, a_woutT.rearrange("(k p) e -> p k e", p=P)).then_inc(s_wio, 16)
            sp.dma_start(X[:, :].rearrange("p (t d) -> p t d", d=D),
                         a_x.rearrange("(t p) d -> p t d", p=P)).then_inc(s_x, 16)
            sp.dma_start(gk[:, :, :], a_gk.rearrange("(k p) e -> p k e", p=P)).then_inc(s_gk, 16)
            up = a_wupT.rearrange("(k p) f -> p k f", p=P)
            gate = a_wgateT.rearrange("(k p) f -> p k f", p=P)
            for c in range(8):
                if c >= 2:
                    sp.wait_ge(s_wul, c - 1)
                src = (up, gate)[c % 2]
                sp.dma_start(wst[c % 2], src[:, :, (c // 2) * 512:(c // 2 + 1) * 512]).then_inc(s_ws[c % 2], 16)
            for b in range(B):
                if b == 0:
                    sp.wait_ge(s_wul, 8)
                else:
                    sp.wait_ge(s_ctl, b)
                sp.dma_start(cTst, a_ctxT[b].rearrange("(k p) t -> p k t", p=P)).then_inc(s_cT, 16)
                if b == 0:
                    sp.wait_ge(s_x2, NT)
                    sp.dma_start(mask, a_mask).then_inc(s_mask, 16)
                else:
                    sp.wait_ge(s_cnl, b)
                sp.dma_start(cNst, a_ctx[b].rearrange("(c p) d -> p c d", p=P)).then_inc(s_cN, 16)
            sp.wait_ge(s_xr, NT)
            sp.dma_start(est[0], a_exp[0]).then_inc(s_ew[0], 16)
            sp.dma_start(est[1], a_exp[1]).then_inc(s_ew[1], 16)
            with sp.Fori(1, NE // 2) as it:
                for j in range(2):
                    sp.wait_ge(s_el, it * 2 + (j - 1))
                    sp.dma_start(est[j], a_exp[bass.ds(it * 2 + j, 1), :, :].rearrange("a p w -> p (a w)"))\
                        .then_inc(s_ew[j], 16)
            for b in range(B):
                sp.wait_ge(s_free, 2 + 4 * ((NE - 1) * B + b) + TT)
                sp.dma_start(a_out[b * S:(b + 1) * S, :].rearrange("(t p) d -> p t d", p=P),
                             X[:, b * TT * D:(b + 1) * TT * D].rearrange("p (t d) -> p t d", d=D)).then_inc(s_out, 16)
            sp.wait_ge(s_out, 16 * B)

        @block.gpsimd
        def _(pool):
            pool.memset(epsc[:, :], EPS).then_inc(s_setup, 1)
            pool.memset(mhalf[:, :], -0.5).then_inc(s_setup, 1)
            for s in range(4):
                if s:
                    pool.wait_ge(s_sl, s)
                pool.dma_start(WA, a_wdT[:, s * P:(s + 1) * P].rearrange("(c p) d -> p c d", p=P)).then_inc(s_wd, 16)
                pool.wait_ge(s_wd, 16 * (s + 1))
                if s:
                    pool.wait_ge(s_w2l, s)
                src, dst = WA, WB
                for n, h in enumerate((1, 2, 4, 8)):
                    i = src.rearrange("p (g t h) d -> p g t (h d)", t=2, h=h)
                    q = dst.rearrange("p (g t h) d -> p g t (h d)", t=2, h=h)
                    if n:
                        pool.wait_ge(s_fly, 8 * s + 2 * n)
                    pool.tensor_tensor(q[:, :, 0, :], i[:, :, 0, :], i[:, :, 1, :], ALU.add).then_inc(s_fly, 1)
                    pool.tensor_tensor(q[:, :, 1, :], i[:, :, 0, :], i[:, :, 1, :], ALU.subtract).then_inc(s_fly, 1)
                    src, dst = dst, src
            pool.wait_ge(s_setup, 2)
            with pool.Fori(0, 5 * B) as n:
                pool.wait_ge(s_mv, n * TT + TT)
                pool.tensor_tensor(ve[:, :], mv[:, :, 1], epsc[:, :], ALU.add).then_inc(s_ve, 1)
                pool.wait_ge(s_ve, n + 1)
                pool.tensor_tensor(rs[:, :], ve[:, :], mhalf[:, :], ALU.pow).then_inc(s_rs, 1)

        @block.scalar
        def _(act):
            act.wait_ge(s_const, 16 * NCONST)
            act.activation(sm[:, 0:1], COLS[:, C_DEC:C_DEC + 1], ACT.Sigmoid).then_inc(s_dec, 1)
            for s in range(4):
                act.wait_ge(s_fly, 8 * (s + 1))
                if s:
                    act.wait_ge(s_w2p, 4 * s)
                act.activation(Sh, WA, ACT.Copy, scale=W_S).then_inc(s_sh, 1)
                act.wait_ge(s_w2f, FC * (s + 1))
                act.activation(w2h[:, :, s * P:(s + 1) * P], WB, ACT.Copy).then_inc(s_w2h, 1)
            act.wait_ge(s_summ, B)
            for c in range(8):
                act.wait_ge(s_ws[c % 2], 16 * (c // 2 + 1))
                o = (c % 2) * INTER + (c // 2) * 512
                act.activation(wh[:, :, o:o + 512], wst[c % 2], ACT.Copy, scale=W_S).then_inc(s_wuh, 1)

            def transposed_hi(q, e, dst, bank, scale, sem_in):
                act.wait_ge(sem_in, q)
                act.activation(dst, PS[:, bank, :], ACT.Copy, scale=scale).then_inc(s_thi, 1)

            def ffn_prep(b):
                for k in range(KC):
                    transposed_hi(b * 4 + (k + 1), None, uh[:, k, :], 4 + k % 2, COLS[:, C_SUG + k:C_SUG + k + 1], s_tr)
                for j in range(KC):
                    transposed_hi(b * 4 + (j + 1), None, hh[:, j, :], 4 + j % 2, 1.0, s_hd)

            def ffn_chunk(F, f, p, first):
                act.wait_ge(s_g, F + 1)
                if not first:
                    act.wait_ge(s_a, F - 1)
                act.activation(gs[p], PS[:, 2 * p, :], ACT.Silu, scale=SG[:, 1, f]).then_inc(s_silu, 1)
                act.wait_ge(s_a, F + 1)
                if not first:
                    act.wait_ge(s_dn, F - 1)
                act.activation(ah[p], af[p], ACT.Copy).then_inc(s_ah, 1)

            def ffn_batch(b):
                for p in range(2):
                    ffn_chunk(b * FC + p, slice(p, p + 1), p, True)
                with act.Fori(1, FC // 2) as i:
                    for p in range(2):
                        ffn_chunk(b * FC + i * 2 + p, bass.ds(i * 2 + p, 1), p, False)

            act.wait_ge(s_pre, 2)
            ffn_prep(0)
            with act.Fori(0, B - 1) as b:
                ffn_batch(b)
                ffn_prep(b + 1)
            ffn_batch(B - 1)

            def keys_hi(b, p):
                act.wait_ge(s_cT, b * 16 + 16)
                act.activation(cTh[p], cTst, ACT.Copy, scale=C_S).then_inc(s_cth, 1)

            def values_hi(b, p):
                act.wait_ge(s_cN, b * 16 + 16)
                act.activation(cNh[p], cNst, ACT.Copy, scale=C_S).then_inc(s_cnh, 1)

            def exp_tile(t, l):
                act.wait_ge(s_nm, t + 1)
                if l:
                    act.wait_ge(s_pt, t)
                act.activation(pr, sc, ACT.Exp, bias=attn[:, l % 2, 1:2], accum_out=attn[:, l % 2, 2:3])\
                    .then_inc(s_p, 1)

            act.wait_ge(s_x2, NT)
            with act.Fori(0, B // 2) as it:
                keys_hi(it * 2, 0)
                for blk in range(2):
                    for k in range(KC):
                        transposed_hi(it * 8 + (4 * B + 4 * blk + k + 1), None, qh[:, k, blk * S:(blk + 1) * S],
                                      6 + k % 2, H_S, s_tr)
                values_hi(it * 2, 0)
                exp_tile(it * 8, 0)
                for l in range(8):
                    act.wait_ge(s_pt, it * 8 + (l + 1))
                    if l:
                        act.wait_ge(s_rd, it * 8 + l)
                    act.activation(pTh, PS[:, 4:6, :].rearrange("p b (c n) -> p (b c) n", n=P), ACT.Copy, scale=P_S)\
                        .then_inc(s_pth, 1)
                    if l == 0:
                        keys_hi(it * 2 + 1, 1)
                        values_hi(it * 2 + 1, 1)
                    if l < 7:
                        exp_tile(it * 8 + (l + 1), l + 1)

            act.wait_ge(s_gk, 16)
            act.activation(gkh[:, :, :], gk[:, :, :], ACT.Copy, scale=E_S).then_inc(s_gkh, 1)

            def expert_hi(e, p):
                act.wait_ge(s_ew[p], e * 8 + (16 - 8 * p))
                act.activation(eh[p], est[p], ACT.Copy, scale=E_S).then_inc(s_eh, 1)

            with act.Fori(0, B) as b:
                for k in range(KC):
                    act.wait_ge(s_tr, b * 4 + (8 * B + k + 1))
                    act.activation(th[:, k, bass.ds(b * S, S)], PS[:, 6 + k % 2, :], ACT.Copy, scale=H_S)\
                        .then_inc(s_thi, 1)
                for t in range(TT):
                    act.wait_ge(s_ro, b * (6 * TT) + (3 * TT + t + 1))
                    act.activation(RT[:, t, 3, :], RT[:, t, 0, :], ACT.Exp, bias=RS[:, t, 0:1]).then_inc(s_rex, 1)
            expert_hi(0, 0)

            def expert_batch(E, l):
                p = l % 2
                act.wait_ge(s_mg, E + 1)
                act.activation(mg0[p], PS[:, 3 * p, :], ACT.Silu, scale=1.0 / (H_S * E_S)).then_inc(s_ms, 1)
                act.wait_ge(s_mm, E + 1)
                act.activation(mg1[p][ML:P, :], PS[0:ML, 3 * p + 1, :], ACT.Silu, scale=1.0 / (H_S * E_S))\
                    .then_inc(s_ms, 1)
                act.wait_ge(s_ma, 2 * E + 1)
                act.activation(mh0[p], ma0[p], ACT.Copy).then_inc(s_mh, 1)
                act.wait_ge(s_ma, 2 * E + 2)
                act.activation(mst[p][ML:P, :], ma1[p][ML:P, :], ACT.Copy).then_inc(s_mh, 1)

            def expert_pair(it, last):
                for l in range(8):
                    expert_batch(it * 8 + l, l)
                    if l % 4 == 1 and not (last and l == 5):
                        expert_hi(it * 2 + (l // 4 + 1), (l // 4 + 1) % 2)

            with act.Fori(0, NE // 2 - 1) as it:
                expert_pair(it, False)
            expert_pair(NE // 2 - 1, True)

        @block.vector
        def _(dve):
            v = nc.vector
            v.memset(ones, 1.0).then_inc(s_pre, 1)
            dve.wait_ge(s_const, 16 * NCONST)
            v.tensor_scalar(SG[:, :, :], COLS[:, C_WU:C_WU + 2 * FC].rearrange("p (a f) -> p a f", a=2),
                            1.0 / (W_S * D ** 0.5), None, ALU.mult).then_inc(s_pre, 1)
            v.tensor_scalar(SDPC[:, :], COLS[:, C_SDP:C_SDP + FC], INTER ** -0.5, None, ALU.mult).then_inc(s_pre, 1)
            dve.wait_ge(s_pre, 3)
            v.tensor_scalar(SG[:, 0, :], SG[:, 0, :], U_S, None, ALU.mult).then_inc(s_pre, 1)
            dve.wait_ge(s_dec, 1)
            v.tensor_tensor_scan(vrow, sm[:, 0:1].to_broadcast([P, T2]), ones, 0.0, ALU.mult, ALU.add)\
                .then_inc(s_pre, 1)
            dve.wait_ge(s_pre, 5)
            v.reduce_sum(sm[:, 1:2], vrow, AXX).then_inc(s_pre, 1)
            dve.wait_ge(s_pre, 6)
            v.tensor_scalar(sm[:, 2:2 + KC], COLS[:, C_BIN:C_BIN + KC], sm[:, 1:2], 1.0 / T2, ALU.mult, ALU.mult)\
                .then_inc(s_pre, 1)
            for b in range(B):
                dve.wait_ge(s_cx[b % 2], 16 * (b // 2 + 1))
                for k in range(KC):
                    if b or k:
                        dve.wait_ge(s_ttr, b * KC + k)
                    v.tensor_tensor_reduce(out=junk, in0=cxT[b % 2][:, k, :], in1=vrow[:, ::-1], scale=1.0, scalar=0.0,
                                           op0=ALU.mult, op1=ALU.add, accum_out=cm[:, k, b:b + 1]).then_inc(s_ttr, 1)
            dve.wait_ge(s_st, 1)
            dve.wait_ge(s_pre, 7)
            for k in range(KC):
                v.tensor_scalar(sT[:, k, :], PS[:, 0, k * B:(k + 1) * B], 1.0 / T2, sm[:, 2 + k:3 + k],
                                ALU.mult, ALU.add).then_inc(s_sT, 1)
            dve.wait_ge(s_sT, KC)
            v.tensor_copy(sTb, sT[:, :, :].rearrange("p k b -> p (k b)").unsqueeze(2).to_broadcast([P, KC * B, P]))\
                .then_inc(s_sTb, 1)
            for b in range(B):
                dve.wait_ge(s_smp, b + 1)
                v.tensor_tensor(SUMM[:, b, :], PS[:, 1 + b % 2, :], ROWS[:, 2, :], ALU.add).then_inc(s_summ, 1)
            for s in range(4):
                dve.wait_ge(s_sh, s + 1)
                v.scalar_tensor_tensor(Sl, WA, W_S, Sh, ALU.mult, ALU.subtract).then_inc(s_sl, 1)
                for c in range(FC):
                    if c % 4 == 0:
                        dve.wait_ge(s_w2p, 4 * s + c // 4 + 1)
                    v.scalar_tensor_tensor(WB[:, c, :], PS[:, 4 + c // 4, (c % 4) * P:(c % 4 + 1) * P],
                                           SDPC[:, c:c + 1], ROWS[:, 3, s * P:(s + 1) * P], ALU.mult, ALU.mult)\
                        .then_inc(s_w2f, 1)
                dve.wait_ge(s_w2h, s + 1)
                dve.wait_ge(s_w2f, FC * (s + 1))
                v.tensor_tensor(w2l[:, :, s * P:(s + 1) * P], WB, w2h[:, :, s * P:(s + 1) * P], ALU.subtract)\
                    .then_inc(s_w2l, 1)
            for c in range(8):
                dve.wait_ge(s_wuh, c + 1)
                o = (c % 2) * INTER + (c // 2) * 512
                v.scalar_tensor_tensor(wl[:, :, o:o + 512], wst[c % 2], W_S, wh[:, :, o:o + 512],
                                       ALU.mult, ALU.subtract).then_inc(s_wul, 1)

            def stats(n, src):
                for t in range(TT):
                    v.bn_stats(st[:, t, :], src(t)).then_inc(s_bn, 1)
                for t in range(TT):
                    wait_apart(dve, s_bn, n * TT + (t + 1), s_passed)
                    v.bn_aggr(mv[:, t, :], st[:, t, :]).then_inc(s_mv, 1)
                dve.wait_ge(s_mv, n * TT + TT)
                dve.wait_ge(s_rs, n + 1)

            def normalise(q, tile):
                wait(dve, s_tr, q * 4)
                for t in range(TT):
                    v.tensor_scalar(Z[:, t, :], xt(tile + t), mv[:, t, 0:1], rs[:, t:t + 1],
                                    ALU.subtract, ALU.mult).then_inc(s_h, 1)

            def mixer_ln(b, tile):
                stats(b * 3, lambda t: xt(tile + t))
                wait(dve, s_tr, b * 4)
                for t in range(TT):
                    v.tensor_scalar(Z[:, t, :], xt(tile + t), mv[:, t, 0:1], rs[:, t:t + 1],
                                    ALU.subtract, ALU.mult).then_inc(s_z, 1)
                for t in range(TT):
                    dve.wait_ge(s_z, b * 20 + (t + 1))
                    v.tensor_tensor(Z[:, t, :], Z[:, t, :], summ(b), ALU.add).then_inc(s_z, 1)
                wait_apart(dve, s_z, b * 20 + 8, s_passed)
                stats(b * 3 + 1, lambda t: Z[:, t, :])
                for t in range(TT):
                    v.scalar_tensor_tensor(Z[:, t, :], Z[:, t, :], mv[:, t, 0:1], ROWS[:, 0, :],
                                           ALU.subtract, ALU.mult).then_inc(s_z, 1)
                for t in range(TT):
                    v.tensor_tensor(xt(tile + t), xt(tile + t), ROWS[:, 1, :], ALU.add).then_inc(s_z, 1)
                for t in range(TT):
                    dve.wait_ge(s_z, b * 20 + (13 + t))
                    v.scalar_tensor_tensor(xt(tile + t), Z[:, t, :], rs[:, t:t + 1], xt(tile + t),
                                           ALU.mult, ALU.add).then_inc(s_z, 1)
                wait_apart(dve, s_z, b * 20 + 20, s_passed)
                stats(b * 3 + 2, lambda t: xt(tile + t))
                normalise(b, tile)

            def summ(b):
                return SUMM[:, :, :].rearrange("p b d -> p (b d)")[:, bass.ds(b * D, D)]

            def ffn_prep_lo(b):
                for k in range(KC):
                    dve.wait_ge(s_thi, b * 8 + (k + 1))
                    v.scalar_tensor_tensor(ul[:, k, :], PS[:, 4 + k % 2, :], COLS[:, C_SUG + k:C_SUG + k + 1], uh[:, k, :],
                                           ALU.mult, ALU.subtract).then_inc(s_tlo, 1)
                for j in range(KC):
                    dve.wait_ge(s_thi, b * 8 + (5 + j))
                    v.tensor_tensor(hl[:, j, :], PS[:, 4 + j % 2, :], hh[:, j, :], ALU.subtract).then_inc(s_tlo, 1)

            def ffn_chunk(F, f, p, first):
                dve.wait_ge(s_silu, F + 1)
                dve.wait_ge(s_u, F + 1)
                if not first:
                    dve.wait_ge(s_ah, F - 1)
                v.scalar_tensor_tensor(af[p], PS[:, 2 * p + 1, :], SG[:, 0, f], gs[p], ALU.mult, ALU.mult).then_inc(s_a, 1)
                dve.wait_ge(s_ah, F + 1)
                if not first:
                    dve.wait_ge(s_dn, F - 1)
                v.tensor_tensor(al[p], af[p], ah[p], ALU.subtract).then_inc(s_al, 1)

            def ffn_batch(b):
                for p in range(2):
                    ffn_chunk(b * FC + p, slice(p, p + 1), p, True)
                with dve.Fori(1, FC // 2) as i:
                    for p in range(2):
                        ffn_chunk(b * FC + i * 2 + p, bass.ds(i * 2 + p, 1), p, False)

            def ffn_add(b):
                dve.wait_ge(s_dn, b * FC + FC)
                for t in range(TT):
                    v.scalar_tensor_tensor(xt(b * TT + t), PS[:, 4 + t, :], 1.0 / (U_S * W_S), xt(b * TT + t),
                                           ALU.mult, ALU.add).then_inc(s_x2, 1)

            dve.wait_ge(s_x, 16)
            dve.wait_ge(s_summ, B)
            mixer_ln(0, 0)
            ffn_prep_lo(0)
            with dve.Fori(0, B - 1) as b:
                ffn_batch(b)
                mixer_ln(b + 1, b * TT + TT)
                ffn_add(b)
                ffn_prep_lo(b + 1)
            ffn_batch(B - 1)
            ffn_add(B - 1)

            dve.wait_ge(s_mask, 16)
            v.tensor_scalar(bias, mask, 1.0, 1e30, ALU.subtract, ALU.mult).then_inc(s_bias, 1)
            v.reduce_max(valid[:, :], mask.rearrange("p (b t) -> p b t", b=B), AXX).then_inc(s_val, 1)
            dve.wait_ge(s_val, 1)
            v.tensor_scalar(valid[:, :], valid[:, :], 1.0 / (P_S * C_S), None, ALU.mult).then_inc(s_val, 1)
            dve.wait_ge(s_bias, 1)
            dve.wait_ge(s_x2, NT)

            def keys_lo(b, p):
                dve.wait_ge(s_cth, b + 1)
                v.scalar_tensor_tensor(cTl[p], cTst, C_S, cTh[p], ALU.mult, ALU.subtract).then_inc(s_ctl, 1)

            def values_lo(b, p):
                dve.wait_ge(s_cnh, b + 1)
                v.scalar_tensor_tensor(cNl[p], cNst, C_S, cNh[p], ALU.mult, ALU.subtract).then_inc(s_cnl, 1)

            def softmax_tile(t, l, b):
                p = l % 2
                dve.wait_ge(s_sc, t + 1)
                if l:
                    dve.wait_ge(s_p, t)
                v.scalar_tensor_tensor(sc, PS[:, 2 * p:2 * p + 2, :].rearrange("p a n -> p (a n)"),
                                       D ** -0.5 / (H_S * C_S), bias[:, bass.ds(b * T2, T2)], ALU.mult, ALU.add)\
                    .then_inc(s_s, 1)
                dve.wait_ge(s_s, t + 1)
                v.reduce_max(attn[:, p, 0:1], sc, AXX).then_inc(s_mx, 1)
                dve.wait_ge(s_mx, t + 1)
                v.tensor_scalar(attn[:, p, 1:2], attn[:, p, 0:1], -1.0, None, ALU.mult).then_inc(s_nm, 1)

            def readout_add(t, l, b):
                p = l % 2
                dve.wait_ge(s_p, t + 1)
                v.reciprocal(attn[:, p, 3:4], attn[:, p, 2:3]).then_inc(s_rc, 1)
                dve.wait_ge(s_rc, t + 1)
                v.tensor_tensor(attn[:, p, 4:5], attn[:, p, 3:4], valid[:, bass.ds(b, 1)], ALU.mult).then_inc(s_rv, 1)
                dve.wait_ge(s_rv, t + 1)
                dve.wait_ge(s_rd, t + 1)
                v.scalar_tensor_tensor(xt(t), PS[:, 6, :], attn[:, p, 4:5], xt(t), ALU.mult, ALU.add).then_inc(s_xr, 1)

            dve.wait_ge(s_val, 2)
            with dve.Fori(0, B // 2) as it:
                keys_lo(it * 2, 0)
                for blk in range(2):
                    n = it * 2 + blk
                    stats(n + 3 * B, lambda t: xt(n * TT + t))
                    normalise(n + B, n * TT)
                    for k in range(KC):
                        dve.wait_ge(s_thi, it * 8 + (8 * B + 4 * blk + k + 1))
                        v.scalar_tensor_tensor(ql[:, k, blk * S:(blk + 1) * S], PS[:, 6 + k % 2, :], H_S,
                                               qh[:, k, blk * S:(blk + 1) * S], ALU.mult, ALU.subtract).then_inc(s_tlo, 1)
                values_lo(it * 2, 0)
                softmax_tile(it * 8, 0, it * 2)
                for l in range(8):
                    dve.wait_ge(s_pth, it * 8 + (l + 1))
                    v.scalar_tensor_tensor(pTl, PS[:, 4:6, :].rearrange("p b (c n) -> p (b c) n", n=P), P_S, pTh,
                                           ALU.mult, ALU.subtract).then_inc(s_ptl, 1)
                    if l == 0:
                        keys_lo(it * 2 + 1, 1)
                        values_lo(it * 2 + 1, 1)
                    if l < 7:
                        softmax_tile(it * 8 + (l + 1), l + 1, it * 2 + (l + 1) // 4)
                    readout_add(it * 8 + l, l, it * 2 + l // 4)

            dve.wait_ge(s_gkh, 1)
            v.scalar_tensor_tensor(gkl[:, :, :], gk[:, :, :], E_S, gkh[:, :, :], ALU.mult, ALU.subtract).then_inc(s_gkl, 1)
            dve.wait_ge(s_xr, NT)

            def router_step(b, n, ins):
                for t in range(TT):
                    if n:
                        wait_apart(dve, s_ro, b * (6 * TT) + ((n - 1) * TT + t + 1), s_passed)
                    ins(t).then_inc(s_ro, 1)

            with dve.Fori(0, B) as b:
                stats(b + 4 * B, lambda t: xt(b * TT + t))
                normalise(b + 2 * B, b * TT)
                for k in range(KC):
                    dve.wait_ge(s_thi, b * 4 + (12 * B + k + 1))
                    v.scalar_tensor_tensor(tl[:, k, bass.ds(b * S, S)], PS[:, 6 + k % 2, :], H_S,
                                           th[:, k, bass.ds(b * S, S)], ALU.mult, ALU.subtract).then_inc(s_tlo, 1)
                dve.wait_ge(s_lg, b + 1)
                router_step(b, 0, lambda t: v.tensor_scalar(RT[:, t, 0, :], PS[:, 0, t * NE:(t + 1) * NE],
                                                            1.0 / (H_S * E_S), None, ALU.mult))
                router_step(b, 1, lambda t: v.max(M8[:, t, :], RT[:, t, 0, :]))
                router_step(b, 2, lambda t: v.match_replace(RT[:, t, 1, :], M8[:, t, :], RT[:, t, 0, :], -3e38))
                router_step(b, 3, lambda t: v.tensor_scalar(RS[:, t, 0:1], M8[:, t, 0:1], -1.0, None, ALU.mult))
                router_step(b, 4, lambda t: v.tensor_tensor(RT[:, t, 2, :], RT[:, t, 0, :], RT[:, t, 1, :], ALU.not_equal))
                for t in range(TT):
                    dve.wait_ge(s_ro, b * (6 * TT) + (4 * TT + t + 1))
                    dve.wait_ge(s_rex, b * TT + (t + 1))
                    v.tensor_tensor_reduce(out=RT[:, t, 1, :], in0=RT[:, t, 2, :], in1=RT[:, t, 3, :], scale=1.0, scalar=0.0,
                                           op0=ALU.mult, op1=ALU.add, accum_out=RS[:, t, 1:2]).then_inc(s_ro, 1)
                dve.wait_ge(s_ro, b * (6 * TT) + 6 * TT)
                v.reciprocal(RS[:, :, 2], RS[:, :, 1]).then_inc(s_rc, 1)
                dve.wait_ge(s_rc, b + (NT + 1))
                for t in range(TT):
                    v.tensor_scalar(G[:, :, :].rearrange("p t e -> p (t e)")[:, bass.ds((b * TT + t) * NE, NE)],
                                    RT[:, t, 1, :], RS[:, t, 2:3], 1.0 / E_S, ALU.mult, ALU.mult).then_inc(s_rv, 1)
            dve.wait_ge(s_rv, 2 * NT)

            def expert_lo(e, p):
                dve.wait_ge(s_eh, e + 1)
                v.scalar_tensor_tensor(el[p], est[p], E_S, eh[p], ALU.mult, ALU.subtract).then_inc(s_el, 1)

            def expert_batch(E, l, e):
                p = l % 2
                dve.wait_ge(s_ms, 2 * E + 2)
                dve.wait_ge(s_mu, E + 1)
                v.scalar_tensor_tensor(ma0[p], PS[:, 3 * p + 2, :], 1.0 / (H_S * E_S), mg0[p], ALU.mult, ALU.mult)\
                    .then_inc(s_ma, 1)
                v.scalar_tensor_tensor(ma1[p][ML:P, :], PS[ML:P, 3 * p + 1, :], 1.0 / (H_S * E_S), mg1[p][ML:P, :],
                                       ALU.mult, ALU.mult).then_inc(s_ma, 1)
                dve.wait_ge(s_mh, 2 * E + 1)
                v.tensor_tensor(ml0[p], ma0[p], mh0[p], ALU.subtract).then_inc(s_ml, 1)
                dve.wait_ge(s_mh, 2 * E + 2)
                v.tensor_tensor(mst[p][0:ML, :], ma1[p][ML:P, :], mst[p][ML:P, :], ALU.subtract).then_inc(s_ml, 1)
                if l % 4 == 1 and e is not None:
                    expert_lo(e, (l // 4 + 1) % 2)
                for t in range(TT):
                    dve.wait_ge(s_mdn, 4 * E + (t + 1))
                    o = (l % 4) * TT + t
                    v.scalar_tensor_tensor(X[:, o * D:(o + 1) * D], PS[:, 6 + t % 2, :], gate_col(o, E, l),
                                           X[:, o * D:(o + 1) * D], ALU.mult, ALU.add).then_inc(s_free, 1)

            def expert_pair(it, last):
                for l in range(8):
                    e = None if last and l == 5 else it * 2 + (l // 4 + 1)
                    expert_batch_at[0] = it * 2 + l // 4
                    expert_batch(it * 8 + l, l, e)

            expert_batch_at = [None]

            def gate_col(o, E, l):
                return G[:, o, bass.ds(expert_batch_at[0], 1)]

            expert_lo(0, 0)
            dve.sem_inc(s_free, 2)
            with dve.Fori(0, NE // 2 - 1) as it:
                expert_pair(it, False)
            expert_pair(NE // 2 - 1, True)

        @block.tensor
        def _(pe):
            mm = nc.tensor.matmul
            pe.wait_ge(s_wio, 32)
            pe.wait_ge(s_ttr, B * KC)
            for ec in range(KC):
                for k in range(KC):
                    last = mm(PS[:, 0, ec * B:(ec + 1) * B], winT[:, k, ec * P:(ec + 1) * P], cm[:, k, :],
                              start=(k == 0), stop=(k == KC - 1))
            last.then_inc(s_st, 1)
            pe.wait_ge(s_sTb, 1)
            for b in range(B):
                wait(pe, s_summ, b - 1)
                for k in range(KC):
                    last = mm(PS[:, 1 + b % 2, :], sTb[:, k * B + b, :], woutT[:, k, :], start=(k == 0), stop=(k == KC - 1))
                last.then_inc(s_smp, 1)
            for s in range(4):
                pe.wait_ge(s_sl, s + 1)
                for g in range(4):
                    if s:
                        pe.wait_ge(s_w2f, FC * (s - 1) + 4 * (g + 1))
                    mm(PS[:, 4 + g, :], had[:, 0, :], Sh[:, 4 * g:4 * g + 4, :], start=True, stop=False)
                    mm(PS[:, 4 + g, :], had[:, 0, :], Sl[:, 4 * g:4 * g + 4, :], start=False, stop=True).then_inc(s_w2p, 1)

            def transposes(q, E, bank):
                pe.wait_ge(s_h, q * TT + TT)
                for k in range(KC):
                    wait(pe, s_tlo, E + (k - 1))
                    for t in range(TT):
                        last = nc.tensor.transpose(PS[:, bank + k % 2, t * P:(t + 1) * P], Z[:, t, k * P:(k + 1) * P], ident[:, :])
                    last.then_inc(s_tr, 1)

            def ffn_prep(b):
                wait(pe, s_x2, b * TT)
                transposes(b, b * 8, 4)
                pe.wait_ge(s_tlo, b * 8 + KC)
                for j in range(KC):
                    if j >= 2:
                        pe.wait_ge(s_tlo, b * 8 + (KC + j - 1))
                    for i in range(KC):
                        sign = bin(i & j).count("1") % 2
                        mm(PS[:, 4 + j % 2, :], had[:, sign, :], uh[:, i, :], start=(i == 0), stop=False)
                        last = mm(PS[:, 4 + j % 2, :], had[:, sign, :], ul[:, i, :], start=False, stop=(i == KC - 1))
                    last.then_inc(s_hd, 1)
                pe.wait_ge(s_tlo, b * 8 + 2 * KC)

            def three(out, lh, ll, rh, rl, first, last_group):
                mm(out, lh, rh, start=first, stop=False)
                mm(out, lh, rl, start=False, stop=False)
                return mm(out, ll, rh, start=False, stop=last_group)

            def cols(t, k, at):
                if isinstance(at, int):
                    return t[:, k, at:at + P]
                return t[:, k, bass.ds(at, P)]

            def up_gate(F, f, p, first):
                if not first:
                    pe.wait_ge(s_a, F - 1)
                for half, bank, done in ((1, 2 * p, s_g), (0, 2 * p + 1, s_u)):
                    for k in range(KC):
                        at = f * P + half * INTER
                        last = three(PS[:, bank, :], cols(wh, k, at), cols(wl, k, at), hh[:, k, :], hl[:, k, :], k == 0, k == KC - 1)
                    last.then_inc(done, 1)

            def down(F, f, p, first, end):
                pe.wait_ge(s_al, F + 1)
                pe.wait_ge(s_ah, F + 1)
                for t in range(TT):
                    a, b_ = ah[p][:, t * P:(t + 1) * P], al[p][:, t * P:(t + 1) * P]
                    fs = slice(f, f + 1) if isinstance(f, int) else bass.ds(f, 1)
                    rh, rl = w2h[:, fs, :].rearrange("p a d -> p (a d)"), w2l[:, fs, :].rearrange("p a d -> p (a d)")
                    last = three(PS[:, 4 + t, :], a, b_, rh, rl, first, end)
                last.then_inc(s_dn, 1)

            def ffn_batch(b):
                up_gate(b * FC, 0, 0, True)
                up_gate(b * FC + 1, 1, 1, True)
                down(b * FC, 0, 0, True, False)
                with pe.Fori(0, FC // 2 - 1) as i:
                    up_gate(b * FC + i * 2 + 2, i * 2 + 2, 0, False)
                    down(b * FC + i * 2 + 1, i * 2 + 1, 1, False, False)
                    up_gate(b * FC + i * 2 + 3, i * 2 + 3, 1, False)
                    down(b * FC + i * 2 + 2, i * 2 + 2, 0, False, False)
                down(b * FC + FC - 1, FC - 1, 1, False, True)

            pe.wait_ge(s_w2l, 4)
            ffn_prep(0)
            pe.wait_ge(s_wul, 8)
            with pe.Fori(0, B - 1) as b:
                ffn_batch(b)
                ffn_prep(b + 1)
            ffn_batch(B - 1)

            def scores(t, l, b):
                p = l % 2
                if l >= 2:
                    pe.wait_ge(s_s, t - 1)
                if l % 4 == 0:
                    pe.wait_ge(s_ctl, b + 1)
                par = l // 4
                for n in range(2):
                    for k in range(KC):
                        last = three(PS[:, 2 * p + n, :], qh[:, k, l * P:(l + 1) * P], ql[:, k, l * P:(l + 1) * P],
                                     cTh[par][:, k, n * 512:(n + 1) * 512], cTl[par][:, k, n * 512:(n + 1) * 512],
                                     k == 0, k == KC - 1)
                last.then_inc(s_sc, 1)

            with pe.Fori(0, B // 2) as it:
                wait(pe, s_x2, NT)
                for blk in range(2):
                    transposes(it * 2 + (B + blk), it * 8 + (8 * B + 4 * blk), 6)
                pe.wait_ge(s_tlo, it * 8 + (8 * B + 8))
                scores(it * 8, 0, it * 2)
                for l in range(8):
                    if l < 7:
                        scores(it * 8 + (l + 1), l + 1, it * 2 + (l + 1) // 4)
                    pe.wait_ge(s_p, it * 8 + (l + 1))
                    if l:
                        pe.wait_ge(s_ptl, it * 8 + l)
                    for c in range(KEYC):
                        last = nc.tensor.transpose(PS[:, 4 + c // 4, (c % 4) * P:(c % 4 + 1) * P], pr[:, c * P:(c + 1) * P], ident[:, :])
                    last.then_inc(s_pt, 1)
                    pe.wait_ge(s_ptl, it * 8 + (l + 1))
                    if l:
                        pe.wait_ge(s_xr, it * 8 + l)
                    if l % 4 == 0:
                        pe.wait_ge(s_cnl, it * 2 + (l // 4 + 1))
                    for c in range(KEYC):
                        last = three(PS[:, 6, :], pTh[:, c, :], pTl[:, c, :], cNh[l // 4][:, c, :], cNl[l // 4][:, c, :],
                                     c == 0, c == KEYC - 1)
                    last.then_inc(s_rd, 1)
                pe.wait_ge(s_xr, it * 8 + 8)

            pe.wait_ge(s_gkl, 1)
            pe.wait_ge(s_xr, NT)
            with pe.Fori(0, B) as b:
                transposes(b + 2 * B, b * 4 + 12 * B, 6)
                pe.wait_ge(s_tlo, b * 4 + (12 * B + KC))
                for t in range(TT):
                    for k in range(KC):
                        at = b * S + t * P
                        last = three(PS[:, 0, t * NE:(t + 1) * NE], cols(th, k, at), cols(tl, k, at),
                                     gkh[:, k, :], gkl[:, k, :], k == 0, k == KC - 1)
                last.then_inc(s_lg, 1)
                pe.wait_ge(s_ro, b * (6 * TT) + TT)

            GU = 2 * M

            def expert_up(E, l, e):
                p = l % 2
                q = (l // 4) % 2
                if l % 4 == 0:
                    pe.wait_ge(s_el, e + 1)
                for j, done in ((0, s_mg), (1, s_mm), (2, s_mu)):
                    for k in range(KC):
                        c = k * GU + j * P
                        last = three(PS[:, 3 * p + j, :], eh[q][:, c:c + P], el[q][:, c:c + P],
                                     th[:, k, (l % 4) * S:(l % 4 + 1) * S], tl[:, k, (l % 4) * S:(l % 4 + 1) * S],
                                     k == 0, k == KC - 1)
                    last.then_inc(done, 1)

            def expert_down(E, l):
                p = l % 2
                q = l // 4
                W0, W1 = KC * GU, KC * GU + D
                pe.wait_ge(s_ml, 2 * E + 2)
                for t in range(TT):
                    pe.wait_ge(s_free, 4 * E + (t + 1))
                    ts = slice(t * P, (t + 1) * P)
                    bank = PS[:, 6 + t % 2, :]
                    three(bank, mh0[p][:, ts], ml0[p][:, ts], eh[q][:, W0:W1], el[q][:, W0:W1], True, False)
                    mm(bank, mst[p][:, ts], eh[q][:, W1:W1 + D], start=False, stop=False)
                    mm(bank, mst[p][ML:P, ts], el[q][ML:P, W1:W1 + D], start=False, stop=True).then_inc(s_mdn, 1)

            def expert_pair(it, last):
                for l in range(8):
                    if l < 7:
                        expert_up(it * 8 + (l + 1), l + 1, it * 2 + (l + 1) // 4)
                    elif not last:
                        expert_up(it * 8 + 8, 8, it * 2 + 2)
                    expert_down(it * 8 + l, l)

            pe.wait_ge(s_ro, 6 * NT)
            expert_up(0, 0, 0)
            with pe.Fori(0, NE // 2 - 1) as it:
                expert_pair(it, False)
            expert_pair(NE // 2 - 1, True)


def kernel(x, ctx_2048, mask_BxS2_bk0, L0_xattn_decay, L0_xattn_W_in, L0_xattn_b_in, L0_xattn_W_out,
           L0_xattn_b_out, L0_xattn_gamma, L0_xattn_beta, L0_ffn_SU_ug, L0_ffn_SU_dp, L0_ffn_Wscale_ug,
           L0_ffn_Wscale_dp, L0_ffn_W_up, L0_ffn_W_gate, L0_ffn_W_down, L1_ffn_gate_kernel, L1_ffn_gate_proj,
           L1_ffn_up_proj, L1_ffn_down_proj):
    import concourse.bacc as bacc
    from concourse.bass_utils import run_bass_kernel_spmd

    asc = np.ascontiguousarray

    def column(v):
        return np.reshape(np.asarray(v), (-1, P)).T

    ws = np.asarray(L0_ffn_Wscale_ug)
    cols = asc(np.concatenate([column(L0_xattn_b_in), column(L0_ffn_SU_ug), column(L0_ffn_SU_dp),
                               column(ws[:INTER]), column(ws[INTER:]),
                               np.broadcast_to(np.reshape(np.asarray(L0_xattn_decay), (1, 1)), (P, 1))], axis=1))
    rows = asc(np.broadcast_to(np.stack([np.asarray(L0_xattn_gamma), np.asarray(L0_xattn_beta),
                                         np.asarray(L0_xattn_b_out), np.asarray(L0_ffn_Wscale_dp)])[None], (P, 4, D)))
    gate, up, down = (np.asarray(a) for a in (L1_ffn_gate_proj, L1_ffn_up_proj, L1_ffn_down_proj))
    gu = np.concatenate([gate, up[:, :, P:], up[:, :, :P]], axis=2)
    gu = np.reshape(np.transpose(np.reshape(gu, (NE, KC, P, 2 * M)), (0, 2, 1, 3)), (NE, P, KC * 2 * M))
    experts = asc(np.concatenate([gu, down[:, :P], np.concatenate([down[:, P:], down[:, P:]], axis=1)], axis=2))
    h = np.array([[1.0]])
    while h.shape[0] < P:
        h = np.block([[h, h], [h, -h]])
    xin = np.asarray(x)
    arrays = {
        "x": asc(np.reshape(xin, (B * S, D))),
        "ctxT": asc(np.transpose(np.asarray(ctx_2048), (0, 2, 1))),
        "ctx": asc(np.asarray(ctx_2048)),
        "mask": asc(np.broadcast_to(np.reshape(np.asarray(mask_BxS2_bk0), (1, B * T2)), (P, B * T2))),
        "winT": asc(np.asarray(L0_xattn_W_in).T),
        "woutT": asc(np.asarray(L0_xattn_W_out).T),
        "cols": cols,
        "rows": rows,
        "wupT": asc(np.asarray(L0_ffn_W_up).T),
        "wgateT": asc(np.asarray(L0_ffn_W_gate).T),
        "wdT": asc(np.asarray(L0_ffn_W_down).T),
        "gk": asc(np.asarray(L1_ffn_gate_kernel)),
        "experts": experts,
        "ident": np.eye(P, dtype=np.float32),
        "had": asc(np.stack([h, -h], axis=1).astype(np.float16)),
    }
    nc = bacc.Bacc("TRN2", target_bir_lowering=False, num_devices=1)
    args = [nc.dram_tensor(f"in_{n}", a.shape, mybir.dt.from_np(a.dtype), kind="ExternalInput").ap() for n, a in arrays.items()]
    out = nc.dram_tensor("out", (B * S, D), F32, kind="ExternalOutput").ap()
    build(nc, *args, out)
    r = run_bass_kernel_spmd(nc, [{f"in_{n}": a for n, a in arrays.items()}], core_ids=[0])
    return np.reshape(r.results[0]["out"], xin.shape)
```

```python
from contextlib import ExitStack

import numpy as np

import concourse.bass as bass
from concourse import mybir

F32 = mybir.dt.float32
F16 = mybir.dt.float16
U8 = mybir.dt.uint8
I32 = mybir.dt.int32
ALU = mybir.AluOpType
ACT = mybir.ActivationFunctionType
AXX = mybir.AxisListType.X

P = 128
B, S, D, T2 = 4, 512, 512, 1024
KC = D // P
TT = S // P
NT = B * TT
INTER = 2048
FC = INTER // P
NE, M, TOPK = 32, 192, 8
ML = M - P
GU = 2 * M
EW = KC * GU + 2 * D
EH = EW // 2
EL = KC * GU + D
E16 = EW + EL
NTOK = B * S
NTILE = NTOK * TOPK // P + NE
TABLE = NTILE + 8
LIST = NTOK // P
TW = D + NE
U = 8
AHEAD = U // 2
V = 4
NEWTON = 13
MAGIC = 0x5F3759DF
KEYC = T2 // P
EPS = 1e-5
W_S = 256.0
U_S = 32.0
H_S = 64.0
C_S = 64.0
P_S = 1024.0
E_S = 64.0
C_BIN, C_SUG, C_SDP, C_WU, C_WG, C_DEC = 0, KC, 2 * KC, 2 * KC + FC, 2 * KC + 2 * FC, 2 * KC + 3 * FC
NCOL = C_DEC + 1


def wait(eng, sem, value):
    if isinstance(value, int) and value <= 0:
        return
    eng.wait_ge(sem, value)


def wait_apart(eng, sem, value, passed):
    eng.wait_ge(sem, value)
    eng.sem_inc(passed, 1)


def build(nc, a_x, a_ctxT, a_ctx, a_mask, a_winT, a_woutT, a_cols, a_rows, a_wupT, a_wgateT, a_wdT,
          a_gk, a_exp, a_ident, a_had, a_tri, d_exp, d_list, d_tok, a_out):
    ctx = ExitStack()
    with ctx:
        def sb(name, shape, dt):
            return ctx.enter_context(nc.sbuf_tensor(name, shape, dt))

        def sem(name):
            return ctx.enter_context(nc.semaphore(name))

        X = sb("X", [P, NT * D], F32)
        HT = sb("HT", [P, 8192], F32)
        Z = sb("Z", [P, TT, D], F32)
        SUMM = sb("SUMM", [P, B, D], F32)
        ROWS = sb("ROWS", [P, 4, D], F32)
        COLS = sb("COLS", [P, NCOL], F32)
        BIG = sb("BIG", [P, 24576], F32)
        EX = sb("EX", [P, 3072], F32)
        ident = sb("ident", [P, P], F32)
        had = sb("had", [P, 2, P], F16)
        st = sb("st", [P, TT, 6], F32)
        mv = sb("mv", [P, TT, 2], F32)
        ve = sb("ve", [P, TT], F32)
        rs = sb("rs", [P, TT], F32)
        epsc = sb("epsc", [P, TT], F32)
        mhalf = sb("mhalf", [P, TT], F32)
        sm = sb("sm", [P, 16], F32)
        SG = sb("SG", [P, 2, FC], F32)
        SDPC = sb("SDPC", [P, FC], F32)
        cm = sb("cm", [P, KC, B], F32)
        sT = sb("sT", [P, KC, B], F32)
        valid = sb("valid", [P, B], F32)
        attn = sb("attn", [P, 2, 6], F32)
        nw = sb("nw", [P, 4, TT], F32)
        gk = sb("gk", [P, KC, NE], F32)
        gkh = sb("gkh", [P, KC, NE], F16)
        gkl = sb("gkl", [P, KC, NE], F16)
        tri = sb("tri", [P, 4, P], F16)
        RT = sb("RT", [P, 4, TT, NE], F32)
        G = sb("G", [P, 2, TT, NE], F32)
        SEL = sb("SEL", [P, TT, NE], F16)
        SELS = sb("SELS", [P, NE], F16)
        M8 = sb("M8", [P, TT, 8], F32)
        RS = sb("RS", [P, 2, TT], F32)
        RI = sb("RI", [P, 3, TT * NE], I32)
        RP = sb("RP", [P, TT * NE], F32)
        EOFF = sb("EOFF", [P, TT, NE], F32)
        POS = sb("POS", [P, 2, TT, 8], I32)
        IDS = sb("IDS", [P, NT], I32)
        IDC = sb("IDC", [P, 2, TT], I32)
        PS = ctx.enter_context(nc.psum_tensor("PS", [P, 8, 512], F32))

        def f16(t, start, shape):
            n = int(np.prod(shape)) // 2
            v = t[:, start:start + n].bitcast(F16)
            if len(shape) == 2:
                return v.rearrange("p (a b) -> p a b", a=shape[0])
            return v

        def f32(t, start, shape):
            v = t[:, start:start + int(np.prod(shape))]
            if len(shape) == 2:
                return v.rearrange("p (a b) -> p a b", a=shape[0])
            return v

        cxT = [f32(BIG, i * 4096, (KC, T2)) for i in range(2)]
        winT = f32(BIG, 8192, (KC, D))
        woutT = f32(BIG, 10240, (KC, D))
        vrow = BIG[:, 12288:12288 + T2]
        ones = BIG[:, 13312:13312 + T2]
        junk = BIG[:, 14336:14336 + T2]
        sTb = Z[:, :, :].rearrange("p a b -> p (a b)").rearrange("p (i m) -> p i m", m=P)
        WA = f32(HT, 0, (FC, P))
        WB = f32(HT, 2048, (FC, P))
        Sh = f16(EX, 0, (FC, P))
        Sl = f16(EX, 1024, (FC, P))
        wst = [f32(HT, 4096 + i * 2048, (KC, 512)) for i in range(2)]
        wh = f16(BIG, 0, (KC, 2 * INTER))
        wl = f16(BIG, 8192, (KC, 2 * INTER))
        w2h = f16(BIG, 16384, (FC, D))
        w2l = f16(BIG, 20480, (FC, D))
        hh = f16(HT, 0, (KC, S))
        hl = f16(HT, 1024, (KC, S))
        uh = f16(HT, 2048, (KC, S))
        ul = f16(HT, 3072, (KC, S))
        gs = [EX[:, i * 512:(i + 1) * 512] for i in range(2)]
        af = [EX[:, 1024 + i * 512:1536 + i * 512] for i in range(2)]
        ah = [f16(EX, 2048 + i * 256, (512,)) for i in range(2)]
        al = [f16(EX, 2560 + i * 256, (512,)) for i in range(2)]
        qh = f16(HT, 0, (KC, 2 * S))
        ql = f16(HT, 2048, (KC, 2 * S))
        cTst = f32(HT, 4096, (KC, T2))
        cTh = [f16(BIG, i * 8192, (KC, T2)) for i in range(2)]
        cTl = [f16(BIG, i * 8192 + 2048, (KC, T2)) for i in range(2)]
        cNh = [f16(BIG, i * 8192 + 4096, (KEYC, D)) for i in range(2)]
        cNl = [f16(BIG, i * 8192 + 6144, (KEYC, D)) for i in range(2)]
        cNst = f32(BIG, 16384, (KEYC, D))
        bias = BIG[:, 20480:24576]
        mask = EX[:, 0:1024].bitcast(U8)
        sc = EX[:, 0:1024]
        pr = EX[:, 1024:2048]
        pTh = f16(EX, 2048, (KEYC, P))
        pTl = f16(EX, 2560, (KEYC, P))
        spare_rows = BIG[:, 15360:15360 + NE * LIST].bitcast(I32)
        est = [HT[:, 4096 + i * EH:4096 + (i + 1) * EH] for i in range(2)]
        eoh = f16(HT, 4096 + 2 * EH, (EH,))
        eol = f16(HT, 4096 + 2 * EH + EH // 2, (EH,))
        rh = f16(SUMM[:, :, :].rearrange("p b d -> p (b d)"), 0, (KC, S))
        rl = f16(SUMM[:, :, :].rearrange("p b d -> p (b d)"), KC * S // 2, (KC, S))
        we = f16(BIG, 0, (2 * E16,))
        o = E16
        xg = [BIG[:, o + i * TW:o + (i + 1) * TW] for i in range(U)]
        o += U * TW
        yt = [BIG[:, o + i * D:o + (i + 1) * D] for i in range(V)]
        o += V * D
        xh = [f16(BIG, o + i * D // 2, (KC, P)) for i in range(2)]
        xl = [f16(BIG, o + D + i * D // 2, (KC, P)) for i in range(2)]
        o += 2 * D
        eg = [BIG[:, o + i * M:o + (i + 1) * M] for i in range(2)]
        o += 2 * M
        ea = [BIG[:, o + i * 2 * P:o + (i + 1) * 2 * P] for i in range(2)]
        o += 4 * P
        eah = [f16(BIG, o + i * P, (2 * P,)) for i in range(2)]
        eal = [f16(BIG, o + (2 + i) * P, (2 * P,)) for i in range(2)]
        zrow = BIG[:, o + 4 * P:o + 4 * P + TW]
        o = [0]

        def ex(n, dt=F32, p=P):
            v = EX[0:p, o[0]:o[0] + n]
            o[0] += n
            return v if dt is F32 else v.bitcast(dt)

        IDX = ex(NE * LIST + 1, I32)
        TROW = ex(TABLE)
        TCMP = ex(TABLE // 2, F16)
        CE = ex(1)
        CI = ex(2, I32)
        CH = ex(1, F16)
        TWK = ex(4 * TABLE, p=1).rearrange("p (a t) -> p a t", a=4)
        TAB = ex(5 * TABLE, I32, p=1).rearrange("p (a t) -> p a t", a=5)
        TCUM = ex(NE, I32, p=1)
        GIX = ex(U, I32)

        def xt(tile):
            return X[:, bass.ds(tile * D, D)]

        s_const, s_wio, s_x, s_gk, s_mask, s_out = (sem(n) for n in (
            "const_landed", "mixer_weights_landed", "x_landed", "router_landed", "mask_landed", "out_landed"))
        s_cx = [sem(f"mixer_context_landed{i}") for i in range(2)]
        s_ws = [sem(f"ffn_weights_landed{i}") for i in range(2)]
        s_wd = sem("down_slice_landed")
        s_cT, s_cN = sem("keys_landed"), sem("values_landed")
        s_est = [sem(f"expert_half_landed{i}") for i in range(2)]
        s_eh, s_el, s_el2, s_eo = sem("expert_half_hi"), sem("expert_half_lo"), sem("expert_rows_lo"), sem("expert_half_stored")
        s_setup, s_dec, s_pre = sem("pool_consts_set"), sem("decay_gate_ready"), sem("mixer_step")
        s_ttr, s_st, s_sT, s_sTb, s_smp, s_summ = (sem(n) for n in (
            "context_summed", "states_product", "states_ready", "states_spread", "summary_product", "summary_ready"))
        s_fly, s_sh, s_sl, s_w2p, s_w2f, s_w2h, s_w2l = (sem(n) for n in (
            "butterfly_done", "down_split_hi", "down_split_lo", "down_product", "down_scaled", "down_hi", "down_lo"))
        s_wuh, s_wul = sem("ffn_weights_hi"), sem("ffn_weights_lo")
        s_bn, s_mv, s_ve, s_rs = (sem(n) for n in ("ln_stats", "ln_moments", "ln_var_eps", "ln_rstd"))
        s_z, s_h = sem("mixer_ln_step"), sem("normalised")
        s_tr, s_thi, s_tlo, s_hd = (sem(n) for n in (
            "transposed", "transposed_hi", "transposed_lo", "hadamard_done"))
        s_g, s_u, s_silu, s_a, s_ah, s_al, s_dn, s_x2 = (sem(n) for n in (
            "gate_product", "up_product", "silu_ready", "hidden_ready", "hidden_hi", "hidden_lo",
            "down_used_hidden", "ffn_added"))
        s_passed, s_ppassed, s_spassed = sem("wait_passed"), sem("pool_wait_passed"), sem("sync_wait_passed")
        s_bias, s_val = sem("bias_ready"), sem("valid_ready")
        s_cth, s_ctl, s_cnh, s_cnl = (sem(n) for n in ("keys_hi", "keys_lo", "values_hi", "values_lo"))
        s_sc, s_s, s_mx, s_nm, s_p, s_pt, s_pth, s_ptl, s_rc, s_rv, s_rd, s_xr = (sem(n) for n in (
            "scores_product", "scores_ready", "max_ready", "negmax_ready", "probs_ready", "probs_transposed",
            "probs_hi", "probs_lo", "sum_inverted", "sum_scaled", "readout_product", "readout_added"))
        s_nw = sem("inverse_root_step")
        s_gkh, s_gkl, s_rc0 = sem("router_hi"), sem("router_lo"), sem("router_consts")
        s_lg, s_L, s_m8, s_mr, s_sel, s_dif, s_rex, s_gx, s_gs, s_grc, s_G = (sem(n) for n in (
            "logits_product", "logits_ready", "top8_ready", "top8_replaced", "selection_ready", "logits_minus_max",
            "router_exp", "selected_exp", "selected_sum", "selected_inverse", "routing_weights_ready"))
        s_rkp, s_rk, s_ro, s_pos, s_idc, s_ss = (sem(n) for n in (
            "rank_product", "rank_copied", "place_step", "places_ready", "batch_ids_ready", "selected_so_far"))
        s_ids = [sem(f"ids_listed{i}") for i in range(2)]
        s_idu = sem("places_used")
        s_lst, s_zst, s_gst, s_res, s_zr, s_spare, s_idx = (sem(n) for n in (
            "lists_cleared", "tokens_stored", "routing_weights_stored", "residual_stored", "zero_row_ready",
            "spare_rows_cleared", "lists_landed"))
        s_tp, s_tq, s_tab = sem("table_product"), sem("table_step"), sem("tables_ready")
        s_wl = sem("expert_landed")
        s_gi = sem("tile_rows_ready")
        s_xg = [sem(f"tile_gathered{i}") for i in range(U)]
        s_add = [sem(f"tile_added{i}") for i in range(V)]
        s_xt, s_xh, s_xl, s_ug, s_es, s_ea, s_at, s_ah2, s_al2, s_ed, s_y = (sem(n) for n in (
            "tile_transposed", "tile_hi", "tile_lo", "tile_gate_up", "tile_silu", "tile_hidden", "hidden_transposed",
            "hidden_t_hi", "hidden_t_lo", "tile_down", "tile_weighted"))

        block = ctx.enter_context(nc.Block())
        NCONST = 5

        @block.sync
        def _(sp):
            sp.dma_start(COLS[:, :], a_cols).then_inc(s_const, 16)
            sp.dma_start(ROWS[:, :, :], a_rows).then_inc(s_const, 16)
            sp.dma_start(ident[:, :], a_ident).then_inc(s_const, 16)
            sp.dma_start(had[:, :, :], a_had).then_inc(s_const, 16)
            sp.dma_start(tri[:, :, :], a_tri).then_inc(s_const, 16)
            sp.wait_ge(s_rc0, 1)
            sp.dma_start(d_list.rearrange("(p c) a -> p (c a)", p=P), spare_rows).then_inc(s_lst, 16)
            for b in range(B):
                if b >= 2:
                    sp.wait_ge(s_ttr, (b - 1) * KC)
                sp.dma_start(cxT[b % 2], a_ctxT[b].rearrange("(k p) t -> p k t", p=P)).then_inc(s_cx[b % 2], 16)
                if b == 1:
                    sp.dma_start(winT, a_winT.rearrange("(k p) e -> p k e", p=P)).then_inc(s_wio, 16)
                    sp.dma_start(woutT, a_woutT.rearrange("(k p) e -> p k e", p=P)).then_inc(s_wio, 16)
            sp.dma_start(X[:, :].rearrange("p (t d) -> p t d", d=D),
                         a_x.rearrange("(t p) d -> p t d", p=P)).then_inc(s_x, 16)
            sp.dma_start(gk[:, :, :], a_gk.rearrange("(k p) e -> p k e", p=P)).then_inc(s_gk, 16)
            up = a_wupT.rearrange("(k p) f -> p k f", p=P)
            gate = a_wgateT.rearrange("(k p) f -> p k f", p=P)
            for c in range(8):
                if c >= 2:
                    sp.wait_ge(s_wul, c - 1)
                src = (up, gate)[c % 2]
                sp.dma_start(wst[c % 2], src[:, :, (c // 2) * 512:(c // 2 + 1) * 512]).then_inc(s_ws[c % 2], 16)
            def load_half(e, h):
                src = a_exp[bass.ds(e, 1), :, h * EH:(h + 1) * EH].rearrange("a p w -> p (a w)")
                sp.dma_start(est[h], src).then_inc(s_est[h], 16)

            def store_half(e, h):
                dst = d_exp[bass.ds(e, 1), :, :].rearrange("a p w -> p (a w)")
                nl = (EH, EL - EH)[h]
                sp.dma_start(dst[:, h * EH:(h + 1) * EH], eoh).then_inc(s_eo, 16)
                sp.dma_start(dst[:, EW + h * EH:EW + h * EH + nl], eol[:, 0:nl]).then_inc(s_eo, 16)

            sp.wait_ge(s_wul, 8)
            for h in range(2):
                load_half(0, h)
            with sp.Fori(0, NE - 1) as e:
                for h in range(2):
                    sp.wait_ge(s_el, e * 2 + (h + 1))
                    store_half(e, h)
                    load_half(e + 1, h)
            for h in range(2):
                sp.wait_ge(s_el, 2 * NE - 1 + h)
                store_half(NE - 1, h)

            def load_keys(b):
                if b:
                    sp.wait_ge(s_ctl, b)
                sp.dma_start(cTst, a_ctxT[b].rearrange("(k p) t -> p k t", p=P)).then_inc(s_cT, 16)

            def load_values(b):
                if b:
                    sp.wait_ge(s_cnl, b)
                sp.dma_start(cNst, a_ctx[b].rearrange("(c p) d -> p c d", p=P)).then_inc(s_cN, 16)

            def store_routed(b):
                rows = d_tok[b * S:(b + 1) * S, :].rearrange("(t p) w -> p t w", p=P)
                sp.wait_ge(s_h, TT * (B + 4 * (b // 2) + 3 + b % 2))
                sp.dma_start(rows[:, :, 0:D], Z[:, :, :]).then_inc(s_zst, 16)
                sp.wait_ge(s_G, b + 1)
                sp.dma_start(rows[:, :, D:TW], G[:, b % 2, :, :]).then_inc(s_gst, 16)

            sp.wait_ge(s_eo, 1 + 64 * NE)
            load_keys(0)
            sp.wait_ge(s_x2, NT)
            sp.dma_start(mask, a_mask).then_inc(s_mask, 16)
            load_values(0)
            load_keys(1)
            load_values(1)
            load_keys(2)
            load_values(2)
            store_routed(0)
            store_routed(1)
            load_keys(3)
            load_values(3)
            store_routed(2)
            for b in range(B):
                sp.wait_ge(s_xr, TT * (b + 1))
                sp.dma_start(a_out[b * S:(b + 1) * S, :].rearrange("(t p) d -> p t d", p=P),
                             X[:, b * TT * D:(b + 1) * TT * D].rearrange("p (t d) -> p t d", d=D)).then_inc(s_res, 16)
            store_routed(3)
            def load_expert(e, h):
                src = d_exp[bass.ds(e, 1), :, :].rearrange("a p w -> p (a w)")
                sp.dma_start(we[:, h * E16:(h + 1) * E16], src).then_inc(s_wl, 16)

            load_expert(0, 0)
            sp.wait_ge(s_wl, 16)
            load_expert(1, 1)
            sp.wait_ge(s_zr, 3)
            sp.dma_start(d_tok[NTOK:NTOK + P, :], zrow).then_inc(s_spare, 16)
            sp.dma_start(a_out[NTOK:NTOK + P, :], zrow[:, 0:D]).then_inc(s_spare, 16)
            for i in range(2):
                sp.wait_ge(s_ids[i], B // 2 * 16 * TT * TOPK)
            sp.dma_start(IDX[:, 0:NE * LIST], d_list.rearrange("(p c) a -> p (c a)", p=P)).then_inc(s_idx, 16)
            sp.wait_ge(s_tab, 1)
            with sp.Fori(1, NE // 2) as i:
                for h in range(2):
                    wait_apart(sp, s_wl, i * 32 + 16 * h, s_spassed)
                    done = sp.value_load(TCUM[0:1, bass.ds(i * 2 + (h - 2), 1)], min_val=1, max_val=NTILE + 1)
                    sp.wait_ge(s_ed, done)
                    load_expert(i * 2 + h, h)
            for w in range(V):
                sp.wait_ge(s_add[w], 16 + 16 * (NTILE // V))

        @block.gpsimd
        def _(pool):
            pool.memset(epsc[:, :], EPS).then_inc(s_setup, 1)
            pool.memset(mhalf[:, :], -0.5).then_inc(s_setup, 1)
            pool.iota(spare_rows, pattern=[[0, NE * LIST]], base=NTOK, channel_multiplier=1).then_inc(s_rc0, 1)
            pool.iota(IDS[:, :], pattern=[[P, NT]], base=0, channel_multiplier=1).then_inc(s_rc0, 1)
            pool.iota(EOFF[:, :, :], pattern=[[0, TT], [LIST, NE]], base=1, channel_multiplier=0,
                      allow_small_or_imprecise_dtypes=True).then_inc(s_rc0, 1)
            pool.memset(SELS[:, :], 0.0).then_inc(s_ss, 1)
            pool.sem_inc(s_idu, 1)
            pool.sem_inc(s_eo, 1)
            pool.sem_inc(s_ed, 1)
            for s in range(4):
                if s:
                    pool.wait_ge(s_sl, s)
                pool.dma_start(WA, a_wdT[:, s * P:(s + 1) * P].rearrange("(c p) d -> p c d", p=P)).then_inc(s_wd, 16)
                pool.wait_ge(s_wd, 16 * (s + 1))
                if s:
                    pool.wait_ge(s_w2l, s)
                src, dst = WA, WB
                for n, h in enumerate((1, 2, 4, 8)):
                    i = src.rearrange("p (g t h) d -> p g t (h d)", t=2, h=h)
                    q = dst.rearrange("p (g t h) d -> p g t (h d)", t=2, h=h)
                    if n:
                        pool.wait_ge(s_fly, 8 * s + 2 * n)
                    pool.tensor_tensor(q[:, :, 0, :], i[:, :, 0, :], i[:, :, 1, :], ALU.add).then_inc(s_fly, 1)
                    pool.tensor_tensor(q[:, :, 1, :], i[:, :, 0, :], i[:, :, 1, :], ALU.subtract).then_inc(s_fly, 1)
                    src, dst = dst, src
            pool.wait_ge(s_setup, 2)
            with pool.Fori(0, 3 * B) as n:
                pool.wait_ge(s_mv, n * TT + TT)
                pool.tensor_tensor(ve[:, :], mv[:, :, 1], epsc[:, :], ALU.add).then_inc(s_ve, 1)
                pool.wait_ge(s_ve, n + 1)
                pool.tensor_tensor(rs[:, :], ve[:, :], mhalf[:, :], ALU.pow).then_inc(s_rs, 1)
            pool.wait_ge(s_lst, 16)
            with pool.Fori(0, B // 2) as it:
                for j in range(2):
                    wait_apart(pool, s_pos, it * 2 + (j + 1), s_ppassed)
                    for t in range(TT):
                        for c in range(TOPK):
                            pool.indirect_dma_start(d_list, bass.IndirectOffsetOnAxis(ap=POS[:, j, t, c:c + 1], axis=0),
                                                    IDC[:, j, t:t + 1], None).then_inc(s_ids[j], 16)
                for j in range(2):
                    pool.wait_ge(s_ids[j], it * (16 * TT * TOPK) + 16 * TT * TOPK)
                pool.sem_inc(s_idu, 1)
            pool.wait_ge(s_xr, NT)
            pool.memset(zrow, 0.0).then_inc(s_zr, 1)
            pool.iota(IDX[:, NE * LIST:NE * LIST + 1], pattern=[[0, 1]], base=NTOK, channel_multiplier=1).then_inc(s_zr, 1)
            pool.iota(TROW, pattern=[[1, TABLE]], base=0, channel_multiplier=0,
                      allow_small_or_imprecise_dtypes=True).then_inc(s_zr, 1)

            pool.wait_ge(s_idx, 16)
            pool.wait_ge(s_tab, 1)
            pool.wait_ge(s_zst, 16 * B)
            pool.wait_ge(s_gst, 16 * B)
            pool.wait_ge(s_res, 16 * B)
            pool.wait_ge(s_spare, 32)
            for w in range(V):
                pool.dma_start(yt[w][0:1, :], d_tok[NTOK:NTOK + 1, 0:D]).then_inc(s_add[w], 16)

            def gather(t, u, n):
                col = pool.value_load(TAB[0:1, 3, bass.ds(t, 1)], min_val=0, max_val=NE * LIST)
                if n is not None:
                    pool.wait_ge(s_add[u % V], n * 16 + 16)
                pool.tensor_copy(GIX[:, u:u + 1], IDX[:, bass.ds(col, 1)]).then_inc(s_gi, 1)
                wait_apart(pool, s_gi, t + 1, s_ppassed)
                pool.indirect_dma_start(xg[u], None, d_tok, bass.IndirectOffsetOnAxis(ap=GIX[:, u:u + 1], axis=0))\
                    .then_inc(s_xg[u], 16)

            def add(t, u):
                first = pool.value_load(TAB[0:1, 4, bass.ds(t, 1)], min_val=0, max_val=NTILE - 1)
                for w in range(V):
                    pool.wait_ge(s_add[w], ((first + (V - 1 - w)) // V) * 16 + 16)
                wait_apart(pool, s_y, t + 1, s_ppassed)
                pool.indirect_dma_start(a_out, bass.IndirectOffsetOnAxis(ap=GIX[:, u:u + 1], axis=0), yt[u % V], None,
                                        compute_op=ALU.add).then_inc(s_add[u % V], 16)

            for t in range(AHEAD):
                gather(t, t, None)
            for u in range(U):
                gather(u + AHEAD, (u + AHEAD) % U, 1 if u + AHEAD >= U else None)
                add(u, u)
            with pool.Fori(1, NTILE // U) as it:
                for u in range(U):
                    t = it * U + u
                    gather(t + AHEAD, (u + AHEAD) % U, it * (U // V) + (u + AHEAD - U) // V + 1)
                    add(t, u)

        @block.scalar
        def _(act):
            act.wait_ge(s_const, 16 * NCONST)
            act.wait_ge(s_lst, 16)
            act.activation(sm[:, 0:1], COLS[:, C_DEC:C_DEC + 1], ACT.Sigmoid).then_inc(s_dec, 1)
            for s in range(4):
                act.wait_ge(s_fly, 8 * (s + 1))
                if s:
                    act.wait_ge(s_w2p, 4 * s)
                act.activation(Sh, WA, ACT.Copy, scale=W_S).then_inc(s_sh, 1)
                act.wait_ge(s_w2f, FC * (s + 1))
                act.activation(w2h[:, :, s * P:(s + 1) * P], WB, ACT.Copy).then_inc(s_w2h, 1)
            act.wait_ge(s_summ, B)
            for c in range(8):
                act.wait_ge(s_ws[c % 2], 16 * (c // 2 + 1))
                o = (c % 2) * INTER + (c // 2) * 512
                act.activation(wh[:, :, o:o + 512], wst[c % 2], ACT.Copy, scale=W_S).then_inc(s_wuh, 1)

            def transposed_hi(q, e, dst, bank, scale, sem_in):
                act.wait_ge(sem_in, q)
                act.activation(dst, PS[:, bank, :], ACT.Copy, scale=scale).then_inc(s_thi, 1)

            def ffn_prep(b):
                for k in range(KC):
                    transposed_hi(b * 4 + (k + 1), None, uh[:, k, :], 4 + k % 2, COLS[:, C_SUG + k:C_SUG + k + 1], s_tr)
                for j in range(KC):
                    transposed_hi(b * 4 + (j + 1), None, hh[:, j, :], 4 + j % 2, 1.0, s_hd)

            def ffn_chunk(F, f, p, first):
                act.wait_ge(s_g, F + 1)
                if not first:
                    act.wait_ge(s_a, F - 1)
                act.activation(gs[p], PS[:, 2 * p, :], ACT.Silu, scale=SG[:, 1, f]).then_inc(s_silu, 1)
                act.wait_ge(s_a, F + 1)
                if not first:
                    act.wait_ge(s_dn, F - 1)
                act.activation(ah[p], af[p], ACT.Copy).then_inc(s_ah, 1)

            def split_half(e, h):
                act.wait_ge(s_est[h], e * 16 + 16)
                act.wait_ge(s_eo, e * 64 + (1 + 32 * h))
                act.activation(eoh, est[h], ACT.Copy, scale=E_S).then_inc(s_eh, 1)

            def ffn_batch(b):
                for p in range(2):
                    ffn_chunk(b * FC + p, slice(p, p + 1), p, True)
                    split_half(b * (FC // 2), p)
                with act.Fori(1, FC // 2) as i:
                    for p in range(2):
                        ffn_chunk(b * FC + i * 2 + p, bass.ds(i * 2 + p, 1), p, False)
                        split_half(b * (FC // 2) + i, p)

            act.wait_ge(s_pre, 2)
            ffn_prep(0)
            with act.Fori(0, B - 1) as b:
                ffn_batch(b)
                ffn_prep(b + 1)
            ffn_batch(B - 1)

            def keys_hi(b, p):
                act.wait_ge(s_cT, b * 16 + 16)
                act.activation(cTh[p], cTst, ACT.Copy, scale=C_S).then_inc(s_cth, 1)

            def values_hi(b, p):
                act.wait_ge(s_cN, b * 16 + 16)
                act.activation(cNh[p], cNst, ACT.Copy, scale=C_S).then_inc(s_cnh, 1)

            def exp_tile(t, l):
                act.wait_ge(s_nm, t + 1)
                if l:
                    act.wait_ge(s_pt, t)
                act.activation(pr, sc, ACT.Exp, bias=attn[:, l % 2, 1:2], accum_out=attn[:, l % 2, 2:3])\
                    .then_inc(s_p, 1)

            def round_hi(q, k, dst, bank):
                transposed_hi(q * 4 + (k + 1), None, dst, bank, H_S, s_tr)

            def router_exp(b):
                act.wait_ge(s_dif, b + 1)
                act.activation(RT[:, 3, :, :], RT[:, 2, :, :], ACT.Exp).then_inc(s_rex, 1)

            act.wait_ge(s_gk, 16)
            act.activation(gkh[:, :, :], gk[:, :, :], ACT.Copy, scale=E_S).then_inc(s_gkh, 1)
            act.wait_ge(s_x2, NT)
            with act.Fori(0, B // 2) as it:
                q = it * 4 + B
                keys_hi(it * 2, 0)
                for blk in range(2):
                    for k in range(KC):
                        round_hi(q + blk, k, qh[:, k, blk * S:(blk + 1) * S], 6 + k % 2)
                values_hi(it * 2, 0)
                exp_tile(it * 8, 0)
                for l in range(8):
                    if l in (5, 6):
                        for k in (2 * (l - 5), 2 * (l - 5) + 1):
                            round_hi(q + 2, k, rh[:, k, :], 7)
                    act.wait_ge(s_pt, it * 8 + (l + 1))
                    if l:
                        act.wait_ge(s_rd, it * 8 + l)
                    act.activation(pTh, PS[:, 4:6, :].rearrange("p b (c n) -> p (b c) n", n=P), ACT.Copy, scale=P_S)\
                        .then_inc(s_pth, 1)
                    if l == 0:
                        keys_hi(it * 2 + 1, 1)
                        values_hi(it * 2 + 1, 1)
                    if l < 7:
                        exp_tile(it * 8 + (l + 1), l + 1)
                router_exp(it * 2)
                for k in range(KC):
                    round_hi(q + 3, k, rh[:, k, :], 6 + k % 2)
                router_exp(it * 2 + 1)

            def tile_hi(t, p):
                act.wait_ge(s_xt, t + 1)
                act.activation(xh[p], PS[:, p, :].rearrange("p (k n) -> p k n", n=P), ACT.Copy, scale=H_S).then_inc(s_xh, 1)

            def tile_silu(t, p):
                act.wait_ge(s_ug, t + 1)
                act.activation(eg[p], PS[:, 2 + p, 0:M], ACT.Silu, scale=1.0 / (H_S * E_S)).then_inc(s_es, 1)

            def hidden_hi(t, p):
                act.wait_ge(s_at, t + 1)
                act.activation(eah[p], PS[:, 4, 0:2 * P], ACT.Copy).then_inc(s_ah2, 1)

            tile_hi(0, 0)
            tile_hi(1, 1)
            tile_silu(0, 0)
            with act.Fori(0, NTILE // U) as it:
                for u in range(U):
                    t = it * U + u
                    act.wait_ge(s_ug, t + 1)
                    tile_hi(t + 2, u % 2)
                    hidden_hi(t, u % 2)
                    tile_silu(t + 1, (u + 1) % 2)

        @block.vector
        def _(dve):
            v = nc.vector
            v.memset(ones, 1.0).then_inc(s_pre, 1)
            dve.wait_ge(s_const, 16 * NCONST)
            v.tensor_scalar(SG[:, :, :], COLS[:, C_WU:C_WU + 2 * FC].rearrange("p (a f) -> p a f", a=2),
                            1.0 / (W_S * D ** 0.5), None, ALU.mult).then_inc(s_pre, 1)
            v.tensor_scalar(SDPC[:, :], COLS[:, C_SDP:C_SDP + FC], INTER ** -0.5, None, ALU.mult).then_inc(s_pre, 1)
            dve.wait_ge(s_pre, 3)
            v.tensor_scalar(SG[:, 0, :], SG[:, 0, :], U_S, None, ALU.mult).then_inc(s_pre, 1)
            dve.wait_ge(s_dec, 1)
            v.tensor_tensor_scan(vrow, sm[:, 0:1].to_broadcast([P, T2]), ones, 0.0, ALU.mult, ALU.add)\
                .then_inc(s_pre, 1)
            dve.wait_ge(s_pre, 5)
            v.reduce_sum(sm[:, 1:2], vrow, AXX).then_inc(s_pre, 1)
            dve.wait_ge(s_pre, 6)
            v.tensor_scalar(sm[:, 2:2 + KC], COLS[:, C_BIN:C_BIN + KC], sm[:, 1:2], 1.0 / T2, ALU.mult, ALU.mult)\
                .then_inc(s_pre, 1)
            for b in range(B):
                dve.wait_ge(s_cx[b % 2], 16 * (b // 2 + 1))
                for k in range(KC):
                    if b or k:
                        dve.wait_ge(s_ttr, b * KC + k)
                    v.tensor_tensor_reduce(out=junk, in0=cxT[b % 2][:, k, :], in1=vrow[:, ::-1], scale=1.0, scalar=0.0,
                                           op0=ALU.mult, op1=ALU.add, accum_out=cm[:, k, b:b + 1]).then_inc(s_ttr, 1)
            dve.wait_ge(s_st, 1)
            dve.wait_ge(s_pre, 7)
            for k in range(KC):
                v.tensor_scalar(sT[:, k, :], PS[:, 0, k * B:(k + 1) * B], 1.0 / T2, sm[:, 2 + k:3 + k],
                                ALU.mult, ALU.add).then_inc(s_sT, 1)
            dve.wait_ge(s_sT, KC)
            v.tensor_copy(sTb, sT[:, :, :].rearrange("p k b -> p (k b)").unsqueeze(2).to_broadcast([P, KC * B, P]))\
                .then_inc(s_sTb, 1)
            for b in range(B):
                dve.wait_ge(s_smp, b + 1)
                v.tensor_tensor(SUMM[:, b, :], PS[:, 1 + b % 2, :], ROWS[:, 2, :], ALU.add).then_inc(s_summ, 1)
            for s in range(4):
                dve.wait_ge(s_sh, s + 1)
                v.scalar_tensor_tensor(Sl, WA, W_S, Sh, ALU.mult, ALU.subtract).then_inc(s_sl, 1)
                for c in range(FC):
                    if c % 4 == 0:
                        dve.wait_ge(s_w2p, 4 * s + c // 4 + 1)
                    v.scalar_tensor_tensor(WB[:, c, :], PS[:, 4 + c // 4, (c % 4) * P:(c % 4 + 1) * P],
                                           SDPC[:, c:c + 1], ROWS[:, 3, s * P:(s + 1) * P], ALU.mult, ALU.mult)\
                        .then_inc(s_w2f, 1)
                dve.wait_ge(s_w2h, s + 1)
                dve.wait_ge(s_w2f, FC * (s + 1))
                v.tensor_tensor(w2l[:, :, s * P:(s + 1) * P], WB, w2h[:, :, s * P:(s + 1) * P], ALU.subtract)\
                    .then_inc(s_w2l, 1)
            for c in range(8):
                dve.wait_ge(s_wuh, c + 1)
                o = (c % 2) * INTER + (c // 2) * 512
                v.scalar_tensor_tensor(wl[:, :, o:o + 512], wst[c % 2], W_S, wh[:, :, o:o + 512],
                                       ALU.mult, ALU.subtract).then_inc(s_wul, 1)

            def moments(n, src):
                for t in range(TT):
                    v.bn_stats(st[:, t, :], src(t)).then_inc(s_bn, 1)
                for t in range(TT):
                    wait_apart(dve, s_bn, n * TT + (t + 1), s_passed)
                    v.bn_aggr(mv[:, t, :], st[:, t, :]).then_inc(s_mv, 1)
                dve.wait_ge(s_mv, n * TT + TT)

            def stats(n, src):
                moments(n, src)
                dve.wait_ge(s_rs, n + 1)

            def inverse_root(m):
                steps = m * NEWTON
                var, half, y, work = (nw[:, i, :] for i in range(4))
                v.tensor_scalar(var, mv[:, :, 1], EPS, None, ALU.add).then_inc(s_nw, 1)
                dve.wait_ge(s_nw, steps + 1)
                v.tensor_scalar(work.bitcast(I32), var.bitcast(I32), 1, None, ALU.logical_shift_right).then_inc(s_nw, 1)
                dve.wait_ge(s_nw, steps + 2)
                v.tensor_scalar(y.bitcast(I32), work.bitcast(I32), -1, MAGIC, ALU.mult, ALU.add).then_inc(s_nw, 1)
                v.tensor_scalar(half, var, -0.5, None, ALU.mult).then_inc(s_nw, 1)
                for i in range((NEWTON - 4) // 3):
                    dve.wait_ge(s_nw, steps + (4 + 3 * i))
                    v.tensor_tensor(work, y, half, ALU.mult).then_inc(s_nw, 1)
                    dve.wait_ge(s_nw, steps + (5 + 3 * i))
                    v.tensor_tensor(work, work, y, ALU.mult).then_inc(s_nw, 1)
                    dve.wait_ge(s_nw, steps + (6 + 3 * i))
                    v.scalar_tensor_tensor(y, work, 1.5, y, ALU.add, ALU.mult).then_inc(s_nw, 1)
                dve.wait_ge(s_nw, steps + NEWTON)

            def normalise(q, tile, rstd):
                wait(dve, s_tr, q * 4)
                for t in range(TT):
                    v.tensor_scalar(Z[:, t, :], xt(tile + t), mv[:, t, 0:1], rstd[:, t:t + 1],
                                    ALU.subtract, ALU.mult).then_inc(s_h, 1)

            def mixer_ln(b, tile):
                stats(b * 3, lambda t: xt(tile + t))
                wait(dve, s_tr, b * 4)
                for t in range(TT):
                    v.tensor_scalar(Z[:, t, :], xt(tile + t), mv[:, t, 0:1], rs[:, t:t + 1],
                                    ALU.subtract, ALU.mult).then_inc(s_z, 1)
                for t in range(TT):
                    dve.wait_ge(s_z, b * 20 + (t + 1))
                    v.tensor_tensor(Z[:, t, :], Z[:, t, :], summ(b), ALU.add).then_inc(s_z, 1)
                wait_apart(dve, s_z, b * 20 + 8, s_passed)
                stats(b * 3 + 1, lambda t: Z[:, t, :])
                for t in range(TT):
                    v.scalar_tensor_tensor(Z[:, t, :], Z[:, t, :], mv[:, t, 0:1], ROWS[:, 0, :],
                                           ALU.subtract, ALU.mult).then_inc(s_z, 1)
                for t in range(TT):
                    v.tensor_tensor(xt(tile + t), xt(tile + t), ROWS[:, 1, :], ALU.add).then_inc(s_z, 1)
                for t in range(TT):
                    dve.wait_ge(s_z, b * 20 + (13 + t))
                    v.scalar_tensor_tensor(xt(tile + t), Z[:, t, :], rs[:, t:t + 1], xt(tile + t),
                                           ALU.mult, ALU.add).then_inc(s_z, 1)
                wait_apart(dve, s_z, b * 20 + 20, s_passed)
                stats(b * 3 + 2, lambda t: xt(tile + t))
                normalise(b, tile, rs)

            def summ(b):
                return SUMM[:, :, :].rearrange("p b d -> p (b d)")[:, bass.ds(b * D, D)]

            def ffn_prep_lo(b):
                for k in range(KC):
                    dve.wait_ge(s_thi, b * 8 + (k + 1))
                    v.scalar_tensor_tensor(ul[:, k, :], PS[:, 4 + k % 2, :], COLS[:, C_SUG + k:C_SUG + k + 1], uh[:, k, :],
                                           ALU.mult, ALU.subtract).then_inc(s_tlo, 1)
                for j in range(KC):
                    dve.wait_ge(s_thi, b * 8 + (5 + j))
                    v.tensor_tensor(hl[:, j, :], PS[:, 4 + j % 2, :], hh[:, j, :], ALU.subtract).then_inc(s_tlo, 1)

            def ffn_chunk(F, f, p, first):
                dve.wait_ge(s_silu, F + 1)
                dve.wait_ge(s_u, F + 1)
                if not first:
                    dve.wait_ge(s_ah, F - 1)
                v.scalar_tensor_tensor(af[p], PS[:, 2 * p + 1, :], SG[:, 0, f], gs[p], ALU.mult, ALU.mult).then_inc(s_a, 1)
                dve.wait_ge(s_ah, F + 1)
                if not first:
                    dve.wait_ge(s_dn, F - 1)
                v.tensor_tensor(al[p], af[p], ah[p], ALU.subtract).then_inc(s_al, 1)

            def split_half(e, h):
                dve.wait_ge(s_eh, e * 2 + (h + 1))
                if h == 0:
                    v.scalar_tensor_tensor(eol, est[0], E_S, eoh, ALU.mult, ALU.subtract).then_inc(s_el, 1)
                else:
                    nl = EL - EH
                    v.scalar_tensor_tensor(eol[:, 0:nl], est[1][:, 0:nl], E_S, eoh[:, 0:nl], ALU.mult, ALU.subtract)\
                        .then_inc(s_el2, 1)
                    dve.wait_ge(s_el2, e + 1)
                    v.scalar_tensor_tensor(eoh[ML:P, nl:EH], est[1][ML:P, nl:EH], E_S, eoh[ML:P, nl:EH],
                                           ALU.mult, ALU.subtract).then_inc(s_el, 1)

            def ffn_batch(b):
                for p in range(2):
                    ffn_chunk(b * FC + p, slice(p, p + 1), p, True)
                    split_half(b * (FC // 2), p)
                with dve.Fori(1, FC // 2) as i:
                    for p in range(2):
                        ffn_chunk(b * FC + i * 2 + p, bass.ds(i * 2 + p, 1), p, False)
                        split_half(b * (FC // 2) + i, p)

            def ffn_add(b):
                dve.wait_ge(s_dn, b * FC + FC)
                for t in range(TT):
                    v.scalar_tensor_tensor(xt(b * TT + t), PS[:, 4 + t, :], 1.0 / (U_S * W_S), xt(b * TT + t),
                                           ALU.mult, ALU.add).then_inc(s_x2, 1)

            dve.wait_ge(s_x, 16)
            dve.wait_ge(s_summ, B)
            mixer_ln(0, 0)
            ffn_prep_lo(0)
            with dve.Fori(0, B - 1) as b:
                ffn_batch(b)
                mixer_ln(b + 1, b * TT + TT)
                ffn_add(b)
                ffn_prep_lo(b + 1)
            ffn_batch(B - 1)
            ffn_add(B - 1)

            dve.wait_ge(s_mask, 16)
            v.tensor_scalar(bias, mask, 1.0, 1e30, ALU.subtract, ALU.mult).then_inc(s_bias, 1)
            v.reduce_max(valid[:, :], mask.rearrange("p (b t) -> p b t", b=B), AXX).then_inc(s_val, 1)
            dve.wait_ge(s_val, 1)
            v.tensor_scalar(valid[:, :], valid[:, :], 1.0 / (P_S * C_S), None, ALU.mult).then_inc(s_val, 1)
            dve.wait_ge(s_bias, 1)
            dve.wait_ge(s_x2, NT)

            def keys_lo(b, p):
                dve.wait_ge(s_cth, b + 1)
                v.scalar_tensor_tensor(cTl[p], cTst, C_S, cTh[p], ALU.mult, ALU.subtract).then_inc(s_ctl, 1)

            def values_lo(b, p):
                dve.wait_ge(s_cnh, b + 1)
                v.scalar_tensor_tensor(cNl[p], cNst, C_S, cNh[p], ALU.mult, ALU.subtract).then_inc(s_cnl, 1)

            def softmax_tile(t, l, b):
                p = l % 2
                dve.wait_ge(s_sc, t + 1)
                if l:
                    dve.wait_ge(s_p, t)
                v.scalar_tensor_tensor(sc, PS[:, 2 * p:2 * p + 2, :].rearrange("p a n -> p (a n)"),
                                       D ** -0.5 / (H_S * C_S), bias[:, bass.ds(b * T2, T2)], ALU.mult, ALU.add)\
                    .then_inc(s_s, 1)
                dve.wait_ge(s_s, t + 1)
                v.reduce_max(attn[:, p, 0:1], sc, AXX).then_inc(s_mx, 1)
                dve.wait_ge(s_mx, t + 1)
                v.tensor_scalar(attn[:, p, 1:2], attn[:, p, 0:1], -1.0, None, ALU.mult).then_inc(s_nm, 1)

            def readout_add(t, l, b):
                p = l % 2
                dve.wait_ge(s_p, t + 1)
                v.reciprocal(attn[:, p, 3:4], attn[:, p, 2:3]).then_inc(s_rc, 1)
                dve.wait_ge(s_rc, t + 1)
                v.tensor_tensor(attn[:, p, 4:5], attn[:, p, 3:4], valid[:, bass.ds(b, 1)], ALU.mult).then_inc(s_rv, 1)
                dve.wait_ge(s_rv, t + 1)
                dve.wait_ge(s_rd, t + 1)
                v.scalar_tensor_tensor(xt(t), PS[:, 6, :], attn[:, p, 4:5], xt(t), ALU.mult, ALU.add).then_inc(s_xr, 1)

            def round_lo(q, k, hi, lo, bank):
                dve.wait_ge(s_thi, q * 4 + (4 * B + k + 1))
                v.scalar_tensor_tensor(lo, PS[:, bank, :], H_S, hi, ALU.mult, ALU.subtract).then_inc(s_tlo, 1)

            def layer_norm(m, b):
                moments(m + 3 * B, lambda t: xt(b * TT + t))
                inverse_root(m)
                normalise(m + B, b * TT, nw[:, 2, :])

            def choose(b, j):
                dve.wait_ge(s_lg, b + 1)
                v.tensor_scalar(RT[:, 0, :, :], PS[:, 7, 0:TT * NE].rearrange("p (t e) -> p t e", e=NE),
                                1.0 / (H_S * E_S), None, ALU.mult).then_inc(s_L, 1)
                wait_apart(dve, s_L, b + 1, s_passed)
                for t in range(TT):
                    v.max(M8[:, t, :], RT[:, 0, t, :]).then_inc(s_m8, 1)
                wait_apart(dve, s_m8, b * TT + TT, s_passed)
                for t in range(TT):
                    v.match_replace(RT[:, 1, t, :], M8[:, t, :], RT[:, 0, t, :], -3e38).then_inc(s_mr, 1)
                v.tensor_tensor(RT[:, 2, :, :], RT[:, 0, :, :], M8[:, :, 0:1].to_broadcast([P, TT, NE]), ALU.subtract)\
                    .then_inc(s_dif, 1)
                dve.wait_ge(s_mr, b * TT + TT)
                v.tensor_tensor(SEL[:, :, :], RT[:, 0, :, :], RT[:, 1, :, :], ALU.not_equal).then_inc(s_sel, 1)
                dve.wait_ge(s_sel, b + 1)
                dve.wait_ge(s_rex, b + 1)
                v.tensor_tensor(RT[:, 1, :, :], SEL[:, :, :], RT[:, 3, :, :], ALU.mult).then_inc(s_gx, 1)
                dve.wait_ge(s_gx, b + 1)
                v.reduce_sum(RS[:, 0, :], RT[:, 1, :, :], AXX).then_inc(s_gs, 1)
                dve.wait_ge(s_gs, b + 1)
                v.reciprocal(RS[:, 1, :], RS[:, 0, :]).then_inc(s_grc, 1)
                dve.wait_ge(s_grc, b + 1)
                v.scalar_tensor_tensor(G[:, j, :, :], RT[:, 1, :, :], 1.0 / E_S,
                                       RS[:, 1, :].unsqueeze(2).to_broadcast([P, TT, NE]), ALU.mult, ALU.mult).then_inc(s_G, 1)

            def place(b, j, it):
                steps = b * (6 + TT)
                dve.wait_ge(s_rkp, b + 1)
                v.tensor_copy(RI[:, 0, :], PS[:, 7, 0:TT * NE]).then_inc(s_rk, 1)
                dve.wait_ge(s_rk, b + 1)
                v.tensor_scalar(RI[:, 1, :], RI[:, 0, :], P - 1, 9, ALU.bitwise_and, ALU.logical_shift_left).then_inc(s_ro, 1)
                v.tensor_scalar(RI[:, 2, :], RI[:, 0, :], 7, None, ALU.logical_shift_right).then_inc(s_ro, 1)
                dve.wait_ge(s_ro, steps + 2)
                v.tensor_tensor(RP[:, :], RI[:, 1, :], RI[:, 2, :], ALU.add).then_inc(s_ro, 1)
                dve.wait_ge(s_ro, steps + 3)
                v.tensor_tensor(RP[:, :], RP[:, :], EOFF[:, :, :].rearrange("p t e -> p (t e)"), ALU.add).then_inc(s_ro, 1)
                dve.wait_ge(s_ro, steps + 4)
                v.tensor_tensor(RP[:, :], RP[:, :], SEL[:, :, :].rearrange("p t e -> p (t e)"), ALU.mult).then_inc(s_ro, 1)
                wait_apart(dve, s_ro, steps + 5, s_passed)
                for t in range(TT):
                    v.max(M8[:, t, :], RP[:, t * NE:(t + 1) * NE]).then_inc(s_ro, 1)
                dve.wait_ge(s_idu, it + 1)
                v.tensor_copy(IDC[:, j, :], IDS[:, bass.ds(b * TT, TT)]).then_inc(s_idc, 1)
                dve.wait_ge(s_idc, b + 1)
                dve.wait_ge(s_ro, steps + (5 + TT))
                v.tensor_scalar(POS[:, j, :, :], M8[:, :, :], -1.0, None, ALU.add).then_inc(s_pos, 1)
                v.reduce_sum(RT[:, 0, 0, :], SEL[:, :, :].rearrange("p t e -> p e t"), AXX).then_inc(s_ro, 1)
                dve.wait_ge(s_ro, steps + (6 + TT))
                v.tensor_tensor(SELS[:, :], SELS[:, :], RT[:, 0, 0, :], ALU.add).then_inc(s_ss, 1)

            dve.wait_ge(s_val, 2)
            dve.wait_ge(s_rc0, 3)
            dve.wait_ge(s_gkh, 1)
            v.scalar_tensor_tensor(gkl[:, :, :], gk[:, :, :], E_S, gkh[:, :, :], ALU.mult, ALU.subtract).then_inc(s_gkl, 1)
            with dve.Fori(0, B // 2) as it:
                m = it * 4
                q = it * 4 + B
                keys_lo(it * 2, 0)
                for blk in range(2):
                    layer_norm(m + blk, it * 2 + blk)
                    for k in range(KC):
                        round_lo(q + blk, k, qh[:, k, blk * S:(blk + 1) * S], ql[:, k, blk * S:(blk + 1) * S], 6 + k % 2)
                values_lo(it * 2, 0)
                softmax_tile(it * 8, 0, it * 2)
                for l in range(8):
                    if l in (5, 6):
                        for k in (2 * (l - 5), 2 * (l - 5) + 1):
                            round_lo(q + 2, k, rh[:, k, :], rl[:, k, :], 7)
                    dve.wait_ge(s_pth, it * 8 + (l + 1))
                    v.scalar_tensor_tensor(pTl, PS[:, 4:6, :].rearrange("p b (c n) -> p (b c) n", n=P), P_S, pTh,
                                           ALU.mult, ALU.subtract).then_inc(s_ptl, 1)
                    if l == 0:
                        keys_lo(it * 2 + 1, 1)
                        values_lo(it * 2 + 1, 1)
                    if l < 7:
                        softmax_tile(it * 8 + (l + 1), l + 1, it * 2 + (l + 1) // 4)
                    if l == 4:
                        wait_apart(dve, s_xr, it * 8 + 4, s_passed)
                        layer_norm(m + 2, it * 2)
                    if l == 7:
                        choose(it * 2, 0)
                    readout_add(it * 8 + l, l, it * 2 + l // 4)
                place(it * 2, 0, it)
                wait_apart(dve, s_xr, it * 8 + 8, s_passed)
                wait_apart(dve, s_zst, it * 32 + 16, s_passed)
                layer_norm(m + 3, it * 2 + 1)
                for k in range(KC):
                    round_lo(q + 3, k, rh[:, k, :], rl[:, k, :], 6 + k % 2)
                choose(it * 2 + 1, 1)
                place(it * 2 + 1, 1, it)
                dve.wait_ge(s_zst, it * 32 + 32)
                dve.wait_ge(s_gst, it * 32 + 32)

            dve.wait_ge(s_zr, 3)
            dve.wait_ge(s_tp, 1)
            v.tensor_scalar(CI[0:NE, 0:1], PS[0:NE, 0, 0:1], P - 1.0, None, ALU.add).then_inc(s_tq, 1)
            dve.wait_ge(s_tq, 1)
            v.tensor_scalar(CI[0:NE, 1:2], CI[0:NE, 0:1], 7, None, ALU.logical_shift_right).then_inc(s_tq, 1)
            dve.wait_ge(s_tq, 2)
            v.tensor_copy(CH[0:NE, 0:1], CI[0:NE, 1:2]).then_inc(s_tq, 1)
            dve.wait_ge(s_tp, 2)
            v.tensor_copy(CE[0:NE, 0:1], PS[0:NE, 1, 0:1]).then_inc(s_tq, 1)
            v.tensor_copy(CH[0:NE, 1:2], PS[0:NE, 1, 0:1]).then_inc(s_tq, 1)
            dve.wait_ge(s_tq, 4)
            v.tensor_scalar(TCMP[0:NE, :], TROW[0:NE, :], CE[0:NE, 0:1], None, ALU.is_ge).then_inc(s_tq, 1)
            dve.wait_ge(s_tp, 3)
            erow, start = PS[0:1, 2, 0:TABLE], PS[0:1, 2, TABLE:2 * TABLE]
            trow = TROW[0:1, :]
            v.tensor_scalar(TAB[:, 0, :], erow, NE - 1.0, None, ALU.min).then_inc(s_tq, 1)
            v.tensor_scalar(TAB[:, 1, :], erow, NE - 1.0, 1.0, ALU.min, ALU.add).then_inc(s_tq, 1)
            v.scalar_tensor_tensor(TWK[:, 0, :], erow, float(LIST), trow, ALU.mult, ALU.add).then_inc(s_tq, 1)
            v.tensor_tensor(TWK[:, 2, :], trow, start, ALU.subtract).then_inc(s_tq, 1)
            v.tensor_scalar(TCUM[:, :], PS[0:1, 2, 2 * TABLE:2 * TABLE + NE], 1.0, None, ALU.add).then_inc(s_tq, 1)
            dve.wait_ge(s_tq, 10)
            v.tensor_scalar(TAB[:, 2, :], TAB[:, 0, :], 1, None, ALU.bitwise_and).then_inc(s_tq, 1)
            v.tensor_scalar(TAB[:, 1, :], TAB[:, 1, :], 16, None, ALU.mult).then_inc(s_tq, 1)
            v.tensor_tensor(TWK[:, 1, :], TWK[:, 0, :], start, ALU.subtract).then_inc(s_tq, 1)
            v.scalar_tensor_tensor(TWK[:, 3, :], erow, float(NE), TWK[:, 2, :], ALU.is_ge, ALU.mult).then_inc(s_tq, 1)
            dve.wait_ge(s_tq, 15)
            v.tensor_scalar(TAB[:, 2, :], TAB[:, 2, :], E16, None, ALU.mult).then_inc(s_tq, 1)
            v.tensor_scalar(TAB[:, 3, :], TWK[:, 1, :], float(NE * LIST), None, ALU.min).then_inc(s_tq, 1)
            v.tensor_tensor(TAB[:, 4, :], TWK[:, 3, :], start, ALU.add).then_inc(s_tq, 1)
            dve.wait_ge(s_tq, 18)
            dve.sem_inc(s_tab, 1)

            def tile_lo(t, p):
                dve.wait_ge(s_xh, t + 1)
                v.scalar_tensor_tensor(xl[p], PS[:, p, :].rearrange("p (k n) -> p k n", n=P), H_S, xh[p],
                                       ALU.mult, ALU.subtract).then_inc(s_xl, 1)

            def hidden_lo(t, p):
                dve.wait_ge(s_ah2, t + 1)
                v.tensor_tensor(eal[p], PS[:, 4, 0:2 * P], eah[p], ALU.subtract).then_inc(s_al2, 1)

            def hidden(t, p):
                dve.wait_ge(s_es, t + 1)
                v.scalar_tensor_tensor(ea[p][:, 0:M], PS[:, 2 + p, M:2 * M], 1.0 / (H_S * E_S), eg[p], ALU.mult, ALU.mult)
                v.scalar_tensor_tensor(ea[p][:, M:2 * P], PS[:, 2 + p, M + P:2 * M], 1.0 / (H_S * E_S), eg[p][:, P:M],
                                       ALU.mult, ALU.mult).then_inc(s_ea, 1)

            def weigh(t, u, n):
                e = dve.value_load(TAB[0:1, 0, bass.ds(t, 1)], min_val=0, max_val=NE - 1)
                dve.wait_ge(s_ed, t + 2)
                dve.wait_ge(s_add[u % V], n * 16 + 16)
                v.tensor_scalar(yt[u % V], PS[:, 5 + u % 2, :], xg[u][:, bass.ds(e + D, 1)], None, ALU.mult).then_inc(s_y, 1)

            tile_lo(0, 0)
            tile_lo(1, 1)
            hidden(0, 0)
            with dve.Fori(0, NTILE // U) as it:
                for u in range(U):
                    t = it * U + u
                    tile_lo(t + 2, u % 2)
                    hidden_lo(t, u % 2)
                    hidden(t + 1, (u + 1) % 2)
                    weigh(t, u, it * (U // V) + u // V)

        @block.tensor
        def _(pe):
            mm = nc.tensor.matmul
            pe.wait_ge(s_wio, 32)
            pe.wait_ge(s_ttr, B * KC)
            for ec in range(KC):
                for k in range(KC):
                    last = mm(PS[:, 0, ec * B:(ec + 1) * B], winT[:, k, ec * P:(ec + 1) * P], cm[:, k, :],
                              start=(k == 0), stop=(k == KC - 1))
            last.then_inc(s_st, 1)
            pe.wait_ge(s_sTb, 1)
            for b in range(B):
                wait(pe, s_summ, b - 1)
                for k in range(KC):
                    last = mm(PS[:, 1 + b % 2, :], sTb[:, k * B + b, :], woutT[:, k, :], start=(k == 0), stop=(k == KC - 1))
                last.then_inc(s_smp, 1)
            for s in range(4):
                pe.wait_ge(s_sl, s + 1)
                for g in range(4):
                    if s:
                        pe.wait_ge(s_w2f, FC * (s - 1) + 4 * (g + 1))
                    mm(PS[:, 4 + g, :], had[:, 0, :], Sh[:, 4 * g:4 * g + 4, :], start=True, stop=False)
                    mm(PS[:, 4 + g, :], had[:, 0, :], Sl[:, 4 * g:4 * g + 4, :], start=False, stop=True).then_inc(s_w2p, 1)

            def transposes(q, E, bank):
                pe.wait_ge(s_h, q * TT + TT)
                for k in range(KC):
                    wait(pe, s_tlo, E + (k - 1))
                    for t in range(TT):
                        last = nc.tensor.transpose(PS[:, bank + k % 2, t * P:(t + 1) * P], Z[:, t, k * P:(k + 1) * P], ident[:, :])
                    last.then_inc(s_tr, 1)

            def ffn_prep(b):
                wait(pe, s_x2, b * TT)
                transposes(b, b * 8, 4)
                pe.wait_ge(s_tlo, b * 8 + KC)
                for j in range(KC):
                    if j >= 2:
                        pe.wait_ge(s_tlo, b * 8 + (KC + j - 1))
                    for i in range(KC):
                        sign = bin(i & j).count("1") % 2
                        mm(PS[:, 4 + j % 2, :], had[:, sign, :], uh[:, i, :], start=(i == 0), stop=False)
                        last = mm(PS[:, 4 + j % 2, :], had[:, sign, :], ul[:, i, :], start=False, stop=(i == KC - 1))
                    last.then_inc(s_hd, 1)
                pe.wait_ge(s_tlo, b * 8 + 2 * KC)

            def three(out, lh, ll, rh, rl, first, last_group):
                mm(out, lh, rh, start=first, stop=False)
                mm(out, lh, rl, start=False, stop=False)
                return mm(out, ll, rh, start=False, stop=last_group)

            def cols(t, k, at):
                if isinstance(at, int):
                    return t[:, k, at:at + P]
                return t[:, k, bass.ds(at, P)]

            def up_gate(F, f, p, first):
                if not first:
                    pe.wait_ge(s_a, F - 1)
                for half, bank, done in ((1, 2 * p, s_g), (0, 2 * p + 1, s_u)):
                    for k in range(KC):
                        at = f * P + half * INTER
                        last = three(PS[:, bank, :], cols(wh, k, at), cols(wl, k, at), hh[:, k, :], hl[:, k, :], k == 0, k == KC - 1)
                    last.then_inc(done, 1)

            def down(F, f, p, first, end):
                pe.wait_ge(s_al, F + 1)
                pe.wait_ge(s_ah, F + 1)
                for t in range(TT):
                    a, b_ = ah[p][:, t * P:(t + 1) * P], al[p][:, t * P:(t + 1) * P]
                    fs = slice(f, f + 1) if isinstance(f, int) else bass.ds(f, 1)
                    rh, rl = w2h[:, fs, :].rearrange("p a d -> p (a d)"), w2l[:, fs, :].rearrange("p a d -> p (a d)")
                    last = three(PS[:, 4 + t, :], a, b_, rh, rl, first, end)
                last.then_inc(s_dn, 1)

            def ffn_batch(b):
                up_gate(b * FC, 0, 0, True)
                up_gate(b * FC + 1, 1, 1, True)
                down(b * FC, 0, 0, True, False)
                with pe.Fori(0, FC // 2 - 1) as i:
                    up_gate(b * FC + i * 2 + 2, i * 2 + 2, 0, False)
                    down(b * FC + i * 2 + 1, i * 2 + 1, 1, False, False)
                    up_gate(b * FC + i * 2 + 3, i * 2 + 3, 1, False)
                    down(b * FC + i * 2 + 2, i * 2 + 2, 0, False, False)
                down(b * FC + FC - 1, FC - 1, 1, False, True)

            pe.wait_ge(s_w2l, 4)
            ffn_prep(0)
            pe.wait_ge(s_wul, 8)
            with pe.Fori(0, B - 1) as b:
                ffn_batch(b)
                ffn_prep(b + 1)
            ffn_batch(B - 1)

            def scores(t, l, b):
                p = l % 2
                if l >= 2:
                    pe.wait_ge(s_s, t - 1)
                if l % 4 == 0:
                    pe.wait_ge(s_ctl, b + 1)
                par = l // 4
                for n in range(2):
                    for k in range(KC):
                        last = three(PS[:, 2 * p + n, :], qh[:, k, l * P:(l + 1) * P], ql[:, k, l * P:(l + 1) * P],
                                     cTh[par][:, k, n * 512:(n + 1) * 512], cTl[par][:, k, n * 512:(n + 1) * 512],
                                     k == 0, k == KC - 1)
                last.then_inc(s_sc, 1)

            def router_chunk(q, k, bank, copied):
                pe.wait_ge(s_tlo, copied)
                for t in range(TT):
                    last = nc.tensor.transpose(PS[:, bank, t * P:(t + 1) * P], Z[:, t, k * P:(k + 1) * P], ident[:, :])
                last.then_inc(s_tr, 1)

            def logits(q):
                pe.wait_ge(s_tlo, q * 4 + (4 * B + KC))
                for t in range(TT):
                    for k in range(KC):
                        ts = slice(t * P, (t + 1) * P)
                        last = three(PS[:, 7, t * NE:(t + 1) * NE], rh[:, k, ts], rl[:, k, ts], gkh[:, k, :], gkl[:, k, :],
                                     k == 0, k == KC - 1)
                last.then_inc(s_lg, 1)

            def rank(b):
                pe.wait_ge(s_sel, b + 1)
                pe.wait_ge(s_ss, b + 1)
                for t in range(TT):
                    out = PS[:, 7, t * NE:(t + 1) * NE]
                    mm(out, tri[:, 0, :], SEL[:, t, :], start=True, stop=False)
                    for before in range(t):
                        mm(out, tri[:, 2, :], SEL[:, before, :], start=False, stop=False)
                    last = mm(out, tri[:, 2, :], SELS[:, :], start=False, stop=True)
                last.then_inc(s_rkp, 1)

            pe.wait_ge(s_gkl, 1)
            with pe.Fori(0, B // 2) as it:
                q = it * 4 + B
                wait(pe, s_x2, NT)
                for blk in range(2):
                    transposes(q + blk, q * 4 + (4 * B + 4 * blk), 6)
                pe.wait_ge(s_tlo, q * 4 + (4 * B + 8))
                scores(it * 8, 0, it * 2)
                for l in range(8):
                    if l < 7:
                        scores(it * 8 + (l + 1), l + 1, it * 2 + (l + 1) // 4)
                    if l in (5, 6):
                        k = 2 * (l - 5) + 1
                        router_chunk(q + 2, k, 7, q * 4 + (4 * B + 8 + k))
                    pe.wait_ge(s_p, it * 8 + (l + 1))
                    if l:
                        pe.wait_ge(s_ptl, it * 8 + l)
                    for c in range(KEYC):
                        last = nc.tensor.transpose(PS[:, 4 + c // 4, (c % 4) * P:(c % 4 + 1) * P], pr[:, c * P:(c + 1) * P], ident[:, :])
                    last.then_inc(s_pt, 1)
                    pe.wait_ge(s_ptl, it * 8 + (l + 1))
                    if l:
                        pe.wait_ge(s_xr, it * 8 + l)
                    if l % 4 == 0:
                        pe.wait_ge(s_cnl, it * 2 + (l // 4 + 1))
                    for c in range(KEYC):
                        last = three(PS[:, 6, :], pTh[:, c, :], pTl[:, c, :], cNh[l // 4][:, c, :], cNl[l // 4][:, c, :],
                                     c == 0, c == KEYC - 1)
                    last.then_inc(s_rd, 1)
                    if l in (4, 5):
                        k = 2 * (l - 4)
                        if k == 0:
                            pe.wait_ge(s_h, q * TT + 3 * TT)
                        router_chunk(q + 2, k, 7, q * 4 + (4 * B + 8 + k))
                    if l == 6:
                        logits(q + 2)
                rank(it * 2)
                pe.wait_ge(s_xr, it * 8 + 8)
                pe.wait_ge(s_rk, it * 2 + 1)
                transposes(q + 3, q * 4 + (4 * B + 12), 6)
                logits(q + 3)
                rank(it * 2 + 1)
                pe.wait_ge(s_rk, it * 2 + 2)

            pe.wait_ge(s_ss, B + 1)
            mm(PS[0:NE, 0, 0:1], SELS[:, :], tri[:, 2, 0:1], start=True, stop=True).then_inc(s_tp, 1)
            pe.wait_ge(s_tq, 3)
            mm(PS[0:NE, 1, 0:1], tri[0:NE, 1, 0:NE], CH[0:NE, 0:1], start=True, stop=True).then_inc(s_tp, 1)
            pe.wait_ge(s_tq, 6)
            mm(PS[0:1, 2, 0:TABLE], tri[0:NE, 2, 0:1], TCMP[0:NE, :], start=True, stop=True)
            mm(PS[0:1, 2, TABLE:2 * TABLE], CH[0:NE, 0:1], TCMP[0:NE, :], start=True, stop=True)
            mm(PS[0:1, 2, 2 * TABLE:2 * TABLE + NE], CH[0:NE, 1:2], tri[0:NE, 3, 0:NE], start=True, stop=True)\
                .then_inc(s_tp, 1)
            pe.wait_ge(s_tab, 1)

            def tile_transpose(t, u, n):
                pe.wait_ge(s_xg[u], n * 16 + 16)
                for k in range(KC):
                    last = nc.tensor.transpose(PS[:, u % 2, k * P:(k + 1) * P], xg[u][:, k * P:(k + 1) * P], ident[:, :])
                last.then_inc(s_xt, 1)

            def weights_at(t):
                return pe.value_load(TAB[0:1, 2, bass.ds(t, 1)], min_val=0, max_val=E16)

            def landing(t):
                return pe.value_load(TAB[0:1, 1, bass.ds(t, 1)], min_val=16, max_val=16 * NE)

            def tile_up(t, p, at):
                for k in range(KC):
                    hi = we[:, bass.ds(at + k * GU, GU)]
                    lo = we[:, bass.ds(at + (EW + k * GU), GU)]
                    last = three(PS[:, 2 + p, 0:GU], xh[p][:, k, :], xl[p][:, k, :], hi, lo, k == 0, k == KC - 1)
                last.then_inc(s_ug, 1)

            def hidden_transpose(p):
                nc.tensor.transpose(PS[:, 4, 0:P], ea[p][:, 0:P], ident[:, :])
                nc.tensor.transpose(PS[:, 4, P:2 * P], ea[p][:, P:2 * P], ident[:, :]).then_inc(s_at, 1)

            def tile_down(t, p, at):
                pe.wait_ge(s_al2, t + 1)
                bank = PS[:, 5 + p, :]
                w0h, w1 = KC * GU, KC * GU + D
                hi, lo = we[:, bass.ds(at + w0h, D)], we[:, bass.ds(at + (EW + w0h), D)]
                stack = we[:, bass.ds(at + w1, D)]
                three(bank, eah[p][:, 0:P], eal[p][:, 0:P], hi, lo, True, False)
                mm(bank, eah[p][:, P:2 * P], stack, start=False, stop=False)
                mm(bank, eal[p][:, P:2 * P], stack, start=False, stop=True).then_inc(s_ed, 1)

            tile_transpose(0, 0, 0)
            tile_transpose(1, 1, 0)
            pe.wait_ge(s_xl, 1)
            landed, at = landing(0), weights_at(0)
            pe.wait_ge(s_wl, landed)
            tile_up(0, 0, at)
            with pe.Fori(0, NTILE // U) as it:
                at = weights_at(it * U)
                for u in range(U):
                    t = it * U + u
                    tile_transpose(t + 2, (u + 2) % U, it + (u + 2) // U)
                    landed, following = landing(t + 1), weights_at(t + 1)
                    pe.wait_ge(s_wl, landed)
                    pe.wait_ge(s_ea, t + 1)
                    hidden_transpose(u % 2)
                    tile_up(t + 1, (u + 1) % 2, following)
                    tile_down(t, u % 2, at)
                    at = following


def kernel(x, ctx_2048, mask_BxS2_bk0, L0_xattn_decay, L0_xattn_W_in, L0_xattn_b_in, L0_xattn_W_out,
           L0_xattn_b_out, L0_xattn_gamma, L0_xattn_beta, L0_ffn_SU_ug, L0_ffn_SU_dp, L0_ffn_Wscale_ug,
           L0_ffn_Wscale_dp, L0_ffn_W_up, L0_ffn_W_gate, L0_ffn_W_down, L1_ffn_gate_kernel, L1_ffn_gate_proj,
           L1_ffn_up_proj, L1_ffn_down_proj):
    import concourse.bacc as bacc
    from concourse.bass_utils import run_bass_kernel_spmd

    asc = np.ascontiguousarray

    def column(v):
        return np.reshape(np.asarray(v), (-1, P)).T

    ws = np.asarray(L0_ffn_Wscale_ug)
    cols = asc(np.concatenate([column(L0_xattn_b_in), column(L0_ffn_SU_ug), column(L0_ffn_SU_dp),
                               column(ws[:INTER]), column(ws[INTER:]),
                               np.broadcast_to(np.reshape(np.asarray(L0_xattn_decay), (1, 1)), (P, 1))], axis=1))
    rows = asc(np.broadcast_to(np.stack([np.asarray(L0_xattn_gamma), np.asarray(L0_xattn_beta),
                                         np.asarray(L0_xattn_b_out), np.asarray(L0_ffn_Wscale_dp)])[None], (P, 4, D)))
    gate, up, down = (np.asarray(a) for a in (L1_ffn_gate_proj, L1_ffn_up_proj, L1_ffn_down_proj))
    gu = np.concatenate([gate, up], axis=2)
    gu = np.reshape(np.transpose(np.reshape(gu, (NE, KC, P, 2 * M)), (0, 2, 1, 3)), (NE, P, KC * 2 * M))
    experts = asc(np.concatenate([gu, down[:, :P], np.concatenate([down[:, P:], down[:, P:]], axis=1)], axis=2))
    h = np.array([[1.0]])
    while h.shape[0] < P:
        h = np.block([[h, h], [h, -h]])
    before = np.triu(np.ones((P, P)))
    xin = np.asarray(x)
    arrays = {
        "x": asc(np.reshape(xin, (B * S, D))),
        "ctxT": asc(np.transpose(np.asarray(ctx_2048), (0, 2, 1))),
        "ctx": asc(np.asarray(ctx_2048)),
        "mask": asc(np.broadcast_to(np.reshape(np.asarray(mask_BxS2_bk0), (1, B * T2)), (P, B * T2))),
        "winT": asc(np.asarray(L0_xattn_W_in).T),
        "woutT": asc(np.asarray(L0_xattn_W_out).T),
        "cols": cols,
        "rows": rows,
        "wupT": asc(np.asarray(L0_ffn_W_up).T),
        "wgateT": asc(np.asarray(L0_ffn_W_gate).T),
        "wdT": asc(np.asarray(L0_ffn_W_down).T),
        "gk": asc(np.asarray(L1_ffn_gate_kernel)),
        "experts": experts,
        "ident": np.eye(P, dtype=np.float32),
        "had": asc(np.stack([h, -h], axis=1).astype(np.float16)),
        "tri": asc(np.stack([before - np.eye(P), before, np.ones((P, P)), np.eye(P)], axis=1).astype(np.float16)),
    }
    nc = bacc.Bacc("TRN2", target_bir_lowering=False, num_devices=1)
    args = [nc.dram_tensor(f"in_{n}", a.shape, mybir.dt.from_np(a.dtype), kind="ExternalInput").ap() for n, a in arrays.items()]
    split = nc.dram_tensor("split_experts", (NE, P, E16), F16, kind="Internal").ap()
    lists = nc.dram_tensor("token_lists", (P * NE * LIST, 1), I32, kind="Internal").ap()
    table = nc.dram_tensor("token_table", (NTOK + P, TW), F32, kind="Internal").ap()
    out = nc.dram_tensor("out", (NTOK + P, D), F32, kind="ExternalOutput").ap()
    build(nc, *args, split, lists, table, out)
    r = run_bass_kernel_spmd(nc, [{f"in_{n}": a for n, a in arrays.items()}], core_ids=[0])
    return np.reshape(r.results[0]["out"][:NTOK], xin.shape)
```

```python
from contextlib import ExitStack

import numpy as np

import concourse.bass as bass
from concourse import mybir

F32 = mybir.dt.float32
F16 = mybir.dt.float16
U8 = mybir.dt.uint8
I32 = mybir.dt.int32
ALU = mybir.AluOpType
ACT = mybir.ActivationFunctionType
AXX = mybir.AxisListType.X

P = 128
B, S, D, T2 = 4, 512, 512, 1024
KC = D // P
TT = S // P
NT = B * TT
INTER = 2048
FC = INTER // P
NE, M, TOPK = 32, 192, 8
ML = M - P
GU = 2 * M
EW = KC * GU + 2 * D
EH = EW // 2
EL = KC * GU + D
E16 = EW + EL
NTOK = B * S
NTILE = NTOK * TOPK // P + NE
TABLE = NTILE + 8
LIST = NTOK // P
TW = D + NE
U = 8
PU = 2 * U
AHEAD = U - 3
V = 4
NEWTON = 13
MAGIC = 0x5F3759DF
KEYC = T2 // P
EPS = 1e-5
W_S = 256.0
U_S = 32.0
N_S = 32.0
H_S = 64.0
C_S = 64.0
P_S = 1024.0
E_S = 64.0
C_BIN, C_SUG, C_SDP, C_WU, C_WG, C_DEC = 0, KC, 2 * KC, 2 * KC + FC, 2 * KC + 2 * FC, 2 * KC + 3 * FC
NCOL = C_DEC + 1


Q_ROUND = {0: 4, 1: 5, 2: 6, 3: 8}
R_ROUND = {0: 7, 1: 9, 2: 10, 3: 11}


CHOOSE = (None, 3, 3, 2)


def half_keys(n):
    return slice(n * T2 // 2, (n + 1) * T2 // 2)


def copied_before(q):
    return KC * (q + min(q, B))


def beside(b, slot, place):
    at = 3 * slot + place
    chunks = []
    if b == 0:
        chunks += [(2 + k, "q", 1, k) for k in range(KC)]
    elif b < B - 1:
        chunks += [(k, "q", b + 1, k) for k in range(KC)]
        chunks += [(5 + k, "r", b - 1, k) for k in range(KC)]
        chunks += [(9, "logits", b - 1, 0), (10, "rank", b - 1, 0)]
    else:
        chunks += [(2 + k, "r", b - 1, k) for k in range(KC)]
        chunks += [(6, "logits", b - 1, 0), (7, "rank", b - 1, 0)]
    for when, *what in chunks:
        if when == at:
            return what
    return None, None, None


def wait(eng, sem, value):
    if isinstance(value, int) and value <= 0:
        return
    eng.wait_ge(sem, value)


def wait_apart(eng, sem, value, passed):
    eng.wait_ge(sem, value)
    eng.sem_inc(passed, 1)


def build(nc, a_x, a_ctxT, a_ctx, a_mask, a_winT, a_woutT, a_cols, a_rows, a_wug, a_wdT,
          a_gk, a_exp, a_ident, a_had, a_tri, d_exp, d_list, d_tok, a_out):
    ctx = ExitStack()
    with ctx:
        def sb(name, shape, dt):
            return ctx.enter_context(nc.sbuf_tensor(name, shape, dt))

        def sem(name):
            return ctx.enter_context(nc.semaphore(name))

        X = sb("X", [P, NT * D], F32)
        HT = sb("HT", [P, 8192], F32)
        Z = sb("Z", [P, TT, D], F32)
        SUMM = sb("SUMM", [P, B, D], F32)
        ROWS = sb("ROWS", [P, 4, D], F32)
        COLS = sb("COLS", [P, NCOL], F32)
        BIG = sb("BIG", [P, 24576], F32)
        EX = sb("EX", [P, 3072], F32)
        ident = sb("ident", [P, P], F32)
        had = sb("had", [P, 2, P], F16)
        st = sb("st", [P, TT, 6], F32)
        mv = sb("mv", [P, TT, 2], F32)
        sm = sb("sm", [P, 16], F32)
        SG = sb("SG", [P, 2, FC], F32)
        cm = sb("cm", [P, KC, B], F32)
        sT = sb("sT", [P, KC, B], F32)
        valid = sb("valid", [P, B], F32)
        attn = sb("attn", [P, 2, 6], F32)
        nw = sb("nw", [P, 4, TT], F32)
        gk = sb("gk", [P, KC, NE], F32)
        gkh = sb("gkh", [P, KC, NE], F16)
        gkl = sb("gkl", [P, KC, NE], F16)
        tri = sb("tri", [P, 4, P], F16)
        RT = sb("RT", [P, 4, TT, NE], F32)
        G = sb("G", [P, 2, TT, NE], F32)
        SEL = sb("SEL", [P, TT, NE], F16)
        SELS = sb("SELS", [P, NE], F16)
        M8 = sb("M8", [P, TT, 8], F32)
        RS = sb("RS", [P, 2, TT], F32)
        RI = sb("RI", [P, 3, TT * NE], I32)
        RP = sb("RP", [P, TT * NE], F32)
        EOFF = sb("EOFF", [P, TT, NE], F32)
        POS = sb("POS", [P, 2, TT, 8], I32)
        IDS = sb("IDS", [P, NT], I32)
        IDC = sb("IDC", [P, 2, TT], I32)
        TROW = sb("TROW", [P, TABLE], F32)
        first = sb("first", [1, 16], F32)
        PS = ctx.enter_context(nc.psum_tensor("PS", [P, 8, 512], F32))

        def f16(t, start, shape):
            n = int(np.prod(shape)) // 2
            v = t[:, start:start + n].bitcast(F16)
            if len(shape) == 2:
                return v.rearrange("p (a b) -> p a b", a=shape[0])
            return v

        def f32(t, start, shape):
            v = t[:, start:start + int(np.prod(shape))]
            if len(shape) == 2:
                return v.rearrange("p (a b) -> p a b", a=shape[0])
            return v

        cxT = [f32(BIG, i * 4096, (KC, T2)) for i in range(B)]
        winT = f32(BIG, 16384, (KC, D))
        woutT = f32(BIG, 18432, (KC, D))
        vrow = BIG[:, 20480:20480 + T2]
        ones = BIG[:, 21504:21504 + T2]
        junk = BIG[:, 22528:22528 + T2]
        ssum = EX[0:B, 2560:2560 + D]
        WA = [f32(X, TT * D, (FC, P)), f32(X, 2 * TT * D, (FC, P)), f32(HT, 2048, (FC, P))]
        WB = f32(X, 3 * TT * D, (FC, P))
        Sh = f16(EX, D, (FC, P))
        Sl = f16(EX, D + 1024, (FC, P))
        wug = f16(BIG, 0, (FC // 2, 2 * KC * 512))
        wst = [f32(HT, 4096, (KC, 512)), f32(HT, 6144, (KC, 512))]
        wst += [f32(BIG, 8192 + i * 2048, (KC, 512)) for i in range(4)] + wst
        w2h = f16(BIG, 16384, (FC, D))
        w2l = f16(BIG, 20480, (FC, D))
        hid = f16(HT, 0, (2 * 2 * KC * S,))

        def had_hi(b, k):
            return hid[:, bass.ds((b % 2) * (2 * KC * S) + k * S, S)]

        def had_lo(b, k):
            return hid[:, bass.ds((b % 2) * (2 * KC * S) + (KC + k) * S, S)]

        Z16 = Z[:, :, :].bitcast(F16)
        uh = [Z16[:, :, k * 2 * P:k * 2 * P + P] for k in range(KC)]
        ul = [Z16[:, :, k * 2 * P + P:(k + 1) * 2 * P] for k in range(KC)]
        gs = [EX[:, i * 512:(i + 1) * 512] for i in range(2)]
        af = [EX[:, 1024 + i * 512:1536 + i * 512] for i in range(2)]
        ah = [f16(EX, 2048 + i * 256, (512,)) for i in range(2)]
        al = [f16(EX, 2560 + i * 256, (512,)) for i in range(2)]
        cTst = f32(HT, 4096, (KC, T2))
        cTh = [f16(BIG, i * 8192, (KC, T2)) for i in range(2)]
        cTl = [f16(BIG, i * 8192 + 2048, (KC, T2)) for i in range(2)]
        cNh = [f16(BIG, i * 8192 + 4096, (KEYC, D)) for i in range(2)]
        cNl = [f16(BIG, i * 8192 + 6144, (KEYC, D)) for i in range(2)]
        cNst = f32(BIG, 16384, (KEYC, D))
        bias = BIG[:, 20480:24576]
        cT0 = f32(BIG, 8192, (KC, T2))
        mask = BIG[:, 12288:13312].bitcast(U8)
        sc = EX[:, 0:1024]
        pr = EX[:, 1024:2048]
        pTh = f16(EX, 2048, (KEYC, P))
        pTl = f16(EX, 2560, (KEYC, P))
        spare_rows = BIG[:, 23552:23552 + NE * LIST].bitcast(I32)
        est = [HT[:, 4096 + i * EH:4096 + (i + 1) * EH] for i in range(2)]
        eoh = f16(HT, 4096 + 2 * EH, (EH,))
        eol = f16(HT, 4096 + 2 * EH + EH // 2, (EH,))
        rh = f16(SUMM[:, :, :].rearrange("p b d -> p (b d)"), 0, (KC, S))
        rl = f16(SUMM[:, :, :].rearrange("p b d -> p (b d)"), KC * S // 2, (KC, S))
        we = f16(BIG, 0, (2 * E16,))
        o = E16
        xg = [BIG[:, o + i * TW:o + (i + 1) * TW] for i in range(U)]
        o += U * TW
        yt = [BIG[:, o + i * D:o + (i + 1) * D] for i in range(V)]
        o += V * D
        xh = [f16(BIG, o + i * D // 2, (KC, P)) for i in range(2)]
        xl = [f16(BIG, o + D + i * D // 2, (KC, P)) for i in range(2)]
        o += 2 * D
        eg = [BIG[:, o + i * M:o + (i + 1) * M] for i in range(2)]
        o += 2 * M
        ea = [BIG[:, o + i * 2 * P:o + (i + 1) * 2 * P] for i in range(2)]
        o += 4 * P
        eah = [f16(BIG, o + i * P, (2 * P,)) for i in range(2)]
        eal = [f16(BIG, o + (2 + i) * P, (2 * P,)) for i in range(2)]
        zrow = BIG[:, o + 4 * P:o + 4 * P + TW]
        o = [0]

        def ex(n, dt=F32, p=P):
            v = EX[0:p, o[0]:o[0] + n]
            o[0] += n
            return v if dt is F32 else v.bitcast(dt)

        IDX = ex(NE * LIST + 1, I32)
        TCMP = ex(TABLE // 2, F16)
        CE = ex(1)
        CI = ex(2, I32)
        CH = ex(1, F16)
        TWK = ex(4 * TABLE, p=1).rearrange("p (a t) -> p a t", a=4)
        TAB = ex(5 * TABLE, I32, p=1).rearrange("p (a t) -> p a t", a=5)
        TCUM = ex(NE, I32, p=1)
        GIX = ex(U, I32)

        def xt(tile):
            return X[:, bass.ds(tile * D, D)]

        s_const, s_rows, s_wio, s_x, s_gk, s_mask, s_out = (sem(n) for n in (
            "const_landed", "rows_landed", "mixer_weights_landed", "x_landed", "router_landed", "mask_landed", "out_landed"))
        s_cx = [sem(f"mixer_context_landed{i}") for i in range(B)]
        s_ws = [sem(f"ffn_weights_landed{i}") for i in range(FC // 2)]
        s_wd = [sem(f"down_slice_landed{i}") for i in range(3)]
        s_cT, s_cN = sem("keys_landed"), sem("values_landed")
        s_cT0 = [sem(f"first_keys_landed{i}") for i in range(2)]
        s_est = [sem(f"expert_half_landed{i}") for i in range(2)]
        s_eh, s_el, s_el2, s_eo = sem("expert_half_hi"), sem("expert_half_lo"), sem("expert_rows_lo"), sem("expert_half_stored")
        s_dec, s_pre = sem("decay_gate_ready"), sem("mixer_step")
        s_ttr, s_st, s_sT, s_sb, s_sTb, s_smp, s_summ = (sem(n) for n in (
            "context_summed", "states_product", "states_ready", "summaries_product", "summaries_copied", "summary_product", "summary_ready"))
        s_fly, s_sh, s_sl, s_w2p, s_w2h, s_w2l = (sem(n) for n in (
            "butterfly_done", "down_split_hi", "down_split_lo", "down_product", "down_hi", "down_lo"))
        s_wuh, s_wul = sem("ffn_weights_hi"), sem("ffn_weights_lo")
        s_bn, s_mv = sem("ln_stats"), sem("ln_moments")
        s_z, s_h = sem("mixer_ln_step"), sem("normalised")
        s_tr, s_thi, s_tlo, s_hd = (sem(n) for n in (
            "transposed", "transposed_hi", "transposed_lo", "hadamard_done"))
        s_g, s_u, s_silu, s_a, s_ah, s_al, s_dn, s_x2 = (sem(n) for n in (
            "gate_product", "up_product", "silu_ready", "hidden_ready", "hidden_hi", "hidden_lo",
            "down_used_hidden", "ffn_added"))
        s_y2 = sem("ffn_scaled")
        s_passed, s_ppassed, s_spassed = sem("wait_passed"), sem("pool_wait_passed"), sem("sync_wait_passed")
        s_bias, s_val = sem("bias_ready"), sem("valid_ready")
        s_cth, s_ctl, s_cnh, s_cnl = (sem(n) for n in ("keys_hi", "keys_lo", "values_hi", "values_lo"))
        s_sc, s_s, s_mx, s_nm, s_p, s_pt, s_pth, s_ptl, s_rc, s_rv, s_rd, s_xr = (sem(n) for n in (
            "scores_product", "scores_ready", "max_ready", "negmax_ready", "probs_ready", "probs_transposed",
            "probs_hi", "probs_lo", "sum_inverted", "sum_scaled", "readout_product", "readout_added"))
        s_nw = sem("inverse_root_step")
        s_gkh, s_gkl, s_rc0 = sem("router_hi"), sem("router_lo"), sem("router_consts")
        s_lg, s_L, s_m8, s_mr, s_sel, s_dif, s_rex, s_gx, s_gs, s_grc, s_G = (sem(n) for n in (
            "logits_product", "logits_ready", "top8_ready", "top8_replaced", "selection_ready", "logits_minus_max",
            "router_exp", "selected_exp", "selected_sum", "selected_inverse", "routing_weights_ready"))
        s_rkp, s_rk, s_ro, s_pos, s_idc, s_ss = (sem(n) for n in (
            "rank_product", "rank_copied", "place_step", "places_ready", "batch_ids_ready", "selected_so_far"))
        s_ids = [sem(f"ids_listed{i}") for i in range(2)]
        s_idu = sem("places_used")
        s_lst, s_zst, s_gst, s_res, s_zr, s_spare, s_idx = (sem(n) for n in (
            "lists_cleared", "tokens_stored", "routing_weights_stored", "residual_stored", "zero_row_ready",
            "spare_rows_cleared", "lists_landed"))
        s_tp, s_tq, s_tab = sem("table_product"), sem("table_step"), sem("tables_ready")
        s_wl = sem("expert_landed")
        s_gi = sem("tile_rows_ready")
        s_xg = [sem(f"tile_gathered{i}") for i in range(U)]
        s_add = [sem(f"tile_added{i}") for i in range(V)]
        s_xt, s_xh, s_xl, s_ug, s_es, s_ea, s_at, s_ah2, s_al2, s_ed, s_y = (sem(n) for n in (
            "tile_transposed", "tile_hi", "tile_lo", "tile_gate_up", "tile_silu", "tile_hidden", "hidden_transposed",
            "hidden_t_hi", "hidden_t_lo", "tile_down", "tile_weighted"))

        block = ctx.enter_context(nc.Block())

        @block.sync
        def _(sp):
            sp.dma_start(COLS[:, :], a_cols).then_inc(s_const, 16)
            for b in range(B):
                sp.dma_start(cxT[b], a_ctxT[b].rearrange("(k p) t -> p k t", p=P)).then_inc(s_cx[b], 16)
            sp.dma_start(winT, a_winT.rearrange("(k p) e -> p k e", p=P)).then_inc(s_wio, 16)
            sp.dma_start(woutT, a_woutT.rearrange("(k p) e -> p k e", p=P)).then_inc(s_wio, 16)

            def load_x(first, last):
                sp.dma_start(X[:, first * D:last * D].rearrange("p (t d) -> p t d", d=D),
                             a_x[first * P:last * P, :].rearrange("(t p) d -> p t d", p=P)).then_inc(s_x, 16)

            load_x(0, TT)
            sp.dma_start(ROWS[:, :, :], a_rows).then_inc(s_rows, 16)
            sp.dma_start(ident[:, :], a_ident).then_inc(s_rows, 16)
            sp.dma_start(had[:, :, :], a_had).then_inc(s_rows, 16)
            sp.dma_start(tri[:, :, :], a_tri).then_inc(s_rows, 16)
            sp.wait_ge(s_rc0, 1)
            sp.dma_start(d_list.rearrange("(p c) a -> p (c a)", p=P), spare_rows).then_inc(s_lst, 16)
            sp.dma_start(gk[:, :, :], a_gk.rearrange("(k p) e -> p k e", p=P)).then_inc(s_gk, 16)
            sp.wait_ge(s_wd[2], 16)
            for c in range(FC // 2):
                if c == 2:
                    sp.wait_ge(s_ttr, B * KC)
                if c >= 6:
                    sp.wait_ge(s_wul, c - 5)
                sp.dma_start(wst[c], a_wug[c].rearrange("p (k f) -> p k f", k=KC)).then_inc(s_ws[c], 16)
            sp.wait_ge(s_fly, 16)
            sp.wait_ge(s_sl, 2)
            load_x(2 * TT, NT)
            def load_half(e, h):
                src = a_exp[bass.ds(e, 1), :, h * EH:(h + 1) * EH].rearrange("a p w -> p (a w)")
                sp.dma_start(est[h], src).then_inc(s_est[h], 16)

            def store_half(e, h):
                dst = d_exp[bass.ds(e, 1), :, :].rearrange("a p w -> p (a w)")
                nl = (EH, EL - EH)[h]
                sp.dma_start(dst[:, h * EH:(h + 1) * EH], eoh).then_inc(s_eo, 16)
                sp.dma_start(dst[:, EW + h * EH:EW + h * EH + nl], eol[:, 0:nl]).then_inc(s_eo, 16)

            sp.wait_ge(s_w2l, 4)
            sp.wait_ge(s_wul, 8)
            for h in range(2):
                load_half(0, h)
            load_x(TT, 2 * TT)
            with sp.Fori(0, NE - 1) as e:
                for h in range(2):
                    sp.wait_ge(s_el, e * 2 + (h + 1))
                    store_half(e, h)
                    load_half(e + 1, h)
            sp.wait_ge(s_el, 2 * NE - 1)
            store_half(NE - 1, 0)
            sp.wait_ge(s_u, B * FC)
            for n in range(2):
                sp.dma_start(cT0[:, :, half_keys(n)], a_ctxT[0, :, half_keys(n)].rearrange("(k p) t -> p k t", p=P))\
                    .then_inc(s_cT0[n], 16)
            sp.dma_start(mask, a_mask).then_inc(s_mask, 16)
            sp.wait_ge(s_el, 2 * NE)
            store_half(NE - 1, 1)

            def load_keys(b):
                sp.wait_ge(s_ctl, b + 1)
                sp.dma_start(cTst, a_ctxT[b].rearrange("(k p) t -> p k t", p=P)).then_inc(s_cT, 16)

            def load_values(b):
                if b:
                    sp.wait_ge(s_cnl, b)
                sp.dma_start(cNst, a_ctx[b].rearrange("(c p) d -> p c d", p=P)).then_inc(s_cN, 16)

            def store_routed(b):
                rows = d_tok[b * S:(b + 1) * S, :].rearrange("(t p) w -> p t w", p=P)
                sp.wait_ge(s_h, TT * (R_ROUND[b] + 1))
                sp.dma_start(rows[:, :, 0:D], Z[:, :, :]).then_inc(s_zst, 16)
                sp.wait_ge(s_G, b + 1)
                sp.dma_start(rows[:, :, D:TW], G[:, b % 2, :, :]).then_inc(s_gst, 16)

            sp.wait_ge(s_dn, B * FC)
            load_values(0)
            sp.wait_ge(s_eo, 1 + 64 * NE)
            load_keys(1)
            load_values(1)
            load_keys(2)
            load_values(2)
            store_routed(0)
            load_keys(3)
            load_values(3)
            store_routed(1)
            store_routed(2)
            for b in range(B):
                sp.wait_ge(s_xr, TT * (b + 1))
                sp.dma_start(a_out[b * S:(b + 1) * S, :].rearrange("(t p) d -> p t d", p=P),
                             X[:, b * TT * D:(b + 1) * TT * D].rearrange("p (t d) -> p t d", d=D)).then_inc(s_res, 16)
            store_routed(3)
            def load_expert(e, h):
                src = d_exp[bass.ds(e, 1), :, :].rearrange("a p w -> p (a w)")
                sp.dma_start(we[:, h * E16:(h + 1) * E16], src).then_inc(s_wl, 16)

            load_expert(0, 0)
            sp.wait_ge(s_wl, 16)
            load_expert(1, 1)
            sp.wait_ge(s_zr, 1)
            sp.dma_start(d_tok[NTOK:NTOK + P, :], zrow).then_inc(s_spare, 16)
            sp.dma_start(a_out[NTOK:NTOK + P, :], zrow[:, 0:D]).then_inc(s_spare, 16)
            for i in range(2):
                sp.wait_ge(s_ids[i], B // 2 * 16 * TT * TOPK)
            sp.dma_start(IDX[:, 0:NE * LIST], d_list.rearrange("(p c) a -> p (c a)", p=P)).then_inc(s_idx, 16)
            sp.wait_ge(s_tab, 1)
            with sp.Fori(1, NE // 2) as i:
                for h in range(2):
                    wait_apart(sp, s_wl, i * 32 + 16 * h, s_spassed)
                    done = sp.value_load(TCUM[0:1, bass.ds(i * 2 + (h - 2), 1)], min_val=1, max_val=NTILE + 1)
                    sp.wait_ge(s_ed, done)
                    load_expert(i * 2 + h, h)
            for w in range(V):
                sp.wait_ge(s_add[w], 16 + 16 * (NTILE // V))

        @block.gpsimd
        def _(pool):
            pool.iota(spare_rows, pattern=[[0, NE * LIST]], base=NTOK, channel_multiplier=1).then_inc(s_rc0, 1)
            pool.iota(IDS[:, :], pattern=[[P, NT]], base=0, channel_multiplier=1).then_inc(s_rc0, 1)
            pool.iota(EOFF[:, :, :], pattern=[[0, TT], [LIST, NE]], base=1, channel_multiplier=0,
                      allow_small_or_imprecise_dtypes=True).then_inc(s_rc0, 1)
            pool.memset(SELS[:, :], 0.0).then_inc(s_ss, 1)
            pool.iota(TROW[:, :], pattern=[[1, TABLE]], base=0, channel_multiplier=0,
                      allow_small_or_imprecise_dtypes=True).then_inc(s_rc0, 1)
            for w in range(V):
                pool.dma_start(first[:, 4 * w:4 * w + 4], a_x[0:1, 4 * w:4 * w + 4]).then_inc(s_add[w], 16)
            pool.sem_inc(s_idu, 1)
            pool.sem_inc(s_eo, 1)
            pool.sem_inc(s_ed, 1)
            def load_slice(s):
                pool.dma_start(WA[s % 3], a_wdT[:, s * P:(s + 1) * P].rearrange("(c p) d -> p c d", p=P))\
                    .then_inc(s_wd[s % 3], 16)

            pool.wait_ge(s_wio, 32)
            for s in range(3):
                load_slice(s)
            for s in range(4):
                pool.wait_ge(s_wd[s % 3], 16 * (s // 3 + 1))
                src, dst = WA[s % 3], WB
                for n, h in enumerate((1, 2)):
                    i = src.rearrange("p (g t h) d -> p g t (h d)", t=2, h=h)
                    q = dst.rearrange("p (g t h) d -> p g t (h d)", t=2, h=h)
                    if s or n:
                        pool.wait_ge(s_fly, 4 * s + 2 * n)
                    pool.tensor_tensor(q[:, :, 0, :], i[:, :, 0, :], i[:, :, 1, :], ALU.add).then_inc(s_fly, 1)
                    pool.tensor_tensor(q[:, :, 1, :], i[:, :, 0, :], i[:, :, 1, :], ALU.subtract).then_inc(s_fly, 1)
                    src, dst = dst, src
                if s == 2:
                    pool.wait_ge(s_sl, 1)
                    load_slice(3)
            pool.wait_ge(s_lst, 16)
            with pool.Fori(0, B // 2) as it:
                for j in range(2):
                    wait_apart(pool, s_pos, it * 2 + (j + 1), s_ppassed)
                    for t in range(TT):
                        for c in range(TOPK):
                            pool.indirect_dma_start(d_list, bass.IndirectOffsetOnAxis(ap=POS[:, j, t, c:c + 1], axis=0),
                                                    IDC[:, j, t:t + 1], None).then_inc(s_ids[j], 16)
                for j in range(2):
                    pool.wait_ge(s_ids[j], it * (16 * TT * TOPK) + 16 * TT * TOPK)
                pool.sem_inc(s_idu, 1)
            pool.wait_ge(s_idx, 16)
            pool.wait_ge(s_tab, 1)
            pool.wait_ge(s_zst, 16 * B)
            pool.wait_ge(s_gst, 16 * B)
            pool.wait_ge(s_res, 16 * B)
            pool.wait_ge(s_spare, 32)
            def gather(t, u, n):
                col = pool.value_load(TAB[0:1, 3, bass.ds(t, 1)], min_val=0, max_val=NE * LIST)
                if n is not None:
                    pool.wait_ge(s_add[u % V], n * 16 + 16)
                pool.tensor_copy(GIX[:, u:u + 1], IDX[:, bass.ds(col, 1)]).then_inc(s_gi, 1)
                wait_apart(pool, s_gi, t + 1, s_ppassed)
                pool.indirect_dma_start(xg[u], None, d_tok, bass.IndirectOffsetOnAxis(ap=GIX[:, u:u + 1], axis=0))\
                    .then_inc(s_xg[u], 16)

            def add(t, u):
                first = pool.value_load(TAB[0:1, 4, bass.ds(t, 1)], min_val=0, max_val=NTILE - 1)
                for w in range(V):
                    pool.wait_ge(s_add[w], ((first + (V - 1 - w)) // V) * 16 + 16)
                wait_apart(pool, s_y, t + 1, s_ppassed)
                pool.indirect_dma_start(a_out, bass.IndirectOffsetOnAxis(ap=GIX[:, u:u + 1], axis=0), yt[u % V], None,
                                        compute_op=ALU.add).then_inc(s_add[u % V], 16)

            for t in range(AHEAD):
                gather(t, t, None)
            for u in range(U):
                gather(u + AHEAD, (u + AHEAD) % U, (u + AHEAD - U) // V + 1 if u + AHEAD >= U else None)
                add(u, u)
            with pool.Fori(1, NTILE // U) as it:
                for u in range(U):
                    t = it * U + u
                    gather(t + AHEAD, (u + AHEAD) % U, it * (U // V) + (u + AHEAD - U) // V + 1)
                    add(t, u)

        @block.scalar
        def _(act):
            act.wait_ge(s_const, 16)
            act.activation(sm[:, 0:1], COLS[:, C_DEC:C_DEC + 1], ACT.Sigmoid).then_inc(s_dec, 1)

            def fold_split_hi(s):
                act.wait_ge(s_fly, 4 * (s + 1))
                wait(act, s_w2p, 4 * s)
                act.activation(Sh, WA[s % 3], ACT.Copy, scale=W_S).then_inc(s_sh, 1)

            def fold_hi(s):
                act.wait_ge(s_w2p, 4 * s + 4)
                act.activation(w2h[:, :, s * P:(s + 1) * P], PS[:, 4:8, :].rearrange("p g (c n) -> p (g c) n", n=P), ACT.Copy,
                               scale=1.0 / N_S).then_inc(s_w2h, 1)

            def ffn_weights_hi(first, last):
                for c in range(first, last):
                    act.wait_ge(s_ws[c], 16)
                    if c >= 4:
                        act.wait_ge(s_wul, c - 1)
                    act.activation(wug[:, c, 0:KC * 512], wst[c].rearrange("p k f -> p (k f)"), ACT.Copy, scale=W_S)\
                        .then_inc(s_wuh, 1)

            def transposed_hi(count, dst, bank, scale):
                act.wait_ge(s_tr, count)
                src = PS[:, bank, :]
                if len(dst.shape) == 3:
                    src = src.rearrange("p (a n) -> p a n", n=P)
                act.activation(dst, src, ACT.Copy, scale=scale).then_inc(s_thi, 1)

            def chunk_hi(b, k):
                transposed_hi(b * 4 + (k + 1), uh[k], 2 + k % 2, COLS[:, C_SUG + k:C_SUG + k + 1])

            def hadamard_hi(b, j):
                act.wait_ge(s_hd, b * 4 + (j + 1))
                act.activation(had_hi(b, j), PS[:, 2 + j % 2, :], ACT.Copy).then_inc(s_thi, 1)

            def ffn_silu(F, f, p):
                act.wait_ge(s_g, F + 1)
                act.activation(gs[p], PS[:, 0, :], ACT.Silu, scale=SG[:, 1, f]).then_inc(s_silu, 1)

            def ffn_chunk_hi(F, p):
                act.wait_ge(s_a, F + 1)
                act.activation(ah[p], af[p], ACT.Copy).then_inc(s_ah, 1)

            def split_half(e, h):
                act.wait_ge(s_est[h], e * 16 + 16)
                act.wait_ge(s_eo, e * 64 + (1 + 32 * h))
                act.activation(eoh, est[h], ACT.Copy, scale=E_S).then_inc(s_eh, 1)

            def first_half(b):
                for p in range(2):
                    if p:
                        ffn_silu(b * FC + p, slice(p, p + 1), p)
                    ffn_chunk_hi(b * FC + p, p)
                    split_half(b * (FC // 2), p)
                with act.Fori(1, FC // 4) as i:
                    for p in range(2):
                        ffn_silu(b * FC + i * 2 + p, bass.ds(i * 2 + p, 1), p)
                        ffn_chunk_hi(b * FC + i * 2 + p, p)
                        split_half(b * (FC // 2) + i, p)

            fold_split_hi(0)
            act.wait_ge(s_summ, B)
            act.wait_ge(s_lst, 16)
            fold_hi(0)
            fold_split_hi(1)
            ffn_weights_hi(0, 2)
            for k in range(2):
                chunk_hi(0, k)
            fold_hi(1)
            for k in range(2, KC):
                chunk_hi(0, k)
            fold_split_hi(2)
            ffn_weights_hi(2, 3)
            for j in range(KC):
                hadamard_hi(0, j)
            ffn_weights_hi(3, 4)
            fold_hi(2)
            fold_split_hi(3)
            ffn_weights_hi(4, 6)
            ffn_silu(0, slice(0, 1), 0)
            ffn_weights_hi(6, 8)
            fold_hi(3)
            def round_hi(q, k, dst, bank):
                transposed_hi(q * 4 + (k + 1), dst, bank, H_S)

            def second_half(b, following):
                for f in range(FC // 2, FC):
                    ffn_silu(b * FC + f, slice(f, f + 1), f % 2)
                    ffn_chunk_hi(b * FC + f, f % 2)
                    split_half(b * (FC // 2) + f // 2, f % 2)
                    following(f)

            def next_ffn(b):
                def work(f):
                    if f in (9, 10):
                        for k in (2 * f - 18, 2 * f - 17):
                            chunk_hi(b, k)
                    if 11 <= f < 15:
                        hadamard_hi(b, f - 11)
                return work

            def next_queries(f):
                if f in (9, 10):
                    for k in (2 * f - 18, 2 * f - 17):
                        round_hi(Q_ROUND[0], k, had_hi(0, k), 2 + k % 2)

            with act.Fori(0, B - 1) as b:
                first_half(b)
                second_half(b, next_ffn(b + 1))
                ffn_silu(b * FC + FC, slice(0, 1), 0)
            first_half(B - 1)
            second_half(B - 1, next_queries)

            def first_keys_hi(n):
                act.wait_ge(s_cT0[n], 16)
                act.activation(cTh[0][:, :, half_keys(n)], cT0[:, :, half_keys(n)], ACT.Copy, scale=C_S).then_inc(s_cth, 1)

            def keys_hi(b):
                act.wait_ge(s_cT, b * 16)
                act.activation(cTh[b % 2], cTst, ACT.Copy, scale=C_S).then_inc(s_cth, 1)

            def values_hi(b):
                act.wait_ge(s_cN, b * 16 + 16)
                if b:
                    act.wait_ge(s_val, B)
                act.activation(cNh[b % 2], cNst, ACT.Copy, scale=C_S).then_inc(s_cnh, 1)

            def exp_tile(t):
                act.wait_ge(s_nm, t + 1)
                wait(act, s_pt, t)
                act.activation(pr, sc, ACT.Exp, bias=attn[:, t % 2, 1:2], accum_out=attn[:, t % 2, 2:3])\
                    .then_inc(s_p, 1)

            def router_exp(b):
                act.wait_ge(s_dif, b + 1)
                act.activation(RT[:, 3, :, :], RT[:, 2, :, :], ACT.Exp).then_inc(s_rex, 1)

            def side(b, slot, place):
                what, of, k = beside(b, slot, place)
                if what == "q":
                    round_hi(Q_ROUND[of], k, had_hi(of, k), 7)
                elif what == "r":
                    round_hi(R_ROUND[of], k, rh[:, k, :], 7)

            act.wait_ge(s_gk, 16)
            act.activation(gkh[:, :, :], gk[:, :, :], ACT.Copy, scale=E_S).then_inc(s_gkh, 1)
            act.wait_ge(s_dn, B * FC)
            for n in range(2):
                first_keys_hi(n)
            values_hi(0)
            exp_tile(0)
            for b in range(B):
                for slot in range(TT):
                    t = b * TT + slot
                    act.wait_ge(s_pt, t + 1)
                    wait(act, s_rd, t)
                    act.activation(pTh, PS[:, 4:6, :].rearrange("p b (c n) -> p (b c) n", n=P), ACT.Copy, scale=P_S)\
                        .then_inc(s_pth, 1)
                    side(b, slot, 0)
                    if slot == CHOOSE[b]:
                        router_exp(b - 1)
                    side(b, slot, 1)
                    if t == 0:
                        for i in range(B):
                            keys = mask[:, i * T2:(i + 1) * T2]
                            act.activation(keys, keys, ACT.Copy, accum_out=valid[:, i:i + 1]).then_inc(s_val, 1)
                    if t < NT - 1:
                        exp_tile(t + 1)
                    if slot == (1 if b else 0) and b < B - 1:
                        keys_hi(b + 1)
                    if slot == (2 if b else 1) and b < B - 1:
                        values_hi(b + 1)
                    side(b, slot, 2)
            for k in range(KC):
                round_hi(R_ROUND[B - 1], k, rh[:, k, :], k)
            router_exp(B - 1)

            def tile_hi(t, p):
                landed = act.value_load(TAB[0:1, 1, bass.ds(t, 1)], min_val=16, max_val=16 * NE)
                act.wait_ge(s_wl, landed)
                act.wait_ge(s_xt, t + 1)
                act.activation(xh[p], PS[:, p, :].rearrange("p (k n) -> p k n", n=P), ACT.Copy, scale=H_S).then_inc(s_xh, 1)

            def tile_silu(t, p):
                act.wait_ge(s_ug, t + 1)
                act.activation(eg[p], PS[:, 2 + p, 0:M], ACT.Silu, scale=1.0 / (H_S * E_S)).then_inc(s_es, 1)

            def hidden_hi(t, p):
                act.wait_ge(s_at, t + 1)
                act.activation(eah[p], PS[:, 4, 0:2 * P], ACT.Copy).then_inc(s_ah2, 1)

            act.wait_ge(s_tab, 1)
            tile_hi(0, 0)
            tile_hi(1, 1)
            tile_silu(0, 0)
            with act.Fori(0, NTILE // U) as it:
                for u in range(U):
                    t = it * U + u
                    tile_hi(t + 2, u % 2)
                    hidden_hi(t, u % 2)
                    tile_silu(t + 1, (u + 1) % 2)

        @block.vector
        def _(dve):
            v = nc.vector
            v.memset(ones, 1.0).then_inc(s_pre, 1)
            dve.wait_ge(s_const, 16)
            v.tensor_scalar(SG[:, :, :], COLS[:, C_WU:C_WU + 2 * FC].rearrange("p (a f) -> p a f", a=2),
                            1.0 / (W_S * D ** 0.5), None, ALU.mult).then_inc(s_pre, 1)
            dve.wait_ge(s_pre, 2)
            v.scalar_tensor_tensor(SG[:, 0, :], SG[:, 0, :], U_S, COLS[:, C_SDP:C_SDP + FC], ALU.mult, ALU.mult)\
                .then_inc(s_pre, 1)
            dve.wait_ge(s_dec, 1)
            v.tensor_tensor_scan(vrow, sm[:, 0:1].to_broadcast([P, T2]), ones, 0.0, ALU.mult, ALU.add)\
                .then_inc(s_pre, 1)
            dve.wait_ge(s_pre, 4)
            v.reduce_sum(sm[:, 1:2], vrow, AXX).then_inc(s_pre, 1)
            dve.wait_ge(s_pre, 5)
            v.tensor_scalar(sm[:, 2:2 + KC], COLS[:, C_BIN:C_BIN + KC], sm[:, 1:2], 1.0 / T2, ALU.mult, ALU.mult)\
                .then_inc(s_pre, 1)
            for b in range(B):
                dve.wait_ge(s_cx[b], 16)
                for k in range(KC):
                    if b or k:
                        dve.wait_ge(s_ttr, b * KC + k)
                    v.tensor_tensor_reduce(out=junk, in0=cxT[b][:, k, :], in1=vrow[:, ::-1], scale=1.0, scalar=0.0,
                                           op0=ALU.mult, op1=ALU.add, accum_out=cm[:, k, b:b + 1]).then_inc(s_ttr, 1)
            def fold_split_lo(s):
                dve.wait_ge(s_sh, s + 1)
                v.scalar_tensor_tensor(Sl, WA[s % 3], W_S, Sh, ALU.mult, ALU.subtract).then_inc(s_sl, 1)

            def fold_lo(s):
                dve.wait_ge(s_w2h, s + 1)
                v.scalar_tensor_tensor(w2l[:, :, s * P:(s + 1) * P], PS[:, 4:8, :].rearrange("p g (c n) -> p (g c) n", n=P),
                                       1.0 / N_S, w2h[:, :, s * P:(s + 1) * P], ALU.mult, ALU.subtract).then_inc(s_w2l, 1)

            def ffn_weights_lo(first, last):
                for c in range(first, last):
                    dve.wait_ge(s_wuh, c + 1)
                    v.scalar_tensor_tensor(wug[:, c, KC * 512:2 * KC * 512], wst[c].rearrange("p k f -> p (k f)"), W_S,
                                           wug[:, c, 0:KC * 512], ALU.mult, ALU.subtract).then_inc(s_wul, 1)

            def moments(n, src):
                for t in range(TT):
                    v.bn_stats(st[:, t, :], src(t)).then_inc(s_bn, 1)
                for t in range(TT):
                    wait_apart(dve, s_bn, n * TT + (t + 1), s_passed)
                    v.bn_aggr(mv[:, t, :], st[:, t, :]).then_inc(s_mv, 1)
                dve.wait_ge(s_mv, n * TT + TT)

            def inverse_root(m):
                steps = m * NEWTON
                var, half, y, work = (nw[:, i, :] for i in range(4))
                v.tensor_scalar(var, mv[:, :, 1], EPS, None, ALU.add).then_inc(s_nw, 1)
                dve.wait_ge(s_nw, steps + 1)
                v.tensor_scalar(work.bitcast(I32), var.bitcast(I32), 1, None, ALU.logical_shift_right).then_inc(s_nw, 1)
                dve.wait_ge(s_nw, steps + 2)
                v.tensor_scalar(y.bitcast(I32), work.bitcast(I32), -1, MAGIC, ALU.mult, ALU.add).then_inc(s_nw, 1)
                v.tensor_scalar(half, var, -0.5, None, ALU.mult).then_inc(s_nw, 1)
                for i in range((NEWTON - 4) // 3):
                    dve.wait_ge(s_nw, steps + (4 + 3 * i))
                    v.tensor_tensor(work, y, half, ALU.mult).then_inc(s_nw, 1)
                    dve.wait_ge(s_nw, steps + (5 + 3 * i))
                    v.tensor_tensor(work, work, y, ALU.mult).then_inc(s_nw, 1)
                    dve.wait_ge(s_nw, steps + (6 + 3 * i))
                    v.scalar_tensor_tensor(y, work, 1.5, y, ALU.add, ALU.mult).then_inc(s_nw, 1)
                dve.wait_ge(s_nw, steps + NEWTON)

            def normalise(used, tile, rstd, dst):
                wait(dve, s_tr, used * 4)
                for t in range(TT):
                    v.tensor_scalar(dst[:, t, :], xt(tile + t), mv[:, t, 0:1], rstd[:, t:t + 1],
                                    ALU.subtract, ALU.mult).then_inc(s_h, 1)

            def mixer_ln(b, stage):
                tile = b * TT
                rstd = nw[:, 2, :]
                if stage == 0:
                    moments(b * 3, lambda t: xt(tile + t))
                elif stage == 1:
                    inverse_root(b * 3)
                    for t in range(TT):
                        v.scalar_tensor_tensor(Z[:, t, :], xt(tile + t), rstd[:, t:t + 1], summ(b), ALU.mult, ALU.add)\
                            .then_inc(s_z, 1)
                elif stage == 2:
                    wait_apart(dve, s_z, b * 16 + 4, s_passed)
                    moments(b * 3 + 1, lambda t: Z[:, t, :])
                    for t in range(TT):
                        v.tensor_tensor(xt(tile + t), xt(tile + t), ROWS[:, 1, :], ALU.add).then_inc(s_z, 1)
                elif stage == 3:
                    inverse_root(b * 3 + 1)
                    for t in range(TT):
                        v.scalar_tensor_tensor(Z[:, t, :], Z[:, t, :], mv[:, t, 0:1], ROWS[:, 0, :],
                                               ALU.subtract, ALU.mult).then_inc(s_z, 1)
                elif stage == 4:
                    for t in range(TT):
                        dve.wait_ge(s_z, b * 16 + (9 + t))
                        v.scalar_tensor_tensor(xt(tile + t), Z[:, t, :], rstd[:, t:t + 1], xt(tile + t),
                                               ALU.mult, ALU.add).then_inc(s_z, 1)
                elif stage == 5:
                    wait_apart(dve, s_z, b * 16 + 16, s_passed)
                    moments(b * 3 + 2, lambda t: xt(tile + t))
                elif stage == 6:
                    inverse_root(b * 3 + 2)
                else:
                    normalise(b, tile, rstd, Z)

            def ln_scale(q, b):
                moments(q + 2 * B, lambda t: xt(b * TT + t))
                inverse_root(q + 2 * B)

            def ln_apply(b, dst, used):
                normalise(used, b * TT, nw[:, 2, :], dst)

            def summ(b):
                return SUMM[:, :, :].rearrange("p b d -> p (b d)")[:, bass.ds(b * D, D)]

            def chunk_lo(b, k):
                dve.wait_ge(s_thi, b * 8 + (k + 1))
                v.scalar_tensor_tensor(ul[k], PS[:, 2 + k % 2, :].rearrange("p (a n) -> p a n", n=P),
                                       COLS[:, C_SUG + k:C_SUG + k + 1], uh[k], ALU.mult, ALU.subtract).then_inc(s_tlo, 1)

            def hadamard_lo(b, j):
                dve.wait_ge(s_thi, b * 8 + (5 + j))
                v.tensor_tensor(had_lo(b, j), PS[:, 2 + j % 2, :], had_hi(b, j), ALU.subtract).then_inc(s_tlo, 1)

            def ffn_chunk(F, f, p):
                dve.wait_ge(s_silu, F + 1)
                dve.wait_ge(s_u, F + 1)
                v.scalar_tensor_tensor(af[p], PS[:, 1, :], SG[:, 0, f], gs[p], ALU.mult, ALU.mult).then_inc(s_a, 1)

            def ffn_chunk_lo(F, p):
                dve.wait_ge(s_ah, F + 1)
                v.tensor_tensor(al[p], af[p], ah[p], ALU.subtract).then_inc(s_al, 1)

            def split_half(e, h):
                dve.wait_ge(s_eh, e * 2 + (h + 1))
                if h == 0:
                    v.scalar_tensor_tensor(eol, est[0], E_S, eoh, ALU.mult, ALU.subtract).then_inc(s_el, 1)
                else:
                    nl = EL - EH
                    v.scalar_tensor_tensor(eol[:, 0:nl], est[1][:, 0:nl], E_S, eoh[:, 0:nl], ALU.mult, ALU.subtract)\
                        .then_inc(s_el2, 1)
                    dve.wait_ge(s_el2, e + 1)
                    v.scalar_tensor_tensor(eoh[ML:P, nl:EH], est[1][ML:P, nl:EH], E_S, eoh[ML:P, nl:EH],
                                           ALU.mult, ALU.subtract).then_inc(s_el, 1)

            def ffn_scale(b):
                dve.wait_ge(s_dn, b * FC + FC)
                for t in range(TT):
                    v.scalar_tensor_tensor(Z[:, t, :], PS[:, 4 + t, :], N_S / (U_S * W_S * INTER ** 0.5), ROWS[:, 3, :], ALU.mult, ALU.mult)\
                        .then_inc(s_y2, 1)

            def ffn_add(b):
                for t in range(TT):
                    dve.wait_ge(s_y2, b * TT + (t + 1))
                    v.tensor_tensor(xt(b * TT + t), xt(b * TT + t), Z[:, t, :], ALU.add).then_inc(s_x2, 1)

            dve.wait_ge(s_x, 16)
            mixer_ln(0, 0)
            dve.wait_ge(s_st, 1)
            dve.wait_ge(s_pre, 6)
            for k in range(KC):
                v.tensor_scalar(sT[:, k, :], PS[:, 0, k * B:(k + 1) * B], 1.0 / T2, sm[:, 2 + k:3 + k],
                                ALU.mult, ALU.add).then_inc(s_sT, 1)
            dve.wait_ge(s_rows, 64)
            dve.wait_ge(s_sT, KC)
            dve.wait_ge(s_sb, 1)
            v.tensor_copy(ssum, PS[0:B, 1, :]).then_inc(s_sTb, 1)

            def spread(b):
                dve.wait_ge(s_smp, b + 1)
                v.tensor_tensor(SUMM[:, b, :], PS[:, 2 + b % 2, :], ROWS[:, 2, :], ALU.add).then_inc(s_summ, 1)

            spread(0)
            dve.wait_ge(s_summ, 1)
            mixer_ln(0, 1)
            for b in range(1, B):
                spread(b)
            fold_split_lo(0)
            mixer_ln(0, 2)
            mixer_ln(0, 3)
            fold_lo(0)
            mixer_ln(0, 4)
            fold_split_lo(1)
            for stage in range(5, 8):
                mixer_ln(0, stage)
            ffn_weights_lo(0, 1)
            for k in range(2):
                chunk_lo(0, k)
            fold_lo(1)
            for k in range(2, KC):
                chunk_lo(0, k)
            fold_split_lo(2)
            for j in range(KC):
                hadamard_lo(0, j)
                if j < 2:
                    ffn_weights_lo(1 + j, 2 + j)
            ffn_weights_lo(3, 4)
            fold_lo(2)
            fold_split_lo(3)
            ffn_weights_lo(4, 8)
            dve.wait_ge(s_w2p, 16)
            ffn_chunk(0, slice(0, 1), 0)
            fold_lo(3)
            ffn_chunk_lo(0, 0)
            with dve.Fori(0, B - 1) as b:
                for f in range(FC):
                    if f:
                        ffn_chunk(b * FC + f, slice(f, f + 1), f % 2)
                        ffn_chunk_lo(b * FC + f, f % 2)
                    split_half(b * (FC // 2) + f // 2, f % 2)
                    if f == 1:
                        dve.wait_ge(s_x, 48)
                        dve.sem_inc(s_passed, 1)
                    if 1 <= f <= 8:
                        mixer_ln(b + 1, f - 1)
                    if f in (9, 10):
                        for k in (2 * f - 18, 2 * f - 17):
                            chunk_lo(b + 1, k)
                    if 11 <= f < 15:
                        hadamard_lo(b + 1, f - 11)
                ffn_chunk(b * FC + FC, slice(0, 1), 0)
                ffn_scale(b)
                ffn_chunk_lo(b * FC + FC, 0)
                ffn_add(b)
            def round_lo(q, k, hi, lo, bank):
                dve.wait_ge(s_thi, copied_before(q) + k + 1)
                v.scalar_tensor_tensor(lo, PS[:, bank, :], H_S, hi, ALU.mult, ALU.subtract).then_inc(s_tlo, 1)

            split_half((B - 1) * (FC // 2), 0)
            ffn_chunk((B - 1) * FC + 1, slice(1, 2), 1)
            ffn_chunk_lo((B - 1) * FC + 1, 1)
            split_half((B - 1) * (FC // 2), 1)
            with dve.Fori(1, FC // 4) as i:
                for p in range(2):
                    ffn_chunk((B - 1) * FC + i * 2 + p, bass.ds(i * 2 + p, 1), p)
                    ffn_chunk_lo((B - 1) * FC + i * 2 + p, p)
                    split_half((B - 1) * (FC // 2) + i, p)
            for f in range(FC // 2, FC):
                ffn_chunk((B - 1) * FC + f, slice(f, f + 1), f % 2)
                ffn_chunk_lo((B - 1) * FC + f, f % 2)
                split_half((B - 1) * (FC // 2) + f // 2, f % 2)
                if f == 8:
                    ln_scale(Q_ROUND[0], 0)
                    ln_apply(0, Z, B)
                if f in (9, 10):
                    for k in (2 * f - 18, 2 * f - 17):
                        round_lo(Q_ROUND[0], k, had_hi(0, k), had_lo(0, k), 2 + k % 2)

            def first_keys_lo(n):
                dve.wait_ge(s_cth, n + 1)
                v.scalar_tensor_tensor(cTl[0][:, :, half_keys(n)], cT0[:, :, half_keys(n)], C_S, cTh[0][:, :, half_keys(n)],
                                       ALU.mult, ALU.subtract).then_inc(s_ctl, 1)

            def keys_lo(b):
                dve.wait_ge(s_cth, b + 2)
                v.scalar_tensor_tensor(cTl[b % 2], cTst, C_S, cTh[b % 2], ALU.mult, ALU.subtract).then_inc(s_ctl, 1)

            def values_lo(b):
                dve.wait_ge(s_cnh, b + 1)
                v.scalar_tensor_tensor(cNl[b % 2], cNst, C_S, cNh[b % 2], ALU.mult, ALU.subtract).then_inc(s_cnl, 1)

            def softmax_tile(t):
                p, b = t % 2, t // TT
                dve.wait_ge(s_sc, t + 1)
                wait(dve, s_p, t)
                v.scalar_tensor_tensor(sc, PS[:, 2 * p:2 * p + 2, :].rearrange("p a n -> p (a n)"),
                                       D ** -0.5 / (H_S * C_S), bias[:, b * T2:(b + 1) * T2], ALU.mult, ALU.add)\
                    .then_inc(s_s, 1)
                dve.wait_ge(s_s, t + 1)
                v.reduce_max(attn[:, p, 0:1], sc, AXX).then_inc(s_mx, 1)
                dve.wait_ge(s_mx, t + 1)
                v.tensor_scalar(attn[:, p, 1:2], attn[:, p, 0:1], -1.0, None, ALU.mult).then_inc(s_nm, 1)

            def readout_add(t):
                p, b = t % 2, t // TT
                dve.wait_ge(s_p, t + 1)
                v.reciprocal(attn[:, p, 3:4], attn[:, p, 2:3]).then_inc(s_rc, 1)
                dve.wait_ge(s_rc, t + 1)
                v.tensor_tensor(attn[:, p, 4:5], attn[:, p, 3:4], valid[:, b:b + 1], ALU.mult).then_inc(s_rv, 1)
                dve.wait_ge(s_rv, t + 1)
                dve.wait_ge(s_rd, t + 1)
                v.scalar_tensor_tensor(xt(t), PS[:, 6, :], attn[:, p, 4:5], xt(t), ALU.mult, ALU.add).then_inc(s_xr, 1)

            def choose(b):
                j = b % 2
                dve.wait_ge(s_lg, b + 1)
                v.tensor_scalar(RT[:, 0, :, :], PS[:, 7, 0:TT * NE].rearrange("p (t e) -> p t e", e=NE),
                                1.0 / (H_S * E_S), None, ALU.mult).then_inc(s_L, 1)
                wait_apart(dve, s_L, b + 1, s_passed)
                for t in range(TT):
                    v.max(M8[:, t, :], RT[:, 0, t, :]).then_inc(s_m8, 1)
                wait_apart(dve, s_m8, b * TT + TT, s_passed)
                for t in range(TT):
                    v.match_replace(RT[:, 1, t, :], M8[:, t, :], RT[:, 0, t, :], -3e38).then_inc(s_mr, 1)
                v.tensor_tensor(RT[:, 2, :, :], RT[:, 0, :, :], M8[:, :, 0:1].to_broadcast([P, TT, NE]), ALU.subtract)\
                    .then_inc(s_dif, 1)
                dve.wait_ge(s_mr, b * TT + TT)
                v.tensor_tensor(SEL[:, :, :], RT[:, 0, :, :], RT[:, 1, :, :], ALU.not_equal).then_inc(s_sel, 1)
                dve.wait_ge(s_sel, b + 1)
                dve.wait_ge(s_rex, b + 1)
                v.tensor_tensor(RT[:, 1, :, :], SEL[:, :, :], RT[:, 3, :, :], ALU.mult).then_inc(s_gx, 1)
                dve.wait_ge(s_gx, b + 1)
                v.reduce_sum(RS[:, 0, :], RT[:, 1, :, :], AXX).then_inc(s_gs, 1)
                dve.wait_ge(s_gs, b + 1)
                v.reciprocal(RS[:, 1, :], RS[:, 0, :]).then_inc(s_grc, 1)
                dve.wait_ge(s_grc, b + 1)
                wait(dve, s_gst, 16 * (b - 1))
                v.scalar_tensor_tensor(G[:, j, :, :], RT[:, 1, :, :], 1.0 / E_S,
                                       RS[:, 1, :].unsqueeze(2).to_broadcast([P, TT, NE]), ALU.mult, ALU.mult).then_inc(s_G, 1)

            def place(b):
                steps, j = b * (6 + TT), b % 2
                dve.wait_ge(s_rkp, b + 1)
                v.tensor_copy(RI[:, 0, :], PS[:, 7, 0:TT * NE]).then_inc(s_rk, 1)
                dve.wait_ge(s_rk, b + 1)
                v.tensor_scalar(RI[:, 1, :], RI[:, 0, :], P - 1, 9, ALU.bitwise_and, ALU.logical_shift_left).then_inc(s_ro, 1)
                v.tensor_scalar(RI[:, 2, :], RI[:, 0, :], 7, None, ALU.logical_shift_right).then_inc(s_ro, 1)
                dve.wait_ge(s_ro, steps + 2)
                v.tensor_tensor(RP[:, :], RI[:, 1, :], RI[:, 2, :], ALU.add).then_inc(s_ro, 1)
                dve.wait_ge(s_ro, steps + 3)
                v.tensor_tensor(RP[:, :], RP[:, :], EOFF[:, :, :].rearrange("p t e -> p (t e)"), ALU.add).then_inc(s_ro, 1)
                dve.wait_ge(s_ro, steps + 4)
                v.tensor_tensor(RP[:, :], RP[:, :], SEL[:, :, :].rearrange("p t e -> p (t e)"), ALU.mult).then_inc(s_ro, 1)
                wait_apart(dve, s_ro, steps + 5, s_passed)
                for t in range(TT):
                    v.max(M8[:, t, :], RP[:, t * NE:(t + 1) * NE]).then_inc(s_ro, 1)
                dve.wait_ge(s_idu, b // 2 + 1)
                v.tensor_copy(IDC[:, j, :], IDS[:, bass.ds(b * TT, TT)]).then_inc(s_idc, 1)
                dve.wait_ge(s_idc, b + 1)
                dve.wait_ge(s_ro, steps + (5 + TT))
                v.tensor_scalar(POS[:, j, :, :], M8[:, :, :], -1.0, None, ALU.add).then_inc(s_pos, 1)
                v.reduce_sum(RT[:, 0, 0, :], SEL[:, :, :].rearrange("p t e -> p e t"), AXX).then_inc(s_ro, 1)
                dve.wait_ge(s_ro, steps + (6 + TT))
                v.tensor_tensor(SELS[:, :], SELS[:, :], RT[:, 0, 0, :], ALU.add).then_inc(s_ss, 1)

            dve.wait_ge(s_rc0, 4)
            dve.wait_ge(s_gkh, 1)
            v.scalar_tensor_tensor(gkl[:, :, :], gk[:, :, :], E_S, gkh[:, :, :], ALU.mult, ALU.subtract).then_inc(s_gkl, 1)
            def side_ln(b, slot, apply):
                if slot == 0 and b:
                    if apply:
                        wait(dve, s_zst, 16 * (b - 1))
                        ln_apply(b - 1, Z, (R_ROUND[b - 2] if b > 1 else Q_ROUND[0]) + 1)
                    else:
                        dve.wait_ge(s_xr, b * TT)
                        ln_scale(R_ROUND[b - 1], b - 1)
                if slot == 0 and b == 0:
                    if apply:
                        ln_apply(1, ROWS, 0)
                    else:
                        ln_scale(Q_ROUND[1], 1)
                if slot == (1 if b else 3) and b + 2 < B:
                    if apply:
                        ln_apply(b + 2, ROWS, Q_ROUND[b + 1] + 1)
                    else:
                        ln_scale(Q_ROUND[b + 2], b + 2)

            def side(b, slot, place_):
                what, of, k = beside(b, slot, place_)
                if what == "q":
                    round_lo(Q_ROUND[of], k, had_hi(of, k), had_lo(of, k), 7)
                elif what == "r":
                    round_lo(R_ROUND[of], k, rh[:, k, :], rl[:, k, :], 7)

            for n in range(2):
                first_keys_lo(n)
            dve.wait_ge(s_mask, 16)
            v.tensor_scalar(bias, mask, 1.0, 1e30, ALU.subtract, ALU.mult).then_inc(s_bias, 1)
            ffn_scale(B - 1)
            dve.wait_ge(s_bias, 1)
            softmax_tile(0)
            ffn_add(B - 1)
            values_lo(0)
            for b in range(B):
                for slot in range(TT):
                    t = b * TT + slot
                    dve.wait_ge(s_pth, t + 1)
                    v.scalar_tensor_tensor(pTl, PS[:, 4:6, :].rearrange("p b (c n) -> p (b c) n", n=P), P_S, pTh,
                                           ALU.mult, ALU.subtract).then_inc(s_ptl, 1)
                    side(b, slot, 0)
                    if slot == CHOOSE[b]:
                        choose(b - 1)
                    side_ln(b, slot, False)
                    if t < NT - 1:
                        softmax_tile(t + 1)
                    side(b, slot, 1)
                    if t == 0:
                        dve.wait_ge(s_val, B)
                        v.tensor_scalar(valid[:, :], valid[:, :], 1.0, 1.0 / (P_S * C_S), ALU.min, ALU.mult).then_inc(s_val, 1)
                        dve.wait_ge(s_val, B + 1)
                    side_ln(b, slot, True)
                    if slot == (2 if b else 1) and b < B - 1:
                        keys_lo(b + 1)
                    if slot == (3 if b else 2) and b < B - 1:
                        values_lo(b + 1)
                    if slot == CHOOSE[b]:
                        place(b - 1)
                    readout_add(t)
                    side(b, slot, 2)
            side_ln(B, 0, False)
            side_ln(B, 0, True)
            for k in range(KC):
                round_lo(R_ROUND[B - 1], k, rh[:, k, :], rl[:, k, :], k)
            choose(B - 1)
            place(B - 1)
            v.memset(zrow, 0.0).then_inc(s_zr, 1)
            v.tensor_scalar(IDX[:, NE * LIST:NE * LIST + 1], IDS[:, 0:1], NTOK, None, ALU.add).then_inc(s_zr, 1)

            dve.wait_ge(s_tp, 1)
            v.tensor_scalar(CI[0:NE, 0:1], PS[0:NE, 0, 0:1], P - 1.0, None, ALU.add).then_inc(s_tq, 1)
            dve.wait_ge(s_tq, 1)
            v.tensor_scalar(CI[0:NE, 1:2], CI[0:NE, 0:1], 7, None, ALU.logical_shift_right).then_inc(s_tq, 1)
            dve.wait_ge(s_tq, 2)
            v.tensor_copy(CH[0:NE, 0:1], CI[0:NE, 1:2]).then_inc(s_tq, 1)
            dve.wait_ge(s_tp, 2)
            v.tensor_copy(CE[0:NE, 0:1], PS[0:NE, 1, 0:1]).then_inc(s_tq, 1)
            v.tensor_copy(CH[0:NE, 1:2], PS[0:NE, 1, 0:1]).then_inc(s_tq, 1)
            dve.wait_ge(s_tq, 4)
            v.tensor_scalar(TCMP[0:NE, :], TROW[0:NE, :], CE[0:NE, 0:1], None, ALU.is_ge).then_inc(s_tq, 1)
            dve.wait_ge(s_tp, 3)
            erow, start = PS[0:1, 2, 0:TABLE], PS[0:1, 2, TABLE:2 * TABLE]
            trow = TROW[0:1, :]
            v.tensor_scalar(TAB[:, 0, :], erow, NE - 1.0, None, ALU.min).then_inc(s_tq, 1)
            v.tensor_scalar(TAB[:, 1, :], erow, NE - 1.0, 1.0, ALU.min, ALU.add).then_inc(s_tq, 1)
            v.scalar_tensor_tensor(TWK[:, 0, :], erow, float(LIST), trow, ALU.mult, ALU.add).then_inc(s_tq, 1)
            v.tensor_tensor(TWK[:, 2, :], trow, start, ALU.subtract).then_inc(s_tq, 1)
            v.tensor_scalar(TCUM[:, :], PS[0:1, 2, 2 * TABLE:2 * TABLE + NE], 1.0, None, ALU.add).then_inc(s_tq, 1)
            dve.wait_ge(s_tq, 10)
            v.tensor_scalar(TAB[:, 2, :], TAB[:, 0, :], 1, None, ALU.bitwise_and).then_inc(s_tq, 1)
            v.tensor_scalar(TAB[:, 1, :], TAB[:, 1, :], 16, None, ALU.mult).then_inc(s_tq, 1)
            v.tensor_tensor(TWK[:, 1, :], TWK[:, 0, :], start, ALU.subtract).then_inc(s_tq, 1)
            v.scalar_tensor_tensor(TWK[:, 3, :], erow, float(NE), TWK[:, 2, :], ALU.is_ge, ALU.mult).then_inc(s_tq, 1)
            dve.wait_ge(s_tq, 15)
            v.tensor_scalar(TAB[:, 2, :], TAB[:, 2, :], E16, None, ALU.mult).then_inc(s_tq, 1)
            v.tensor_scalar(TAB[:, 3, :], TWK[:, 1, :], float(NE * LIST), None, ALU.min).then_inc(s_tq, 1)
            v.tensor_tensor(TAB[:, 4, :], TWK[:, 3, :], start, ALU.add).then_inc(s_tq, 1)
            dve.wait_ge(s_tq, 18)
            dve.wait_ge(s_zr, 2)
            dve.sem_inc(s_tab, 1)

            def tile_lo(t, p):
                dve.wait_ge(s_xh, t + 1)
                v.scalar_tensor_tensor(xl[p], PS[:, p, :].rearrange("p (k n) -> p k n", n=P), H_S, xh[p],
                                       ALU.mult, ALU.subtract).then_inc(s_xl, 1)

            def hidden_lo(t, p):
                dve.wait_ge(s_ah2, t + 1)
                v.tensor_tensor(eal[p], PS[:, 4, 0:2 * P], eah[p], ALU.subtract).then_inc(s_al2, 1)

            def hidden(t, p):
                dve.wait_ge(s_es, t + 1)
                v.scalar_tensor_tensor(ea[p][:, 0:M], PS[:, 2 + p, M:2 * M], 1.0 / (H_S * E_S), eg[p], ALU.mult, ALU.mult)
                v.scalar_tensor_tensor(ea[p][:, M:2 * P], PS[:, 2 + p, M + P:2 * M], 1.0 / (H_S * E_S), eg[p][:, P:M],
                                       ALU.mult, ALU.mult).then_inc(s_ea, 1)

            def weigh(t, u, n):
                e = dve.value_load(TAB[0:1, 0, bass.ds(t, 1)], min_val=0, max_val=NE - 1)
                dve.wait_ge(s_ed, t + 2)
                dve.wait_ge(s_add[u % V], n * 16 + 16)
                v.tensor_scalar(yt[u % V], PS[:, 5 + u % 2, :], xg[u][:, bass.ds(e + D, 1)], None, ALU.mult).then_inc(s_y, 1)

            tile_lo(0, 0)
            tile_lo(1, 1)
            hidden(0, 0)
            with dve.Fori(0, NTILE // U) as it:
                for u in range(U):
                    t = it * U + u
                    tile_lo(t + 2, u % 2)
                    hidden_lo(t, u % 2)
                    hidden(t + 1, (u + 1) % 2)
                    weigh(t, u, it * (U // V) + u // V)

        @block.tensor
        def _(pe):
            mm = nc.tensor.matmul
            pe.wait_ge(s_wio, 32)
            pe.wait_ge(s_ttr, B * KC)
            for ec in range(KC):
                for k in range(KC):
                    last = mm(PS[:, 0, ec * B:(ec + 1) * B], winT[:, k, ec * P:(ec + 1) * P], cm[:, k, :],
                              start=(k == 0), stop=(k == KC - 1))
            last.then_inc(s_st, 1)
            pe.wait_ge(s_sT, KC)
            for k in range(KC):
                last = mm(PS[0:B, 1, :], sT[:, k, :], woutT[:, k, :], start=(k == 0), stop=(k == KC - 1))
            last.then_inc(s_sb, 1)
            pe.wait_ge(s_rows, 64)
            pe.wait_ge(s_sTb, 1)
            for b in range(B):
                wait(pe, s_summ, b - 1)
                mm(PS[:, 2 + b % 2, :], ident[0:B, b:b + 1].to_broadcast([B, P]), ssum, start=True, stop=True).then_inc(s_smp, 1)
            def fold(s):
                pe.wait_ge(s_sl, s + 1)
                wait(pe, s_w2l, s)
                for g in range(4):
                    for i in range(4):
                        sign = bin(i & g).count("1") % 2
                        mm(PS[:, 4 + g, :], had[:, sign, :], Sh[:, 4 * i:4 * i + 4, :], start=(i == 0), stop=False)
                        last = mm(PS[:, 4 + g, :], had[:, sign, :], Sl[:, 4 * i:4 * i + 4, :], start=False, stop=(i == 3))
                    last.then_inc(s_w2p, 1)

            def transpose_chunk(src, bank, k):
                for t in range(TT):
                    last = nc.tensor.transpose(PS[:, bank, t * P:(t + 1) * P], src[:, t, k * P:(k + 1) * P], ident[:, :])
                last.then_inc(s_tr, 1)

            def chunk_in_turn(E, k):
                wait(pe, s_tlo, E + (k - 1))
                transpose_chunk(Z, 2 + k % 2, k)

            def hadamard(b, j):
                pe.wait_ge(s_tlo, b * 8 + max(KC, KC + j - 1))
                for i in range(KC):
                    sign = bin(i & j).count("1") % 2
                    mm(PS[:, 2 + j % 2, :], had[:, sign, :], uh[i], start=(i == 0), stop=False)
                    last = mm(PS[:, 2 + j % 2, :], had[:, sign, :], ul[i], start=False, stop=(i == KC - 1))
                last.then_inc(s_hd, 1)

            def three(out, lh, ll, rh, rl, first, last_group):
                mm(out, lh, rh, start=first, stop=False)
                mm(out, lh, rl, start=False, stop=False)
                return mm(out, ll, rh, start=False, stop=last_group)

            def up_gate(F, b, pair, p):
                for half, done, read in ((1, s_g, s_silu), (0, s_u, s_a)):
                    if not isinstance(F, int) or F:
                        pe.wait_ge(read, F)
                    for k in range(KC):
                        at = k * 512 + (half * 2 + p) * P
                        wh, wl = (wug_cols(pair, at + i * KC * 512) for i in range(2))
                        last = three(PS[:, 1 - half, :], wh, wl, had_hi(b, k), had_lo(b, k), k == 0, k == KC - 1)
                    last.then_inc(done, 1)

            def wug_cols(pair, at):
                if isinstance(pair, int):
                    return wug[:, pair, at:at + P]
                return wug[:, :, :].rearrange("p c f -> p (c f)")[:, bass.ds(pair * (2 * KC * 512) + at, P)]

            def down(F, f, p, first, end):
                pe.wait_ge(s_al, F + 1)
                if first:
                    pe.wait_ge(s_wul, 8)
                    pe.wait_ge(s_w2l, 4)
                for t in range(TT):
                    a, b_ = ah[p][:, t * P:(t + 1) * P], al[p][:, t * P:(t + 1) * P]
                    fs = slice(f, f + 1) if isinstance(f, int) else bass.ds(f, 1)
                    rh, rl = w2h[:, fs, :].rearrange("p a d -> p (a d)"), w2l[:, fs, :].rearrange("p a d -> p (a d)")
                    last = three(PS[:, 4 + t, :], a, b_, rh, rl, first, end)
                last.then_inc(s_dn, 1)

            def ffn_step(b, i, p, first=False):
                f = i * 2 + p
                up_gate(b * FC + f + 1, b, i + p, 1 - p)
                down(b * FC + f, f, p, first, False)

            def ffn_steps(b, last):
                for p in range(2):
                    ffn_step(b, 0, p, p == 0)
                with pe.Fori(1, last // 2) as i:
                    for p in range(2):
                        ffn_step(b, i, p)

            fold(0)
            fold(1)
            pe.wait_ge(s_summ, B)
            pe.wait_ge(s_h, TT)
            for k in range(KC):
                chunk_in_turn(0, k)
            for j in range(KC):
                hadamard(0, j)
            fold(2)
            pe.wait_ge(s_tlo, 2 * KC)
            pe.wait_ge(s_wul, 1)
            up_gate(0, 0, 0, 0)
            fold(3)
            def second_half(b, q, following):
                for f in range(FC // 2, FC - 1):
                    if f == 9:
                        pe.wait_ge(s_h, q * TT + TT)
                    if f in (9, 10):
                        for k in (2 * f - 18, 2 * f - 17):
                            chunk_in_turn(q * 8, k)
                    if f >= 11 and following is not None:
                        hadamard(following, f - 11)
                    ffn_step(b, f // 2, f % 2)

            with pe.Fori(0, B - 1) as b:
                ffn_steps(b, FC // 2)
                second_half(b, b + 1, b + 1)
                pe.wait_ge(s_tlo, b * 8 + (8 + 2 * KC))
                up_gate(b * FC + FC, b + 1, 0, 0)
                down(b * FC + FC - 1, FC - 1, 1, False, True)
            ffn_steps(B - 1, FC // 2)
            second_half(B - 1, Q_ROUND[0], None)
            down(B * FC - 1, FC - 1, 1, False, True)

            def scores(t):
                p, b, slot = t % 2, t // TT, t % TT
                wait(pe, s_s, t - 1)
                if slot == 0:
                    pe.wait_ge(s_ctl, b + 2 if b else 1)
                    pe.wait_ge(s_tlo, copied_before(Q_ROUND[b]) + KC)
                for n in range(2):
                    if t == 0 and n:
                        pe.wait_ge(s_ctl, 2)
                    for k in range(KC):
                        ts = slice(slot * P, (slot + 1) * P)
                        last = three(PS[:, 2 * p + n, :], had_hi(b, k)[:, ts], had_lo(b, k)[:, ts],
                                     cTh[b % 2][:, k, n * 512:(n + 1) * 512], cTl[b % 2][:, k, n * 512:(n + 1) * 512],
                                     k == 0, k == KC - 1)
                last.then_inc(s_sc, 1)

            def chunk_alone(src, q, k, ranked):
                if k == 0:
                    pe.wait_ge(s_h, q * TT + TT)
                    wait(pe, s_rk, ranked)
                pe.wait_ge(s_tlo, copied_before(q) + k)
                transpose_chunk(src, 7, k)

            def logits(q):
                pe.wait_ge(s_tlo, copied_before(q) + KC)
                for t in range(TT):
                    for k in range(KC):
                        ts = slice(t * P, (t + 1) * P)
                        last = three(PS[:, 7, t * NE:(t + 1) * NE], rh[:, k, ts], rl[:, k, ts], gkh[:, k, :], gkl[:, k, :],
                                     k == 0, k == KC - 1)
                last.then_inc(s_lg, 1)

            def rank(b):
                pe.wait_ge(s_sel, b + 1)
                pe.wait_ge(s_ss, b + 1)
                for t in range(TT):
                    out = PS[:, 7, t * NE:(t + 1) * NE]
                    mm(out, tri[:, 0, :], SEL[:, t, :], start=True, stop=False)
                    for before in range(t):
                        mm(out, tri[:, 2, :], SEL[:, before, :], start=False, stop=False)
                    last = mm(out, tri[:, 2, :], SELS[:, :], start=False, stop=True)
                last.then_inc(s_rkp, 1)

            pe.wait_ge(s_gkl, 1)
            def side(b, slot, place):
                what, of, k = beside(b, slot, place)
                if what == "q":
                    chunk_alone(ROWS, Q_ROUND[of], k, max(b - 1, 0))
                elif what == "r":
                    chunk_alone(Z, R_ROUND[of], k, of)
                elif what == "logits":
                    logits(R_ROUND[of])
                elif what == "rank":
                    rank(of)

            scores(0)
            for b in range(B):
                for slot in range(TT):
                    t = b * TT + slot
                    if t == 0:
                        scores(1)
                        pe.wait_ge(s_x2, NT)
                    pe.wait_ge(s_p, t + 1)
                    wait(pe, s_ptl, t)
                    for c in range(KEYC):
                        last = nc.tensor.transpose(PS[:, 4 + c // 4, (c % 4) * P:(c % 4 + 1) * P], pr[:, c * P:(c + 1) * P], ident[:, :])
                    last.then_inc(s_pt, 1)
                    side(b, slot, 0)
                    if 0 < t < NT - 1:
                        scores(t + 1)
                    side(b, slot, 1)
                    pe.wait_ge(s_ptl, t + 1)
                    wait(pe, s_xr, t)
                    if slot == 0:
                        pe.wait_ge(s_cnl, b + 1)
                    for c in range(KEYC):
                        last = three(PS[:, 6, :], pTh[:, c, :], pTl[:, c, :], cNh[b % 2][:, c, :], cNl[b % 2][:, c, :],
                                     c == 0, c == KEYC - 1)
                    last.then_inc(s_rd, 1)
                    side(b, slot, 2)
            pe.wait_ge(s_h, TT * (R_ROUND[B - 1] + 1))
            for k in range(KC):
                transpose_chunk(Z, k, k)
            logits(R_ROUND[B - 1])
            rank(B - 1)

            pe.wait_ge(s_ss, B + 1)
            mm(PS[0:NE, 0, 0:1], SELS[:, :], tri[:, 2, 0:1], start=True, stop=True).then_inc(s_tp, 1)
            pe.wait_ge(s_tq, 3)
            mm(PS[0:NE, 1, 0:1], tri[0:NE, 1, 0:NE], CH[0:NE, 0:1], start=True, stop=True).then_inc(s_tp, 1)
            pe.wait_ge(s_tq, 6)
            mm(PS[0:1, 2, 0:TABLE], tri[0:NE, 2, 0:1], TCMP[0:NE, :], start=True, stop=True)
            mm(PS[0:1, 2, TABLE:2 * TABLE], CH[0:NE, 0:1], TCMP[0:NE, :], start=True, stop=True)
            mm(PS[0:1, 2, 2 * TABLE:2 * TABLE + NE], CH[0:NE, 1:2], tri[0:NE, 3, 0:NE], start=True, stop=True)\
                .then_inc(s_tp, 1)
            pe.wait_ge(s_tab, 1)

            def tile_transpose(t, u, n):
                pe.wait_ge(s_xg[u], n * 16 + 16)
                for k in range(KC):
                    last = nc.tensor.transpose(PS[:, u % 2, k * P:(k + 1) * P], xg[u][:, k * P:(k + 1) * P], ident[:, :])
                last.then_inc(s_xt, 1)

            def weights_at(t):
                return pe.value_load(TAB[0:1, 2, bass.ds(t, 1)], min_val=0, max_val=E16)

            def tile_up(t, p, at):
                for k in range(KC):
                    hi = we[:, bass.ds(at + k * GU, GU)]
                    lo = we[:, bass.ds(at + (EW + k * GU), GU)]
                    last = three(PS[:, 2 + p, 0:GU], xh[p][:, k, :], xl[p][:, k, :], hi, lo, k == 0, k == KC - 1)
                last.then_inc(s_ug, 1)

            def hidden_transpose(p):
                nc.tensor.transpose(PS[:, 4, 0:P], ea[p][:, 0:P], ident[:, :])
                nc.tensor.transpose(PS[:, 4, P:2 * P], ea[p][:, P:2 * P], ident[:, :]).then_inc(s_at, 1)

            def tile_down(t, p, at):
                pe.wait_ge(s_al2, t + 1)
                bank = PS[:, 5 + p, :]
                w0h, w1 = KC * GU, KC * GU + D
                hi, lo = we[:, bass.ds(at + w0h, D)], we[:, bass.ds(at + (EW + w0h), D)]
                stack = we[:, bass.ds(at + w1, D)]
                three(bank, eah[p][:, 0:P], eal[p][:, 0:P], hi, lo, True, False)
                mm(bank, eah[p][:, P:2 * P], stack, start=False, stop=False)
                mm(bank, eal[p][:, P:2 * P], stack, start=False, stop=True).then_inc(s_ed, 1)

            tile_transpose(0, 0, 0)
            tile_transpose(1, 1, 0)
            pe.wait_ge(s_xl, 1)
            tile_up(0, 0, weights_at(0))
            with pe.Fori(0, NTILE // PU) as it:
                for u in range(PU):
                    t = it * PU + u
                    tile_transpose(t + 2, (u + 2) % U, it * (PU // U) + (u + 2) // U)
                    following = weights_at(t + 1)
                    pe.wait_ge(s_ea, t + 1)
                    hidden_transpose(u % 2)
                    tile_up(t + 1, (u + 1) % 2, following)
                    if u == 0:
                        at = weights_at(t)
                    tile_down(t, u % 2, at)
                    at = following


def kernel(x, ctx_2048, mask_BxS2_bk0, L0_xattn_decay, L0_xattn_W_in, L0_xattn_b_in, L0_xattn_W_out,
           L0_xattn_b_out, L0_xattn_gamma, L0_xattn_beta, L0_ffn_SU_ug, L0_ffn_SU_dp, L0_ffn_Wscale_ug,
           L0_ffn_Wscale_dp, L0_ffn_W_up, L0_ffn_W_gate, L0_ffn_W_down, L1_ffn_gate_kernel, L1_ffn_gate_proj,
           L1_ffn_up_proj, L1_ffn_down_proj):
    import concourse.bacc as bacc
    from concourse.bass_utils import run_bass_kernel_spmd

    asc = np.ascontiguousarray

    def column(v):
        return np.reshape(np.asarray(v), (-1, P)).T

    ws = np.asarray(L0_ffn_Wscale_ug)
    cols = asc(np.concatenate([column(L0_xattn_b_in), column(L0_ffn_SU_ug), column(L0_ffn_SU_dp),
                               column(ws[:INTER]), column(ws[INTER:]),
                               np.broadcast_to(np.reshape(np.asarray(L0_xattn_decay), (1, 1)), (P, 1))], axis=1))
    rows = asc(np.broadcast_to(np.stack([np.asarray(L0_xattn_gamma), np.asarray(L0_xattn_beta),
                                         np.asarray(L0_xattn_b_out), np.asarray(L0_ffn_Wscale_dp)])[None], (P, 4, D)))
    gate, up, down = (np.asarray(a) for a in (L1_ffn_gate_proj, L1_ffn_up_proj, L1_ffn_down_proj))
    gu = np.concatenate([gate, up], axis=2)
    gu = np.reshape(np.transpose(np.reshape(gu, (NE, KC, P, 2 * M)), (0, 2, 1, 3)), (NE, P, KC * 2 * M))
    experts = asc(np.concatenate([gu, down[:, :P], np.concatenate([down[:, P:], down[:, P:]], axis=1)], axis=2))
    h = np.array([[1.0]])
    while h.shape[0] < P:
        h = np.block([[h, h], [h, -h]])
    before = np.triu(np.ones((P, P)))
    wug = [np.reshape(np.asarray(w).T, (KC, P, FC // 2, 2 * P)) for w in (L0_ffn_W_up, L0_ffn_W_gate)]
    wug = asc(np.reshape(np.transpose(np.concatenate(wug, axis=3), (2, 1, 0, 3)), (FC // 2, P, KC * 4 * P)))
    xin = np.asarray(x)
    arrays = {
        "x": asc(np.reshape(xin, (B * S, D))),
        "ctxT": asc(np.transpose(np.asarray(ctx_2048), (0, 2, 1))),
        "ctx": asc(np.asarray(ctx_2048)),
        "mask": asc(np.broadcast_to(np.reshape(np.asarray(mask_BxS2_bk0), (1, B * T2)), (P, B * T2))),
        "winT": asc(np.asarray(L0_xattn_W_in).T),
        "woutT": asc(np.asarray(L0_xattn_W_out).T),
        "cols": cols,
        "rows": rows,
        "wug": wug,
        "wdT": asc(np.asarray(L0_ffn_W_down).T),
        "gk": asc(np.asarray(L1_ffn_gate_kernel)),
        "experts": experts,
        "ident": np.eye(P, dtype=np.float32),
        "had": asc(np.stack([h, -h], axis=1).astype(np.float16)),
        "tri": asc(np.stack([before - np.eye(P), before, np.ones((P, P)), np.eye(P)], axis=1).astype(np.float16)),
    }
    nc = bacc.Bacc("TRN2", target_bir_lowering=False, num_devices=1)
    args = [nc.dram_tensor(f"in_{n}", a.shape, mybir.dt.from_np(a.dtype), kind="ExternalInput").ap() for n, a in arrays.items()]
    split = nc.dram_tensor("split_experts", (NE, P, E16), F16, kind="Internal").ap()
    lists = nc.dram_tensor("token_lists", (P * NE * LIST, 1), I32, kind="Internal").ap()
    table = nc.dram_tensor("token_table", (NTOK + P, TW), F32, kind="Internal").ap()
    out = nc.dram_tensor("out", (NTOK + P, D), F32, kind="ExternalOutput").ap()
    build(nc, *args, split, lists, table, out)
    r = run_bass_kernel_spmd(nc, [{f"in_{n}": a for n, a in arrays.items()}], core_ids=[0])
    return np.reshape(r.results[0]["out"][:NTOK], xin.shape)
```
